# Optimizing a Trainium2 kernel written in Bass

```python
import numpy as np
import jax
import jax.numpy as jnp

def _softmax(x, axis=-1):
    return jax.nn.softmax(x, axis=axis)

def _gelu(x):
    return jax.nn.gelu(x, approximate=True)

def _silu(x):
    return jax.nn.silu(x)

def _sigmoid(x):
    return jax.nn.sigmoid(x)

def _layernorm(x, axis=-1, eps=1e-05):
    m = jnp.mean(x, axis=axis, keepdims=True)
    v = jnp.var(x, axis=axis, keepdims=True)
    return (x - m) / jnp.sqrt(v + eps)

def _scatter_add(tgt, idx, src, axis=0):
    return tgt.at[idx].add(src)

def _segment_sum(src, seg, n):
    return jax.ops.segment_sum(src, seg, n)
kernel_name = 'mk_early_fusion_d2_tok_img256_r4_02622d'

def setup_inputs(seed: int=0):
    np.random.seed(seed)
    _w = jnp.asarray

    def _rec_inputs():
        import jax
        import jax.numpy as jnp
        _rk = jax.random.key(seed)
        x = -0.00040386 + 0.999972 * jax.random.normal(jax.random.fold_in(_rk, 1), (8, 3, 64, 64), jnp.float32)
        txt = -0.0054313 + 0.191732 * jax.random.normal(jax.random.fold_in(_rk, 2), (8, 77, 64), jnp.float32)
        return (x, txt)
    x, txt = _rec_inputs()

    def _L0_tok_setup():
        import jax, jax.numpy as jnp
        import numpy as np
        EPS = 1e-05
        P = 8
        DIM = 64
        NUM_TOKENS = 64
        PATCH_DIM = 3 * P * P

        def layernorm(x, g, b):
            mu = jnp.mean(x, axis=-1, keepdims=True)
            var = jnp.mean(jnp.square(x - mu), axis=-1, keepdims=True)
            return (x - mu) * jax.lax.rsqrt(var + EPS) * g + b
        key = jax.random.key(seed)
        ks = jax.random.split(key, 8)
        b, c, h, w = (16, 3, 128, 128)
        x = jax.random.normal(ks[0], (b, c, h, w), dtype=jnp.float32)
        ln1_g = jnp.ones((PATCH_DIM,), jnp.float32)
        ln1_b = jnp.zeros((PATCH_DIM,), jnp.float32)
        W1 = jax.random.normal(ks[1], (PATCH_DIM, DIM), jnp.float32) * 0.02
        b1 = jnp.zeros((DIM,), jnp.float32)
        ln2_g = jnp.ones((DIM,), jnp.float32)
        ln2_b = jnp.zeros((DIM,), jnp.float32)
        Wp1 = jax.random.normal(ks[2], (DIM, DIM), jnp.float32) * 0.02
        bp1 = jnp.zeros((DIM,), jnp.float32)
        lnp_g = jnp.ones((DIM,), jnp.float32)
        lnp_b = jnp.zeros((DIM,), jnp.float32)
        Wp2 = jax.random.normal(ks[3], (DIM, NUM_TOKENS), jnp.float32) * 0.02
        bp2 = jnp.zeros((NUM_TOKENS,), jnp.float32)
        return {'x': x, 'ln1_g': ln1_g, 'ln1_b': ln1_b, 'W1': W1, 'b1': b1, 'ln2_g': ln2_g, 'ln2_b': ln2_b, 'Wp1': Wp1, 'bp1': bp1, 'lnp_g': lnp_g, 'lnp_b': lnp_b, 'Wp2': Wp2, 'bp2': bp2}
    _L0_tok_all = _L0_tok_setup()
    _L0_tok_in = {k: v for k, v in _L0_tok_all.items() if k in ('ln1_g', 'ln1_b', 'W1', 'b1', 'ln2_g', 'ln2_b', 'Wp1', 'bp1', 'lnp_g', 'lnp_b', 'Wp2', 'bp2')}
    del _L0_tok_all

    def _L0_attn_setup():
        import jax, jax.numpy as jnp
        import numpy as np
        DIM = 64
        HEADS = 8
        DIM_HEAD = 32
        LANDMARKS = 128
        PINV_ITERS = 6
        KERNEL = 33
        SCALE = DIM_HEAD ** (-0.5)
        LN_EPS = 1e-05

        def _pinv(a, iters=PINV_ITERS):
            abs_a = jnp.abs(a)
            col = jnp.max(abs_a.sum(axis=-1))
            row = jnp.max(abs_a.sum(axis=-2))
            z = jnp.swapaxes(a, -1, -2) / (col * row)
            I = jnp.eye(a.shape[-1], dtype=a.dtype)
            for _ in range(iters):
                az = a @ z
                z = 0.25 * z @ (13.0 * I - az @ (15.0 * I - az @ (7.0 * I - az)))
            return z

        def _reference_tuple_inner(x, ln_g, ln_b, w_qkv, w_out, b_out, res_kernel):
            b, n, d = x.shape
            mu = jnp.mean(x, -1, keepdims=True)
            var = jnp.var(x, -1, keepdims=True)
            xn = (x - mu) * jax.lax.rsqrt(var + LN_EPS) * ln_g + ln_b
            pad = -n % LANDMARKS
            xp = jnp.pad(xn, ((0, 0), (pad, 0), (0, 0)))
            N = n + pad
            qkv = xp @ w_qkv
            q, k, v = jnp.split(qkv, 3, axis=-1)
            to_h = lambda t: t.reshape(b, N, HEADS, DIM_HEAD).transpose(0, 2, 1, 3)
            q = to_h(q) * SCALE
            k = to_h(k)
            v = to_h(v)
            l = N // LANDMARKS
            q_l = q.reshape(b, HEADS, LANDMARKS, l, DIM_HEAD).mean(3)
            k_l = k.reshape(b, HEADS, LANDMARKS, l, DIM_HEAD).mean(3)
            attn1 = jax.nn.softmax(jnp.einsum('bhid,bhjd->bhij', q, k_l), -1)
            attn2 = jax.nn.softmax(jnp.einsum('bhid,bhjd->bhij', q_l, k_l), -1)
            attn3 = jax.nn.softmax(jnp.einsum('bhid,bhjd->bhij', q_l, k), -1)
            attn2_inv = _pinv(attn2)
            a12 = attn1 @ attn2_inv
            out = a12 @ (attn3 @ v)
            res = jax.lax.conv_general_dilated(v, res_kernel, (1, 1), ((KERNEL // 2, KERNEL // 2), (0, 0)), feature_group_count=HEADS, dimension_numbers=('NCHW', 'OIHW', 'NCHW'))
            out = out + res
            out = out.transpose(0, 2, 1, 3).reshape(b, N, HEADS * DIM_HEAD)
            out = out @ w_out + b_out
            out = out[:, -n:]
            att = a12 @ attn3
            return (x + out, att, pad, n)
        key = jax.random.key(seed)
        ks = jax.random.split(key, 4)
        b, n = (1, 1000)
        inner = HEADS * DIM_HEAD
        s = 0.02
        return {'x': jax.random.normal(ks[0], (b, n, DIM), jnp.float32), 'ln_g': jnp.ones((DIM,), jnp.float32), 'ln_b': jnp.zeros((DIM,), jnp.float32), 'w_qkv': jax.random.normal(ks[1], (DIM, 3 * inner), jnp.float32) * s, 'w_out': jax.random.normal(ks[2], (inner, DIM), jnp.float32) * s, 'b_out': jnp.zeros((DIM,), jnp.float32), 'res_kernel': jax.random.normal(ks[3], (HEADS, 1, KERNEL, 1), jnp.float32) * s}
    _L0_attn_all = _L0_attn_setup()
    _L0_attn_in = {k: v for k, v in _L0_attn_all.items() if k in ('ln_g', 'ln_b', 'w_qkv', 'w_out', 'b_out', 'res_kernel')}
    del _L0_attn_all

    def _L0_ffn_setup():
        import jax, jax.numpy as jnp
        import numpy as np
        TOP_K = 2
        LN_EPS = 1e-05
        key = jax.random.key(seed)
        ks = jax.random.split(key, 8)
        B, S, D, E, H = (16, 256, 64, 8, 256)
        x = jax.random.normal(ks[0], (B, S, D), dtype=jnp.float32)
        Wr = jax.random.normal(ks[1], (D, E), dtype=jnp.float32) * 0.1
        br = jnp.zeros((E,), dtype=jnp.float32)
        ln_g = jnp.ones((E, D), dtype=jnp.float32)
        ln_b = jnp.zeros((E, D), dtype=jnp.float32)
        W1 = jax.random.normal(ks[2], (E, D, H), dtype=jnp.float32) * (1.0 / np.sqrt(D))
        b1 = jnp.zeros((E, H), dtype=jnp.float32)
        W2 = jax.random.normal(ks[3], (E, H, D), dtype=jnp.float32) * (1.0 / np.sqrt(H))
        b2 = jnp.zeros((E, D), dtype=jnp.float32)
        return {'x': x, 'Wr': Wr, 'br': br, 'ln_g': ln_g, 'ln_b': ln_b, 'W1': W1, 'b1': b1, 'W2': W2, 'b2': b2}
    _L0_ffn_all = _L0_ffn_setup()
    _L0_ffn_in = {k: v for k, v in _L0_ffn_all.items() if k in ('Wr', 'br', 'ln_g', 'ln_b', 'W1', 'b1', 'W2', 'b2')}
    del _L0_ffn_all

    def _L1_attn_setup():
        import jax, jax.numpy as jnp
        import numpy as np
        EPS = 1e-05

        def _ln(x, scale):
            mu = jnp.mean(x, axis=-1, keepdims=True)
            var = jnp.var(x, axis=-1, keepdims=True)
            return (x - mu) / jnp.sqrt(var + EPS) * scale
        key = jax.random.key(seed)
        k = jax.random.split(key, 8)
        B, S, E, H = (4, 512, 64, 8)
        n_layer = 12
        x = jax.random.normal(k[0], (B, S, E), dtype=jnp.float32)
        e = jax.random.normal(k[1], (B, S, E), dtype=jnp.float32)
        p = jax.random.normal(k[2], (S, E), dtype=jnp.float32)
        W_q = 0.02 * jax.random.normal(k[3], (H, E, E), dtype=jnp.float32)
        W_k = 0.02 * jax.random.normal(k[4], (H, E, E), dtype=jnp.float32)
        W_v = 0.02 * jax.random.normal(k[5], (H, E, E), dtype=jnp.float32)
        W_o = 0.02 / np.sqrt(2 * n_layer) * jax.random.normal(k[6], (E, H * E), dtype=jnp.float32)
        gamma = jnp.ones((1, H, 1, 1), dtype=jnp.float32)
        ln_scale = jnp.ones((E,), dtype=jnp.float32)
        return {'x': x, 'e': e, 'p': p, 'ln_scale': ln_scale, 'W_q': W_q, 'W_k': W_k, 'W_v': W_v, 'W_o': W_o, 'gamma': gamma}
    _L1_attn_all = _L1_attn_setup()
    _L1_attn_in = {k: v for k, v in _L1_attn_all.items() if k in ('e', 'p', 'ln_scale', 'W_q', 'W_k', 'W_v', 'W_o', 'gamma')}
    del _L1_attn_all

    def _L1_ffn_setup():
        import jax, jax.numpy as jnp
        import numpy as np
        B, A = (1024, 8)
        IN, OUT = (64, 64)
        SH1, SH2 = (64, 128)
        EH1, EH2 = (128, 64)
        E, TOPK = (4, 2)

        def _shared_mlp(x, W1, b1, W2, b2, W3, b3):
            h = jax.nn.relu(x @ W1 + b1)
            h = jax.nn.relu(h @ W2 + b2)
            return h @ W3 + b3

        def _experts_mlp(x, eW1, eb1, eW2, eb2, eW3, eb3):
            h = jax.nn.relu(jnp.einsum('baf,efh->ebah', x, eW1) + eb1[:, None, None, :])
            h = jax.nn.relu(jnp.einsum('ebah,ehg->ebag', h, eW2) + eb2[:, None, None, :])
            o = jnp.einsum('ebag,ego->ebao', h, eW3) + eb3[:, None, None, :]
            return jnp.moveaxis(o, 0, -1)
        key = jax.random.key(seed)
        ks = jax.random.split(key, 16)
        s = 0.05
        return {'x': jax.random.normal(ks[0], (B, A, IN), jnp.float32), 'sW1': jax.random.normal(ks[1], (IN, SH1), jnp.float32) * s, 'sb1': jnp.zeros((SH1,), jnp.float32), 'sW2': jax.random.normal(ks[2], (SH1, SH2), jnp.float32) * s, 'sb2': jnp.zeros((SH2,), jnp.float32), 'sW3': jax.random.normal(ks[3], (SH2, OUT), jnp.float32) * s, 'sb3': jnp.zeros((OUT,), jnp.float32), 'eW1': jax.random.normal(ks[4], (E, IN, EH1), jnp.float32) * s, 'eb1': jnp.zeros((E, EH1), jnp.float32), 'eW2': jax.random.normal(ks[5], (E, EH1, EH2), jnp.float32) * s, 'eb2': jnp.zeros((E, EH2), jnp.float32), 'eW3': jax.random.normal(ks[6], (E, EH2, OUT), jnp.float32) * s, 'eb3': jnp.zeros((E, OUT), jnp.float32), 'gW': jax.random.normal(ks[7], (IN, E), jnp.float32) * s, 'gb': jnp.zeros((E,), jnp.float32)}
    _L1_ffn_all = _L1_ffn_setup()
    _L1_ffn_in = {k: v for k, v in _L1_ffn_all.items() if k in ('sW1', 'sb1', 'sW2', 'sb2', 'sW3', 'sb3', 'eW1', 'eb1', 'eW2', 'eb2', 'eW3', 'eb3', 'gW', 'gb')}
    del _L1_ffn_all
    return {'x': x, 'txt': txt, 'L0_tok_ln1_g': _L0_tok_in['ln1_g'], 'L0_tok_ln1_b': _L0_tok_in['ln1_b'], 'L0_tok_W1': _L0_tok_in['W1'], 'L0_tok_b1': _L0_tok_in['b1'], 'L0_tok_ln2_g': _L0_tok_in['ln2_g'], 'L0_tok_ln2_b': _L0_tok_in['ln2_b'], 'L0_tok_Wp1': _L0_tok_in['Wp1'], 'L0_tok_bp1': _L0_tok_in['bp1'], 'L0_tok_lnp_g': _L0_tok_in['lnp_g'], 'L0_tok_lnp_b': _L0_tok_in['lnp_b'], 'L0_tok_Wp2': _L0_tok_in['Wp2'], 'L0_tok_bp2': _L0_tok_in['bp2'], 'L0_attn_ln_g': _L0_attn_in['ln_g'], 'L0_attn_ln_b': _L0_attn_in['ln_b'], 'L0_attn_w_qkv': _L0_attn_in['w_qkv'], 'L0_attn_w_out': _L0_attn_in['w_out'], 'L0_attn_b_out': _L0_attn_in['b_out'], 'L0_attn_res_kernel': _L0_attn_in['res_kernel'], 'L0_ffn_Wr': _L0_ffn_in['Wr'], 'L0_ffn_br': _L0_ffn_in['br'], 'L0_ffn_ln_g': _L0_ffn_in['ln_g'], 'L0_ffn_ln_b': _L0_ffn_in['ln_b'], 'L0_ffn_W1': _L0_ffn_in['W1'], 'L0_ffn_b1': _L0_ffn_in['b1'], 'L0_ffn_W2': _L0_ffn_in['W2'], 'L0_ffn_b2': _L0_ffn_in['b2'], 'L1_attn_e': _L1_attn_in['e'], 'L1_attn_p': _L1_attn_in['p'], 'L1_attn_ln_scale': _L1_attn_in['ln_scale'], 'L1_attn_W_q': _L1_attn_in['W_q'], 'L1_attn_W_k': _L1_attn_in['W_k'], 'L1_attn_W_v': _L1_attn_in['W_v'], 'L1_attn_W_o': _L1_attn_in['W_o'], 'L1_attn_gamma': _L1_attn_in['gamma'], 'L1_ffn_sW1': _L1_ffn_in['sW1'], 'L1_ffn_sb1': _L1_ffn_in['sb1'], 'L1_ffn_sW2': _L1_ffn_in['sW2'], 'L1_ffn_sb2': _L1_ffn_in['sb2'], 'L1_ffn_sW3': _L1_ffn_in['sW3'], 'L1_ffn_sb3': _L1_ffn_in['sb3'], 'L1_ffn_eW1': _L1_ffn_in['eW1'], 'L1_ffn_eb1': _L1_ffn_in['eb1'], 'L1_ffn_eW2': _L1_ffn_in['eW2'], 'L1_ffn_eb2': _L1_ffn_in['eb2'], 'L1_ffn_eW3': _L1_ffn_in['eW3'], 'L1_ffn_eb3': _L1_ffn_in['eb3'], 'L1_ffn_gW': _L1_ffn_in['gW'], 'L1_ffn_gb': _L1_ffn_in['gb']}

def reference(x, txt, L0_tok_ln1_g, L0_tok_ln1_b, L0_tok_W1, L0_tok_b1, L0_tok_ln2_g, L0_tok_ln2_b, L0_tok_Wp1, L0_tok_bp1, L0_tok_lnp_g, L0_tok_lnp_b, L0_tok_Wp2, L0_tok_bp2, L0_attn_ln_g, L0_attn_ln_b, L0_attn_w_qkv, L0_attn_w_out, L0_attn_b_out, L0_attn_res_kernel, L0_ffn_Wr, L0_ffn_br, L0_ffn_ln_g, L0_ffn_ln_b, L0_ffn_W1, L0_ffn_b1, L0_ffn_W2, L0_ffn_b2, L1_attn_e, L1_attn_p, L1_attn_ln_scale, L1_attn_W_q, L1_attn_W_k, L1_attn_W_v, L1_attn_W_o, L1_attn_gamma, L1_ffn_sW1, L1_ffn_sb1, L1_ffn_sW2, L1_ffn_sb2, L1_ffn_sW3, L1_ffn_sb3, L1_ffn_eW1, L1_ffn_eb1, L1_ffn_eW2, L1_ffn_eb2, L1_ffn_eW3, L1_ffn_eb3, L1_ffn_gW, L1_ffn_gb):
    import jax
    import jax.numpy as jnp

    def _L0_tok_ref(x, ln1_g, ln1_b, W1, b1, ln2_g, ln2_b, Wp1, bp1, lnp_g, lnp_b, Wp2, bp2):
        import jax, jax.numpy as jnp
        import numpy as np
        EPS = 1e-05
        P = 8
        DIM = 64
        NUM_TOKENS = 64
        PATCH_DIM = 3 * P * P

        def layernorm(x, g, b):
            mu = jnp.mean(x, axis=-1, keepdims=True)
            var = jnp.mean(jnp.square(x - mu), axis=-1, keepdims=True)
            return (x - mu) * jax.lax.rsqrt(var + EPS) * g + b
        b, c, H, W = x.shape
        hp, wp = (H // P, W // P)
        patches = x.reshape(b, c, hp, P, wp, P)
        patches = jnp.transpose(patches, (0, 2, 4, 3, 5, 1))
        patches = patches.reshape(b, hp * wp, P * P * c)
        tokens = layernorm(patches, ln1_g, ln1_b)
        tokens = tokens @ W1 + b1
        tokens = layernorm(tokens, ln2_g, ln2_b)
        q = tokens
        k = tokens
        tokens = jnp.concatenate([q, k, tokens], axis=1)
        h1 = layernorm(tokens @ Wp1 + bp1, lnp_g, lnp_b)
        h1 = jax.nn.silu(h1)
        return h1 @ Wp2 + bp2

    def _L0_attn_ref(x, ln_g, ln_b, w_qkv, w_out, b_out, res_kernel):
        import jax, jax.numpy as jnp
        import numpy as np
        DIM = 64
        HEADS = 8
        DIM_HEAD = 32
        LANDMARKS = 128
        PINV_ITERS = 6
        KERNEL = 33
        SCALE = DIM_HEAD ** (-0.5)
        LN_EPS = 1e-05

        def _pinv(a, iters=PINV_ITERS):
            abs_a = jnp.abs(a)
            col = jnp.max(abs_a.sum(axis=-1))
            row = jnp.max(abs_a.sum(axis=-2))
            z = jnp.swapaxes(a, -1, -2) / (col * row)
            I = jnp.eye(a.shape[-1], dtype=a.dtype)
            for _ in range(iters):
                az = a @ z
                z = 0.25 * z @ (13.0 * I - az @ (15.0 * I - az @ (7.0 * I - az)))
            return z

        def _reference_tuple_inner(x, ln_g, ln_b, w_qkv, w_out, b_out, res_kernel):
            b, n, d = x.shape
            mu = jnp.mean(x, -1, keepdims=True)
            var = jnp.var(x, -1, keepdims=True)
            xn = (x - mu) * jax.lax.rsqrt(var + LN_EPS) * ln_g + ln_b
            pad = -n % LANDMARKS
            xp = jnp.pad(xn, ((0, 0), (pad, 0), (0, 0)))
            N = n + pad
            qkv = xp @ w_qkv
            q, k, v = jnp.split(qkv, 3, axis=-1)
            to_h = lambda t: t.reshape(b, N, HEADS, DIM_HEAD).transpose(0, 2, 1, 3)
            q = to_h(q) * SCALE
            k = to_h(k)
            v = to_h(v)
            l = N // LANDMARKS
            q_l = q.reshape(b, HEADS, LANDMARKS, l, DIM_HEAD).mean(3)
            k_l = k.reshape(b, HEADS, LANDMARKS, l, DIM_HEAD).mean(3)
            attn1 = jax.nn.softmax(jnp.einsum('bhid,bhjd->bhij', q, k_l), -1)
            attn2 = jax.nn.softmax(jnp.einsum('bhid,bhjd->bhij', q_l, k_l), -1)
            attn3 = jax.nn.softmax(jnp.einsum('bhid,bhjd->bhij', q_l, k), -1)
            attn2_inv = _pinv(attn2)
            a12 = attn1 @ attn2_inv
            out = a12 @ (attn3 @ v)
            res = jax.lax.conv_general_dilated(v, res_kernel, (1, 1), ((KERNEL // 2, KERNEL // 2), (0, 0)), feature_group_count=HEADS, dimension_numbers=('NCHW', 'OIHW', 'NCHW'))
            out = out + res
            out = out.transpose(0, 2, 1, 3).reshape(b, N, HEADS * DIM_HEAD)
            out = out @ w_out + b_out
            out = out[:, -n:]
            att = a12 @ attn3
            return (x + out, att, pad, n)
        return _reference_tuple_inner(x, ln_g, ln_b, w_qkv, w_out, b_out, res_kernel)[0]

    def _L0_ffn_ref(x, Wr, br, ln_g, ln_b, W1, b1, W2, b2):
        import jax, jax.numpy as jnp
        import numpy as np
        TOP_K = 2
        LN_EPS = 1e-05
        B, S, D = x.shape
        N = B * S
        xt = x.reshape(N, D)
        logits = xt @ Wr + br
        probs = jax.nn.softmax(logits, axis=-1)
        top_p, top_idx = jax.lax.top_k(probs, TOP_K)
        weights = top_p / top_p.sum(axis=-1, keepdims=True)
        mu = xt.mean(axis=-1, keepdims=True)
        var = ((xt - mu) ** 2).mean(axis=-1, keepdims=True)
        xn = (xt - mu) * jax.lax.rsqrt(var + LN_EPS)
        xe = xn[None, :, :] * ln_g[:, None, :] + ln_b[:, None, :]
        h = jax.nn.gelu(jnp.einsum('end,edh->enh', xe, W1) + b1[:, None, :], approximate=False)
        y = jnp.einsum('enh,ehd->end', h, W2) + b2[:, None, :]
        y_tok = jnp.transpose(y, (1, 0, 2))
        sel = jnp.take_along_axis(y_tok, top_idx[:, :, None], axis=1)
        out = (weights[:, :, None] * sel).sum(axis=1)
        return out.reshape(B, S, D)

    def _L1_attn_ref(x, e, p, ln_scale, W_q, W_k, W_v, W_o, gamma):
        import jax, jax.numpy as jnp
        import numpy as np
        EPS = 1e-05

        def _ln(x, scale):
            mu = jnp.mean(x, axis=-1, keepdims=True)
            var = jnp.var(x, axis=-1, keepdims=True)
            return (x - mu) / jnp.sqrt(var + EPS) * scale
        B, S, E = x.shape
        H = W_q.shape[0]
        xn = _ln(x, ln_scale)
        Q = jnp.einsum('bse,hef->bhsf', xn, W_q)
        K = jnp.einsum('bse,hef->bhsf', xn, W_k)
        V = jnp.einsum('bse,hef->bhsf', xn, W_v)
        q2 = jnp.sum(Q * Q, axis=-1)[..., :, None]
        k2 = jnp.sum(K * K, axis=-1)[..., None, :]
        qk = jnp.einsum('bhsf,bhtf->bhst', Q, K)
        sqdist = jnp.maximum(q2 + k2 - 2.0 * qk, 0.0)
        scores = jnp.exp(-gamma * sqdist)
        out = jnp.einsum('bhst,bhtf->bhsf', scores, V)
        out = out.transpose(0, 2, 1, 3).reshape(B, S, H * E)
        return out @ W_o.T

    def _L1_ffn_ref(x, sW1, sb1, sW2, sb2, sW3, sb3, eW1, eb1, eW2, eb2, eW3, eb3, gW, gb):
        import jax, jax.numpy as jnp
        import numpy as np
        B, A = (1024, 8)
        IN, OUT = (64, 64)
        SH1, SH2 = (64, 128)
        EH1, EH2 = (128, 64)
        E, TOPK = (4, 2)

        def _shared_mlp(x, W1, b1, W2, b2, W3, b3):
            h = jax.nn.relu(x @ W1 + b1)
            h = jax.nn.relu(h @ W2 + b2)
            return h @ W3 + b3

        def _experts_mlp(x, eW1, eb1, eW2, eb2, eW3, eb3):
            h = jax.nn.relu(jnp.einsum('baf,efh->ebah', x, eW1) + eb1[:, None, None, :])
            h = jax.nn.relu(jnp.einsum('ebah,ehg->ebag', h, eW2) + eb2[:, None, None, :])
            o = jnp.einsum('ebag,ego->ebao', h, eW3) + eb3[:, None, None, :]
            return jnp.moveaxis(o, 0, -1)
        all_out = _experts_mlp(x, eW1, eb1, eW2, eb2, eW3, eb3)
        shared = _shared_mlp(x, sW1, sb1, sW2, sb2, sW3, sb3)
        gates = jax.nn.softmax(x @ gW + gb, axis=-1)
        topv, topi = jax.lax.top_k(gates, TOPK)
        topw = jax.nn.softmax(topv, axis=-1)
        sel = jnp.take_along_axis(all_out, topi[:, :, None, :], axis=-1)
        gated = jnp.sum(sel * topw[:, :, None, :], axis=-1)
        return shared + gated
    h = _L0_tok_ref(x, L0_tok_ln1_g, L0_tok_ln1_b, L0_tok_W1, L0_tok_b1, L0_tok_ln2_g, L0_tok_ln2_b, L0_tok_Wp1, L0_tok_bp1, L0_tok_lnp_g, L0_tok_lnp_b, L0_tok_Wp2, L0_tok_bp2)
    h = jnp.concatenate([h, txt], axis=1)
    h = h + _L0_attn_ref(_layernorm(h, axis=-1), L0_attn_ln_g, L0_attn_ln_b, L0_attn_w_qkv, L0_attn_w_out, L0_attn_b_out, L0_attn_res_kernel)
    h = h + _L0_ffn_ref(_layernorm(h, axis=-1), L0_ffn_Wr, L0_ffn_br, L0_ffn_ln_g, L0_ffn_ln_b, L0_ffn_W1, L0_ffn_b1, L0_ffn_W2, L0_ffn_b2)
    h = h + _L1_attn_ref(_layernorm(h, axis=-1), L1_attn_e, L1_attn_p, L1_attn_ln_scale, L1_attn_W_q, L1_attn_W_k, L1_attn_W_v, L1_attn_W_o, L1_attn_gamma)
    h = h + _L1_ffn_ref(_layernorm(h, axis=-1), L1_ffn_sW1, L1_ffn_sb1, L1_ffn_sW2, L1_ffn_sb2, L1_ffn_sW3, L1_ffn_sb3, L1_ffn_eW1, L1_ffn_eb1, L1_ffn_eW2, L1_ffn_eb2, L1_ffn_eW3, L1_ffn_eb3, L1_ffn_gW, L1_ffn_gb)
    return h

_drawn_inputs = setup_inputs


def setup_inputs(seed=0):
    import zlib

    import numpy as np

    out = dict(_drawn_inputs(seed))
    spreads = {'L0_tok_ln1_g': (1.0, 0.2),
     'L0_tok_ln1_b': (0.0, 0.1),
     'L0_tok_b1': (0.0, 0.1),
     'L0_tok_ln2_g': (1.0, 0.2),
     'L0_tok_ln2_b': (0.0, 0.1),
     'L0_tok_bp1': (0.0, 0.1),
     'L0_tok_lnp_g': (1.0, 0.2),
     'L0_tok_lnp_b': (0.0, 0.1),
     'L0_tok_bp2': (0.0, 0.1),
     'L0_attn_ln_g': (1.0, 0.2),
     'L0_attn_ln_b': (0.0, 0.64),
     'L0_attn_b_out': (0.0, 0.1),
     'L0_ffn_br': (0.0, 0.1),
     'L0_ffn_ln_g': (1.0, 0.2),
     'L0_ffn_ln_b': (0.0, 0.1),
     'L0_ffn_b1': (0.0, 0.1),
     'L0_ffn_b2': (0.0, 0.1),
     'L1_attn_ln_scale': (1.0, 0.2),
     'L1_attn_gamma': (1.0, 0.2),
     'L1_ffn_sb1': (0.0, 0.8),
     'L1_ffn_sb2': (0.0, 0.28),
     'L1_ffn_sb3': (0.0, 0.1),
     'L1_ffn_eb1': (0.0, 0.8),
     'L1_ffn_eb2': (0.0, 0.63),
     'L1_ffn_eb3': (0.0, 0.1),
     'L1_ffn_gb': (0.0, 0.309)}
    factors = {'L0_attn_res_kernel': 3.148, 'L1_ffn_eW1': 3.335, 'L1_ffn_eW2': 2.711}
    for name, (base, spread) in spreads.items():
        noise = np.random.default_rng([zlib.crc32(name.encode()), seed]).standard_normal(out[name].shape)
        drawn = base * np.exp(spread * noise) if base else spread * noise
        out[name] = jnp.asarray(drawn.astype(out[name].dtype))
    for name, factor in factors.items():
        out[name] = (out[name] * factor).astype(out[name].dtype)
    return out
```

```python
from contextlib import ExitStack

import numpy as np

import concourse.bass as bass
from concourse import mybir

F32 = mybir.dt.float32
U32 = mybir.dt.uint32
ALU = mybir.AluOpType
ACT = mybir.ActivationFunctionType
AX = mybir.AxisListType

B = 8
D = 64
NI = 64
NX = 77
COPIES = 3
N = COPIES * NI + NX
LM = 128
PAD = -N % LM
GRP = (N + PAD) // LM
ZL = PAD // GRP
NL = LM - ZL + 1
U = NI + NX + 1
UT = U // 2
UL = U + NL
H = 8
DH = 32
SC = DH ** -0.5
TAPS = 33
HALO = TAPS // 2
CW = 304
NP = 270
TT = 90
NT = 3
SW = NL + DH
ITERS = 6
EPS = 1e-5
PF = 192
E0 = 8
EH = 256
E1 = 4
ROOT = float(np.sqrt(ZL))

C_ID, C_CEN, C_AVG, C_AVP, C_D, C_IOTA, C_EPS, C_EPS2, C_DV, C_KW = (
    0, 128, 192, 256, 384, 475, 483, 484, 485, 486)
C_BS = 488
C_W = 488 + 32


def shape_constants():
    c = np.zeros((128, C_W), np.float32)
    c[:, C_ID:C_ID + 128] = np.eye(128)
    c[:D, C_CEN:C_CEN + D] = np.eye(D) - 1.0 / D
    c[:D, C_AVG:C_AVG + D] = 1.0 / D
    c[:, C_AVP:C_AVP + 128] = 1.0 / PF
    c[:NL, C_D:C_D + NL] = 1.0
    c[0, C_D:C_D + NL] = ROOT
    c[:, C_IOTA:C_IOTA + 8] = np.arange(8)
    c[:, C_EPS] = EPS
    c[:, C_EPS2] = EPS * EPS
    c[:, C_DV] = 1.0
    c[0, C_DV] = ROOT
    c[:, C_KW:C_KW + 2] = 1.0
    c[:NI, C_KW] = COPIES
    for p in range(4):
        c[0:D, C_BS + 8 * p + 2 * p] = 1.0
        c[D:128, C_BS + 8 * p + 2 * p + 1] = 1.0
    return c


V_B1, V_G2, V_B2, V_BP1, V_GP, V_BP, V_BP2, V_GA, V_BA, V_BO, V_LS, V_SB1 = range(12)
V_FG, V_FB = 12, 20
V_W = 28
W_P1, W_P2, W_QKV, W_R, W_G, W_S1, W_S2, W_E1, W_Q, W_K, W_VT, W_OT, W_F1 = (
    0, 64, 128, 896, 904, 908, 972, 1100, 1612, 2124, 2636, 3148, 3660)
W_W = 3660 + E0 * EH
X_B1, X_SB2, X_EB1, X_EB2, X_GAM, X_GAR, X_BR, X_GB, X_KD, X_S3, X_E2, X_E3, X_WVT, X_WO, X_F2 = (
    0, 16, 17, 21, 23, 31, 33, 41, 45, 111, 175, 431, 559, 815, 943)
X_W = 943 + 2 * E0 * D


LOOP1 = ["n_proj", "n_qk", "n_score", "n_max", "n_sub", "n_exp", "n_z", "n_e0", "n_a", "n_cs", "n_c1", "n_cm"]
LOOP2 = ["f_x", "f_u", "f_res", "f_qk", "f_v", "f_qks", "f_s3", "f_s1", "f_vu", "f_e3", "f_t3", "f_p3", "f_as",
         "f_t2", "f_d1", "f_w", "f_at", "f_aa", "f_y0", "f_w0", "f_st", "f_m1", "f_m2", "f_p1", "f_t1", "f_ta",
         "f_tx", "f_td", "f_pt", "f_um", "f_o", "f_oo", "f_out", "f_sub3", "f_m3", "f_mm1", "f_e1", "f_z1",
         "f_e10", "f_z3", "f_r3"]
LOOP3 = ["m_x", "m_ws", "m_h", "m_g", "m_y", "m_yw", "m_ac", "m_o", "m_res"]
LOOP4 = ["d_x", "d_q", "d_k", "d_qa", "d_ka", "d_sq", "d_nq", "d_nk", "d_n", "d_row", "d_v", "d_vm", "d_s", "d_cl", "d_e",
         "d_pv", "d_res"]
LOOP5 = ["g_x", "g_l1", "g_s1", "g_h1", "g_l2", "g_h2", "g_l3", "g_gw", "g_sum", "g_fin", "g_put"]


def program(nc, xpatch, txt, w1, ln1, vec, mat, wide, b2, b3, const, out):
    with ExitStack() as ctx:
        def sb(name, shape, dt=F32):
            return ctx.enter_context(nc.sbuf_tensor(name, shape, dt))

        sems = {}

        def sem(name):
            if name not in sems:
                sems[name] = nc.alloc_semaphore(name=name)
            return sems[name]

        def phase_over():
            done = [sems.pop(name) for name in list(sems) if name != "loaded"]
            nc.clear_and_free_semaphores(done)
            nc.all_engine_barrier()

        PS = ctx.enter_context(nc.psum_tensor("PS", [128, 8, 512], F32))
        CO = sb("CO", [128, C_W])
        VE = sb("VE", [D, V_W])
        MA = sb("MA", [D, W_W])
        WI = sb("WI", [128, X_W])
        B2 = sb("B2", [E0, D])
        B3 = sb("B3", [E1 + 1, D])
        W1A = sb("W1A", [128, D])
        W1B = sb("W1B", [D, D])
        G1A = sb("G1A", [128, 2])
        G1B = sb("G1B", [D, 2])
        ident = CO[:, C_ID:C_ID + 128]
        NG = sb("NG", [128, H + 2])
        TAP = sb("TAP", [128, HALO + 1, D])
        FW1 = sb("FW1", [D, E0, EH])
        FB1 = sb("FB1", [128, 2 * E0])
        WVO = sb("WVO", [D, H, D])
        HU = sb("HU", [D, B, U])
        XL = sb("XL", [D, B, U])
        HX = sb("HX", [D, B, U])
        XAP = sb("XAP", [D, B, UL])
        XC = sb("XC", [128, B, CW])
        AA = sb("AA", [NL, B, H, NL])
        CM = sb("CM", [NL, B, H])
        RC = sb("RC", [NL, 1])
        RCK = sb("RCK", [NL, 1])
        HT = sb("HT", [D, B, NP])

        s_load = sem("loaded")

        def col(t, c, p=128, n=1):
            return t[0:p, c:c + n]

        def at(i, n, k):
            return i * n + (k + 1)

        def started(eng, names):
            for name in names:
                eng.sem_inc(sem(name), 1)

        def need(eng, *waits):
            for name, value in waits:
                eng.wait_ge(sem(name), value)
            eng.wait_ge(s_load, 16)

        def ln_pe(pe, tag, src, ready, chunks, width):
            pe.wait_ge(*ready)
            for c in range(chunks):
                nc.tensor.matmul(PS[0:D, c, 0:width], CO[0:D, C_CEN:C_CEN + D], src(c),
                                 start=True, stop=True).then_inc(sem(tag + "_centred"), 1)
            for c in range(chunks):
                pe.wait_ge(sem(tag + "_squared"), c + 1)
                if c >= 3:
                    pe.wait_ge(sem(tag + "_rooted"), c - 2)
                nc.tensor.matmul(PS[0:D, 5 + c % 3, 0:width], CO[0:D, C_AVG:C_AVG + D],
                                 LSQ[:, c % 2, 0:width],
                                 start=True, stop=True).then_inc(sem(tag + "_var"), 1)

        def ln_act(act, tag, chunks, width, twice):
            for c in range(chunks):
                act.wait_ge(sem(tag + "_centred"), c + 1)
                if c >= 2:
                    act.wait_ge(sem(tag + "_var"), c - 1)
                nc.scalar.activation(LSQ[:, c % 2, 0:width], PS[0:D, c, 0:width],
                                     ACT.Square).then_inc(sem(tag + "_squared"), 1)
                if c >= 1:
                    ln_root(act, tag, c - 1, width, twice)
            ln_root(act, tag, chunks - 1, width, twice)

        def ln_root(act, tag, c, width, twice):
            act.wait_ge(sem(tag + "_var"), c + 1)
            if c >= 2:
                act.wait_ge(sem(tag + "_inv"), len(twice) * (c - 1))
            for n, t in enumerate(twice):
                last = nc.scalar.activation(LST[:, c % 2, n, 0:width], PS[0:D, 5 + c % 3, 0:width],
                                            ACT.Sqrt, scale=1.0 + EPS if t else 1.0,
                                            bias=col(CO, C_EPS2 if t else C_EPS, D))
            last.then_inc(sem(tag + "_rooted"), 1)

        def ln_dve(dve, tag, chunks, width, outs):
            k = len(outs)
            for c in range(chunks):
                dve.wait_ge(sem(tag + "_rooted"), c + 1)
                for n in range(k):
                    nc.vector.reciprocal(LRS[:, c % 2, n, 0:width],
                                         LST[:, c % 2, n, 0:width]).then_inc(sem(tag + "_inv"), 1)
                for n, dst in enumerate(outs):
                    dve.wait_ge(sem(tag + "_inv"), k * c + n + 1)
                    nc.vector.tensor_tensor(dst(c), PS[0:D, c, 0:width], LRS[:, c % 2, n, 0:width],
                                            ALU.mult).then_inc(sem(tag + "_done"), 1)

        LSQ = sb("LSQ", [D, 2, 512])
        LST = sb("LST", [D, 2, 2, 512])
        LRS = sb("LRS", [D, 2, 2, 512])

        S = ExitStack()

        def ts(name, shape, dt=F32):
            return S.enter_context(nc.sbuf_tensor(name, shape, dt))

        XA0 = ts("XA0", [128, 512])
        XA1 = ts("XA1", [D, 512])
        XC0 = ts("XC0", [128, 512])
        XC1 = ts("XC1", [D, 512])
        XQ0 = ts("XQ0", [128, 512])
        XQ1 = ts("XQ1", [D, 512])
        XS = ts("XS", [128, 512])
        TK = ts("TK", [D, 512])
        TN = ts("TN", [D, 512])
        WOK = ts("WOK", [128, 2, (TAPS + 1) * D])
        TS = B * NI
        assert TS == 512
        with nc.Block() as block:
            @block.sync
            def _(sp):
                sp.dma_start(CO[:, :], const).then_inc(s_load, 16)
                sp.dma_start(XA0[:, :], xpatch[0:128, :]).then_inc(s_load, 16)
                sp.dma_start(XA1[:, :], xpatch[128:PF, :]).then_inc(s_load, 16)
                sp.dma_start(G1A[:, :], ln1[0:128, :]).then_inc(s_load, 16)
                sp.dma_start(G1B[:, :], ln1[128:PF, :]).then_inc(s_load, 16)
                sp.dma_start(W1A[:, :], w1[0:128, :]).then_inc(s_load, 16)
                sp.dma_start(W1B[:, :], w1[128:PF, :]).then_inc(s_load, 16)
                sp.dma_start(VE[:, :], vec).then_inc(s_load, 16)
                sp.dma_start(B2[:, :], b2).then_inc(s_load, 16)
                sp.dma_start(B3[:, :], b3).then_inc(s_load, 16)
                sp.dma_start(HU[:, :, NI:NI + NX], txt.rearrange("f (b n) -> f b n", b=B)).then_inc(s_load, 16)
                sp.wait_ge(sem("seq_built"), 2)
                flat = XC[:, :, :].rearrange("p b w -> p (b w)")
                sp.dma_start(flat[D:128, 0:B * CW - 1], flat[0:D, 1:B * CW]).then_inc(sem("seq_shift"), 16)
                sp.wait_ge(sem("seq_shift"), 16)

            @block.scalar
            def _(act):
                act.dma_start(MA[:, :], mat).then_inc(sem("mats"), 16)
                act.dma_start(WI[:, :], wide).then_inc(sem("wides"), 16)
                act.wait_ge(sem("p_cent"), 2)
                nc.scalar.activation(XQ0[:, :], XC0[:, :], ACT.Square)
                nc.scalar.activation(XQ1[:, :], XC1[:, :], ACT.Square).then_inc(sem("p_sq"), 1)
                act.wait_ge(sem("p_var"), 1)
                nc.scalar.activation(XS[:, :], PS[:, 1, :], ACT.Sqrt, bias=col(CO, C_EPS)).then_inc(sem("p_std"), 1)
                ln_act(act, "t2", 1, TS, [False])
                ln_act(act, "tp", 1, TS, [False])
                act.wait_ge(sem("tp_aff"), 1)
                nc.scalar.activation(TN[:, :], XA1[:, :], ACT.Silu).then_inc(sem("silu"), 1)
                ln_act(act, "a", 4, 2 * U, [False, True])
                act.wait_ge(sem("pool_raw"), 2)
                nc.scalar.mul(XAP[:, :, U + 1:UL], XAP[:, :, U + 1:UL], 1.0 / GRP).then_inc(sem("pooled"), 1)
                for c in range(5):
                    act.wait_ge(sem("tap_mm"), c + 1)
                    k = 8 if c < 4 else 2
                    src = PS[:, 5 + c % 3, 0:k * D].rearrange("p (j e o) -> p j e o", e=2, o=D)
                    nc.scalar.copy(TAP[0:D, 4 * c:4 * c + k // 2, :], src[0:D, :, 0, :])
                    nc.scalar.copy(TAP[D:128, 4 * c:4 * c + k // 2, :],
                                   src[D:128, :, 1, :]).then_inc(sem("tap_out"), 1)
                act.wait_ge(sem("wvo_mm"), 1)
                nc.scalar.mul(WVO[:, :, :], PS[0:D, 0, :].rearrange("p (h o) -> p h o", h=H),
                              VE[:, V_LS:V_LS + 1]).then_inc(sem("wvo"), 1)

            @block.gpsimd
            def _(pool):
                nc.gpsimd.memset(XC[:, :, :], 0.0).then_inc(sem("seq_zero"), 1)
                nc.gpsimd.memset(HU[:, :, U - 1:U], 0.0)
                nc.gpsimd.memset(XAP[:, :, U - 1:U + 1], 0.0).then_inc(sem("zeroed"), 1)
                nc.gpsimd.memset(HT[:, :, N:NP], 0.0)
                nc.gpsimd.memset(WOK[:, :, TAPS * D:], 0.0)
                pool.wait_ge(sem("wides"), 16)
                for t in range(2):
                    wo = WI[:, X_WO + t * D:X_WO + (t + 1) * D].unsqueeze(1).broadcast_to([128, TAPS, D])
                    kd = WI[:, X_KD + t * TAPS:X_KD + (t + 1) * TAPS].unsqueeze(2).broadcast_to([128, TAPS, D])
                    nc.gpsimd.tensor_tensor(WOK[:, t, 0:TAPS * D].rearrange("p (k o) -> p k o", o=D),
                                            wo, kd, ALU.mult).then_inc(sem("wok"), 1)
                pool.wait_ge(sem("mats"), 16)
                pool.wait_ge(s_load, 16 * 11)
                nc.gpsimd.tensor_tensor(FW1[:, :, :], MA[:, W_F1:W_F1 + E0 * EH].rearrange("p (e n) -> p e n", e=E0),
                                        VE[:, V_FG:V_FG + E0].unsqueeze(2).broadcast_to([D, E0, EH]),
                                        ALU.mult).then_inc(sem("fw1"), 1)
                nc.gpsimd.tensor_scalar(MA[:, W_Q:W_Q + 2 * H * D], MA[:, W_Q:W_Q + 2 * H * D],
                                        VE[:, V_LS:V_LS + 1], None, ALU.mult).then_inc(sem("wqk"), 1)

            @block.tensor
            def _(pe):
                pe.wait_ge(s_load, 16 * 11)
                avp = CO[:, C_AVP:C_AVP + 128]
                nc.tensor.matmul(PS[:, 0, :], avp, XA0[:, :], start=True, stop=False)
                nc.tensor.matmul(PS[:, 0, :], avp[0:D, :], XA1[:, :], start=False, stop=True).then_inc(sem("p_mean"), 1)
                pe.wait_ge(sem("p_sq"), 1)
                nc.tensor.matmul(PS[:, 1, :], avp, XQ0[:, :], start=True, stop=False)
                nc.tensor.matmul(PS[:, 1, :], avp[0:D, :], XQ1[:, :], start=False, stop=True).then_inc(sem("p_var"), 1)
                pe.wait_ge(sem("p_aff"), 2)
                nc.tensor.matmul(PS[0:D, 2, :], W1A[:, :], XC0[:, :], start=True, stop=False)
                nc.tensor.matmul(PS[0:D, 2, :], W1B[:, :], XC1[:, :], start=False, stop=True).then_inc(sem("tok1"), 1)
                ln_pe(pe, "t2", lambda c: TK[:, :], (sem("tok1_b"), 1), 1, TS)
                pe.wait_ge(sem("t2_aff"), 1)
                pe.wait_ge(sem("mats"), 16)
                nc.tensor.matmul(PS[0:D, 3, :], MA[:, W_P1:W_P1 + D], TN[:, :], start=True, stop=True).then_inc(sem("tok2"), 1)
                ln_pe(pe, "tp", lambda c: TK[:, :], (sem("tok2_b"), 1), 1, TS)
                pe.wait_ge(sem("silu"), 1)
                nc.tensor.matmul(PS[0:D, 4, :], MA[:, W_P2:W_P2 + D], TN[:, :], start=True, stop=True).then_inc(sem("tok3"), 1)
                ln_pe(pe, "a", lambda c: HU[:, 2 * c:2 * c + 2, :].rearrange("p b n -> p (b n)"), (sem("stream"), 1), 4, 2 * U)
                pe.wait_ge(sem("a_done"), 8)
                for j in range(2 * E0):
                    nc.tensor.matmul(PS[:, 4, j:j + 1], MA[:, W_F1 + j * 128:W_F1 + (j + 1) * 128],
                                     VE[:, V_FB + j // 2:V_FB + j // 2 + 1], start=True, stop=True
                                     ).then_inc(sem("fb1_mm"), 1)
                pe.wait_ge(sem("wok"), 2)
                for c in range(5):
                    w = 512 if c < 4 else 2 * D
                    if c >= 3:
                        pe.wait_ge(sem("tap_out"), c - 2)
                    for t in range(2):
                        last = nc.tensor.matmul(PS[:, 5 + c % 3, 0:w], WI[:, X_WVT + t * 128:X_WVT + (t + 1) * 128],
                                                WOK[:, t, c * 512:c * 512 + w], start=t == 0, stop=t == 1)
                    last.then_inc(sem("tap_mm"), 1)
                for h in range(H):
                    last = nc.tensor.matmul(PS[0:D, 0, h * D:(h + 1) * D], MA[:, W_VT + h * D:W_VT + (h + 1) * D],
                                            MA[:, W_OT + h * D:W_OT + (h + 1) * D], start=True, stop=True)
                last.then_inc(sem("wvo_mm"), 1)

            @block.vector
            def _(dve):
                v = nc.vector
                dve.wait_ge(sem("p_mean"), 1)
                v.tensor_tensor(XC0[:, :], XA0[:, :], PS[:, 0, :], ALU.subtract).then_inc(sem("p_cent"), 1)
                v.tensor_tensor(XC1[:, :], XA1[:, :], PS[0:D, 0, :], ALU.subtract).then_inc(sem("p_cent"), 1)
                dve.wait_ge(sem("p_std"), 1)
                v.reciprocal(XQ0[:, :], XS[:, :]).then_inc(sem("p_rstd"), 1)
                dve.wait_ge(sem("p_rstd"), 1)
                v.tensor_tensor(XA0[:, :], XC0[:, :], XQ0[:, :], ALU.mult).then_inc(sem("p_norm"), 1)
                v.tensor_tensor(XA1[:, :], XC1[:, :], XQ0[0:D, :], ALU.mult).then_inc(sem("p_norm"), 1)
                dve.wait_ge(sem("p_norm"), 2)
                v.tensor_scalar(XC0[:, :], XA0[:, :], G1A[:, 0:1], G1A[:, 1:2], ALU.mult, ALU.add).then_inc(sem("p_aff"), 1)
                v.tensor_scalar(XC1[:, :], XA1[:, :], G1B[:, 0:1], G1B[:, 1:2], ALU.mult, ALU.add).then_inc(sem("p_aff"), 1)
                dve.wait_ge(sem("tok1"), 1)
                v.tensor_scalar(TK[:, :], PS[0:D, 2, :], VE[:, V_B1:V_B1 + 1], None, ALU.add).then_inc(sem("tok1_b"), 1)
                ln_dve(dve, "t2", 1, TS, [lambda c: TN[:, :]])
                dve.wait_ge(sem("t2_done"), 1)
                v.tensor_scalar(TN[:, :], TN[:, :], VE[:, V_G2:V_G2 + 1], VE[:, V_B2:V_B2 + 1], ALU.mult, ALU.add
                                ).then_inc(sem("t2_aff"), 1)
                dve.wait_ge(sem("tok2"), 1)
                v.tensor_scalar(TK[:, :], PS[0:D, 3, :], VE[:, V_BP1:V_BP1 + 1], None, ALU.add).then_inc(sem("tok2_b"), 1)
                ln_dve(dve, "tp", 1, TS, [lambda c: TN[:, :]])
                dve.wait_ge(sem("tp_done"), 1)
                v.tensor_scalar(XA1[:, :], TN[:, :], VE[:, V_GP:V_GP + 1], VE[:, V_BP:V_BP + 1], ALU.mult, ALU.add
                                ).then_inc(sem("tp_aff"), 1)
                dve.wait_ge(sem("tok3"), 1)
                dve.wait_ge(sem("zeroed"), 1)
                v.tensor_scalar(HU[:, :, 0:NI], PS[0:D, 4, :].rearrange("p (b n) -> p b n", b=B),
                                VE[:, V_BP2:V_BP2 + 1], None, ALU.add).then_inc(sem("stream"), 1)
                flat = lambda t, c: t[:, 2 * c:2 * c + 2, :].rearrange("p b n -> p (b n)")
                ln_dve(dve, "a", 4, 2 * U, [lambda c: flat(XL, c), lambda c: flat(HX, c)])
                dve.wait_ge(sem("a_done"), 8)
                v.tensor_scalar(XAP[:, :, 0:U - 1], HX[:, :, 0:U - 1], VE[:, V_GA:V_GA + 1], VE[:, V_BA:V_BA + 1],
                                ALU.mult, ALU.add).then_inc(sem("a_in"), 1)
                dve.wait_ge(sem("a_in"), 1)
                dve.wait_ge(sem("seq_zero"), 1)
                v.tensor_copy(XC[0:D, :, HALO:HALO + COPIES * NI].rearrange("p b (r n) -> p b r n", r=COPIES),
                              XAP[:, :, 0:NI].unsqueeze(2).broadcast_to([D, B, COPIES, NI])).then_inc(sem("seq_built"), 1)
                v.tensor_copy(XC[0:D, :, HALO + COPIES * NI:HALO + N], XAP[:, :, NI:NI + NX]).then_inc(sem("seq_built"), 1)
                dve.wait_ge(sem("seq_built"), 2)
                first = GRP - PAD % GRP
                v.tensor_reduce(XAP[:, :, U + 1:U + 2], XC[0:D, :, HALO:HALO + first], AX.X, ALU.add
                                ).then_inc(sem("pool_raw"), 1)
                v.tensor_reduce(XAP[:, :, U + 2:UL],
                                XC[0:D, :, HALO + first:HALO + N].rearrange("p b (j t) -> p b j t", t=GRP),
                                AX.X, ALU.add).then_inc(sem("pool_raw"), 1)
                v.scalar_tensor_tensor(out=HX[:, :, :], in0=HU[:, :, :], scalar=VE[:, V_BO:V_BO + 1], in1=XL[:, :, :],
                                       op0=ALU.add, op1=ALU.add).then_inc(sem("resid"), 1)
                dve.wait_ge(sem("fb1_mm"), 2 * E0)
                dve.wait_ge(sem("wides"), 16)
                v.tensor_scalar(NG[:, :], WI[:, X_GAM:X_GAM + H + 2], -1.0, None, ALU.mult)
                v.tensor_tensor(FB1[:, :], PS[:, 4, 0:2 * E0], WI[:, X_B1:X_B1 + 2 * E0], ALU.add).then_inc(sem("fb1"), 1)
        phase_over()
        S.close()


        S = ExitStack()
        QL = ts("QL", [128, 4, NL])
        DD = ts("DD", [NL, H, NL])
        EE = ts("EE", [NL, H, NL])
        MX = ts("MX", [NL, H])
        MX2 = ts("MX2", [NL, H])
        ZZ = ts("ZZ", [NL, 4, H])
        with nc.Block() as block:
            @block.sync
            def _(sp):
                started(sp, LOOP1)

            @block.tensor
            def _(pe):
                with pe.Fori(0, B) as i:
                    need(pe, ("n_qk", at(i, 1, 0)))
                    for j in range(4):
                        last = nc.tensor.matmul(PS[:, 0, j * NL:(j + 1) * NL],
                                                MA[:, W_QKV + j * 128:W_QKV + (j + 1) * 128],
                                                XAP[:, i, U:UL], start=True, stop=True)
                    last.then_inc(sem("n_proj"), 1)
                    need(pe, ("n_qk", at(i, 1, 1)), ("n_sub", at(i, 1, 0)))
                    for g in range(H):
                        r, hh = g // 2, g % 2
                        last = nc.tensor.matmul(PS[0:NL, 1 + r, hh * NL:(hh + 1) * NL],
                                                QL[32 * r:32 * r + 32, hh, :], QL[32 * r:32 * r + 32, 2 + hh, :],
                                                start=True, stop=True)
                    last.then_inc(sem("n_score"), 1)
                    need(pe, ("n_a", at(i, 1, 1)), ("n_cm", at(i, 1, 0)))
                    for q in range(2):
                        last = nc.tensor.matmul(PS[0:NL, 5 + q, 0:4 * NL], CO[0:NL, C_D:C_D + NL],
                                                AA[:, i, 4 * q:4 * q + 4, :].rearrange("p h n -> p (h n)"),
                                                start=True, stop=True)
                    last.then_inc(sem("n_cs"), 1)

            @block.scalar
            def _(act):
                with act.Fori(0, B) as i:
                    need(act, ("n_proj", at(i, 1, 1)), ("n_score", at(i, 1, 0)))
                    nc.scalar.copy(QL[:, :, :], PS[:, 0, 0:4 * NL].rearrange("p (j n) -> p j n", j=4)
                                   ).then_inc(sem("n_qk"), 1)
                    need(act, ("n_sub", at(i, 1, 1)), ("n_a", at(i, 1, 0)))
                    nc.scalar.activation(EE[:, :, :], DD[:, :, :], ACT.Exp, scale=SC).then_inc(sem("n_exp"), 1)

            @block.vector
            def _(dve):
                v = nc.vector
                score = PS[0:NL, 1:5, 0:2 * NL].rearrange("p r (k n) -> p r k n", k=2)
                with dve.Fori(0, B) as i:
                    need(dve, ("n_score", at(i, 1, 1)))
                    v.tensor_reduce(MX[:, :].rearrange("p (r k) -> p r k", k=2), score, AX.X, ALU.max
                                    ).then_inc(sem("n_max"), 1)
                    need(dve, ("n_max", at(i, 1, 1)), ("n_exp", at(i, 1, 0)))
                    v.tensor_tensor(DD[:, :, :].rearrange("p (r k) n -> p r k n", k=2), score,
                                    MX[:, :].rearrange("p (r k) -> p r k", k=2).unsqueeze(3).broadcast_to([NL, 4, 2, NL]),
                                    ALU.subtract).then_inc(sem("n_sub"), 1)
                    need(dve, ("n_exp", at(i, 1, 1)))
                    v.tensor_reduce(ZZ[:, 0, :], EE[:, :, :], AX.X, ALU.add).then_inc(sem("n_z"), 1)
                    need(dve, ("n_z", at(i, 4, 1)))
                    v.scalar_tensor_tensor(out=ZZ[:, 1, :], in0=EE[:, :, 0], scalar=float(ZL - 1), in1=ZZ[:, 0, :],
                                           op0=ALU.mult, op1=ALU.add).then_inc(sem("n_z"), 1)
                    need(dve, ("n_z", at(i, 4, 2)))
                    v.reciprocal(ZZ[:, 2, :], ZZ[:, 1, :]).then_inc(sem("n_z"), 1)
                    v.tensor_scalar(EE[:, :, 0], EE[:, :, 0], ROOT, None, ALU.mult).then_inc(sem("n_e0"), 1)
                    need(dve, ("n_z", at(i, 4, 3)))
                    v.tensor_scalar(ZZ[:, 3, :], ZZ[:, 2, :], CO[0:NL, C_DV:C_DV + 1], None, ALU.mult
                                    ).then_inc(sem("n_z"), 1)
                    need(dve, ("n_z", at(i, 4, 4)), ("n_e0", at(i, 1, 1)))
                    v.tensor_tensor(AA[:, i, :, :], EE[:, :, :], ZZ[:, 3, :].unsqueeze(2).broadcast_to([NL, H, NL]),
                                    ALU.mult).then_inc(sem("n_a"), 1)
                    need(dve, ("n_cs", at(i, 1, 1)))
                    sums = PS[0:NL, 5:7, 0:4 * NL].rearrange("p q (k n) -> p q k n", k=4)
                    v.tensor_reduce(MX2[:, :].rearrange("p (q k) -> p q k", k=4), sums[:, :, :, 1:NL], AX.X, ALU.max
                                    ).then_inc(sem("n_c1"), 1)
                    need(dve, ("n_c1", at(i, 1, 1)))
                    v.scalar_tensor_tensor(out=CM[:, i, :].rearrange("p (q k) -> p q k", k=4), in0=sums[:, :, :, 0],
                                           scalar=1.0 / ROOT, in1=MX2[:, :].rearrange("p (q k) -> p q k", k=4),
                                           op0=ALU.mult, op1=ALU.max).then_inc(sem("n_cm"), 1)
                dve.wait_ge(sem("n_cm"), B + 1)
                v.tensor_reduce(MX2[:, 0:1], CM[:, :, :], AX.XY, ALU.max).then_inc(sem("n_top"), 1)
                dve.wait_ge(sem("n_top"), 1)
                v.reciprocal(RC[:, :], MX2[:, 0:1]).then_inc(sem("n_rc"), 1)
                dve.wait_ge(sem("n_rc"), 1)
                v.tensor_scalar(RCK[:, :], RC[:, :], (13.0 / 4.0) ** ITERS, None, ALU.mult)
        phase_over()
        S.close()

        S = ExitStack()
        XS = ts("XS_", [D, UL])
        QK = ts("QK", [128, 2, 2, UL])
        VU = ts("VU", [UT, 2, H * DH])
        AS = ts("AS", [NL, H, NL])
        AT = ts("AT", [NL, H, NL])
        M3 = ts("M3", [NL, H])
        E3 = ts("E3", [NL, H, U])
        Z3 = ts("Z3", [NL, 4, H])
        P3 = ts("P3", [UT, H, 2, NL])
        M1 = ts("M1", [UT, 2 * H])
        E1_ = ts("E1_", [UT, 2 * H, NL])
        P1 = ts("P1", [UT, 2 * H, NL])
        Z1 = ts("Z1", [UT, 3, 2 * H])
        PT = ts("PT", [NL, H, U])
        ST = ts("ST", [NL, H, SW])
        TA = ts("TA", [NL, H, SW])
        TX = ts("TX", [NL, H, SW])
        TD = ts("TD", [NL, H, SW])
        UU = ts("UU", [NL, H, DH])
        OO = ts("OO", [128, 2, U])
        with nc.Block() as block:
            @block.sync
            def _(sp):
                started(sp, LOOP2)

            def taps(i, j0, j1):
                for j in range(j0, j1):
                    nc.tensor.matmul(PS[0:D, 3, 0:NP], TAP[:, j, :], XC[:, i, 2 * j:2 * j + NP],
                                     start=j == 0, stop=False, skip_group_check=True)

            @block.tensor
            def _(pe):
                with pe.Fori(0, B) as i:
                    need(pe, ("f_x", at(i, 1, 1)), ("f_u", at(i, 1, 0)), ("f_res", at(i, 2, 0)), ("f_oo", at(i, 1, 0)))
                    for j in range(4):
                        last = nc.tensor.matmul(PS[:, j // 2, (j % 2) * UL:(j % 2 + 1) * UL],
                                                MA[:, W_QKV + j * 128:W_QKV + (j + 1) * 128],
                                                XS[:, :], start=True, stop=True)
                    last.then_inc(sem("f_qk"), 1)
                    for t in range(2):
                        last = nc.tensor.matmul(PS[0:UT, 2, t * 256:(t + 1) * 256], XS[:, t * UT:(t + 1) * UT],
                                                MA[:, W_QKV + 512:W_QKV + 768], start=True, stop=True)
                    last.then_inc(sem("f_v"), 1)
                    need(pe, ("f_qks", at(i, 2, 2)), ("f_st", at(i, 2 * ITERS, 0)))
                    for g in range(H):
                        r, hh = g // 2, g % 2
                        last = nc.tensor.matmul(PS[0:NL, 4 + r, hh * U:(hh + 1) * U],
                                                QK[32 * r:32 * r + 32, 0, hh, U:UL], QK[32 * r:32 * r + 32, 1, hh, 0:U],
                                                start=True, stop=True)
                    last.then_inc(sem("f_s3"), 1)
                    need(pe, ("f_vu", at(i, 1, 1)))
                    for g in range(H):
                        r, hh = g // 2, g % 2
                        for t in range(2):
                            c = (2 * hh + t) * NL
                            last = nc.tensor.matmul(PS[0:UT, r, c:c + NL],
                                                    QK[32 * r:32 * r + 32, 0, hh, t * UT:(t + 1) * UT],
                                                    QK[32 * r:32 * r + 32, 1, hh, U:UL], start=True, stop=True)
                    last.then_inc(sem("f_s1"), 1)
                    need(pe, ("f_e3", at(i, 1, 1)))
                    for g in range(H):
                        for t in range(2):
                            c = ((g % 2) * 2 + t) * NL
                            last = nc.tensor.transpose(PS[0:UT, 4 + g // 2, c:c + NL], E3[:, g, t * UT:(t + 1) * UT],
                                                       ident[0:NL, 0:NL])
                    last.then_inc(sem("f_t3"), 1)
                    need(pe, ("f_p3", at(i, 1, 1)), ("f_as", at(i, 1, 1)))
                    for g in range(H):
                        last = nc.tensor.transpose(PS[0:NL, 4 + g // 4, (g % 4) * NL:(g % 4 + 1) * NL], AS[:, g, :],
                                                   ident[0:NL, 0:NL])
                    last.then_inc(sem("f_t2"), 1)
                    need(pe, ("f_d1", at(i, 1, 1)))
                    for g in range(H):
                        h = g % 2 * 4 + g // 2
                        for t in range(2):
                            last = nc.tensor.matmul(PS[0:NL, 3, g * DH:(g + 1) * DH], P3[:, g, t, :],
                                                    VU[:, t, h * DH:(h + 1) * DH], start=t == 0, stop=t == 1)
                    last.then_inc(sem("f_w"), 1)
                    need(pe, ("f_at", at(i, 1, 1)))
                    for g in range(H):
                        last = nc.tensor.matmul(PS[0:NL, 6 + g // 4, (g % 4) * NL:(g % 4 + 1) * NL], AT[:, g, :],
                                                AT[:, g, :], start=True, stop=True)
                    last.then_inc(sem("f_aa"), 1)
                    for it in range(ITERS):
                        for q in range(2):
                            if it == 0:
                                need(pe, ("f_y0", at(i, 2, 2)), ("f_w0", at(i, 1, 1)))
                            else:
                                need(pe, ("f_st", at(i, 2 * ITERS, 2 * it - 1 + q)))
                            for g in range(4 * q, 4 * q + 4):
                                last = nc.tensor.matmul(PS[0:NL, 4 + q, (g % 4) * SW:(g % 4 + 1) * SW],
                                                        ST[:, g, 0:NL], ST[:, g, :], start=True, stop=True)
                            last.then_inc(sem("f_m1"), 1)
                        if it == 0:
                            need(pe, ("f_p1", at(i, 1, 1)))
                            for g in range(H):
                                for t in range(2):
                                    c = g % 3 * U + t * UT
                                    last = nc.tensor.transpose(PS[0:NL, g // 3, c:c + UT], P1[:, 2 * g + t, :],
                                                               ident[0:UT, 0:UT])
                            last.then_inc(sem("f_t1"), 1)
                        else:
                            taps(i, (it - 1) * 3, min(it * 3, 17))
                        for q in range(2):
                            need(pe, ("f_ta", at(i, 2 * ITERS, 2 * it + q + 1)), ("f_tx", at(i, 2 * ITERS, 2 * it + q + 1)))
                            for g in range(4 * q, 4 * q + 4):
                                c0 = 0 if it < ITERS - 1 else NL
                                last = nc.tensor.matmul(PS[0:NL, 6 + q, (g % 4) * SW + c0:(g % 4 + 1) * SW],
                                                        TA[:, g, 0:NL], TX[:, g, c0:SW], start=True, stop=True)
                            last.then_inc(sem("f_m2"), 1)
                    taps(i, 15, 17)
                    need(pe, ("f_st", at(i, 2 * ITERS, 2 * ITERS)), ("f_pt", at(i, 1, 1)))
                    for g in range(H):
                        last = nc.tensor.matmul(PS[0:NL, 0, g * DH:(g + 1) * DH], AS[:, g, :], ST[:, g, NL:SW],
                                                start=True, stop=True)
                    last.then_inc(sem("f_um"), 1)
                    need(pe, ("f_u", at(i, 1, 1)))
                    for g in range(H):
                        r, hh = g // 2, g % 2
                        last = nc.tensor.matmul(PS[32 * r:32 * r + 32, 1, hh * U:(hh + 1) * U], UU[:, g, :], PT[:, g, :],
                                                start=True, stop=True)
                    last.then_inc(sem("f_o"), 1)
                    need(pe, ("f_oo", at(i, 1, 1)))
                    for t in range(2):
                        wo = WI[:, X_WO + t * D:X_WO + (t + 1) * D]
                        nc.tensor.matmul(PS[0:D, 3, 0:COPIES * NI], wo,
                                         OO[:, t, 0:NI].unsqueeze(1).broadcast_to([128, COPIES, NI]),
                                         start=False, stop=False, skip_group_check=True)
                        last = nc.tensor.matmul(PS[0:D, 3, COPIES * NI:N], wo, OO[:, t, NI:NI + NX],
                                                start=False, stop=t == 1, skip_group_check=True)
                    last.then_inc(sem("f_out"), 1)

            @block.scalar
            def _(act):
                with act.Fori(0, B) as i:
                    need(act, ("f_qk", at(i, 1, 1)), ("f_s1", at(i, 1, 0)))
                    nc.scalar.copy(QK[:, 0, :, :], PS[:, 0, 0:2 * UL].rearrange("p (j n) -> p j n", j=2)
                                   ).then_inc(sem("f_qks"), 1)
                    need(act, ("f_sub3", at(i, 1, 1)))
                    nc.scalar.activation(E3[:, :, :], E3[:, :, :], ACT.Exp, scale=SC).then_inc(sem("f_e3"), 1)
                    need(act, ("f_t3", at(i, 1, 1)))
                    nc.scalar.copy(P3[:, :, :, :].rearrange("p (b g) t n -> p b (g t n)", b=4), PS[0:UT, 4:8, 0:4 * NL]
                                   ).then_inc(sem("f_p3"), 1)
                    need(act, ("f_t2", at(i, 1, 1)))
                    nc.scalar.copy(AT[:, :, :].rearrange("p (b g) n -> p b (g n)", b=2), PS[0:NL, 4:6, 0:4 * NL]
                                   ).then_inc(sem("f_at"), 1)
                    need(act, ("f_d1", at(i, 1, 1)))
                    nc.scalar.activation(E1_[:, :, :], E1_[:, :, :], ACT.Exp, scale=SC).then_inc(sem("f_e1"), 1)
                    need(act, ("f_aa", at(i, 1, 1)))
                    for q in range(2):
                        nc.scalar.mul(ST[:, 4 * q:4 * q + 4, 0:NL],
                                      PS[0:NL, 6 + q, 0:4 * NL].rearrange("p (g n) -> p g n", g=4),
                                      RC[:, 0:1]).then_inc(sem("f_y0"), 1)
                    kappa = 1.0
                    for it in range(ITERS):
                        for q in range(2):
                            need(act, ("f_m1", at(i, 2 * ITERS, 2 * it + q + 1)))
                            nc.scalar.mul(TA[:, 4 * q:4 * q + 4, :],
                                          PS[0:NL, 4 + q, 0:4 * SW].rearrange("p (g n) -> p g n", g=4),
                                          15.0 / 13.0 * kappa).then_inc(sem("f_ta"), 1)
                        if it == 0:
                            need(act, ("f_t1", at(i, 1, 1)))
                            nc.scalar.copy(PT[:, 0:6, :].rearrange("p (b g) n -> p b (g n)", b=2),
                                           PS[0:NL, 0:2, 0:3 * U])
                            nc.scalar.copy(PT[:, 6:8, :].rearrange("p g n -> p (g n)"),
                                           PS[0:NL, 2, 0:2 * U]).then_inc(sem("f_pt"), 1)
                        kappa *= 13.0 / 4.0
                    need(act, ("f_um", at(i, 1, 1)))
                    nc.scalar.mul(UU[:, :, :], PS[0:NL, 0, 0:H * DH].rearrange("p (g n) -> p g n", g=H), RCK[:, 0:1]
                                  ).then_inc(sem("f_u"), 1)
                    need(act, ("f_o", at(i, 1, 1)))
                    nc.scalar.copy(OO[:, :, :], PS[:, 1, 0:2 * U].rearrange("p (t n) -> p t n", t=2)).then_inc(sem("f_oo"), 1)

            @block.gpsimd
            def _(pool):
                with pool.Fori(0, B) as i:
                    need(pool, ("f_v", at(i, 1, 0)))
                    nc.gpsimd.tensor_copy(XS[:, :], XAP[:, i, :]).then_inc(sem("f_x"), 1)
                    need(pool, ("f_um", at(i, 1, 0)))
                    nc.gpsimd.tensor_copy(AS[:, :, :], AA[:, i, :, :]).then_inc(sem("f_as"), 1)
                    need(pool, ("f_z1", at(i, 3, 3)), ("f_e10", at(i, 1, 1)), ("f_t1", at(i, 1, 0)))
                    nc.gpsimd.tensor_tensor(P1[:, :, :], E1_[:, :, :],
                                            Z1[:, 2, :].unsqueeze(2).broadcast_to([UT, 2 * H, NL]),
                                            ALU.mult).then_inc(sem("f_p1"), 1)
                    for it in range(ITERS):
                        for q in range(2):
                            need(pool, ("f_ta", at(i, 2 * ITERS, 2 * it + q + 1)))
                            nc.gpsimd.tensor_tensor(TD[:, 4 * q:4 * q + 4, :], ST[:, 4 * q:4 * q + 4, :],
                                                    TA[:, 4 * q:4 * q + 4, :], ALU.subtract).then_inc(sem("f_td"), 1)

            @block.vector
            def _(dve):
                v = nc.vector
                s3 = PS[0:NL, 4:8, 0:2 * U].rearrange("p r (k n) -> p r k n", k=2)
                s1 = PS[0:UT, 0:4, 0:4 * NL].rearrange("p r (k n) -> p r k n", k=4)
                with dve.Fori(0, B) as i:
                    need(dve, ("f_qk", at(i, 1, 1)), ("f_s1", at(i, 1, 0)))
                    v.tensor_copy(QK[:, 1, :, :], PS[:, 1, 0:2 * UL].rearrange("p (j n) -> p j n", j=2)
                                  ).then_inc(sem("f_qks"), 1)
                    need(dve, ("f_v", at(i, 1, 1)), ("f_w", at(i, 1, 0)))
                    v.tensor_tensor(VU[:, :, :], PS[0:UT, 2, :].rearrange("p (t n) -> p t n", t=2),
                                    CO[0:UT, C_KW:C_KW + 2].unsqueeze(2).broadcast_to([UT, 2, H * DH]),
                                    ALU.mult).then_inc(sem("f_vu"), 1)
                    need(dve, ("f_s3", at(i, 1, 1)))
                    v.tensor_reduce(M3[:, :].rearrange("p (r k) -> p r k", k=2), s3, AX.X, ALU.max).then_inc(sem("f_m3"), 1)
                    need(dve, ("f_m3", at(i, 1, 1)), ("f_t3", at(i, 1, 0)))
                    v.tensor_tensor(E3[:, :, :].rearrange("p (r k) n -> p r k n", k=2), s3,
                                    M3[:, :].rearrange("p (r k) -> p r k", k=2).unsqueeze(3).broadcast_to([NL, 4, 2, U]),
                                    ALU.subtract).then_inc(sem("f_sub3"), 1)
                    need(dve, ("f_s1", at(i, 1, 1)))
                    v.tensor_reduce(M1[:, :].rearrange("p (r k) -> p r k", k=4), s1, AX.X, ALU.max).then_inc(sem("f_mm1"), 1)
                    need(dve, ("f_mm1", at(i, 1, 1)), ("f_p1", at(i, 1, 0)))
                    v.tensor_tensor(E1_[:, :, :].rearrange("p (r k) n -> p r k n", k=4), s1,
                                    M1[:, :].rearrange("p (r k) -> p r k", k=4).unsqueeze(3).broadcast_to([UT, 4, 4, NL]),
                                    ALU.subtract).then_inc(sem("f_d1"), 1)
                    need(dve, ("f_e3", at(i, 1, 1)))
                    v.tensor_reduce(Z3[:, 0, :], E3[:, :, 0:NI], AX.X, ALU.add).then_inc(sem("f_z3"), 1)
                    v.tensor_reduce(Z3[:, 1, :], E3[:, :, :], AX.X, ALU.add).then_inc(sem("f_z3"), 1)
                    need(dve, ("f_z3", at(i, 5, 2)))
                    v.scalar_tensor_tensor(out=Z3[:, 2, :], in0=Z3[:, 0, :], scalar=float(COPIES - 1), in1=Z3[:, 1, :],
                                           op0=ALU.mult, op1=ALU.add).then_inc(sem("f_z3"), 1)
                    need(dve, ("f_z3", at(i, 5, 3)))
                    v.scalar_tensor_tensor(out=Z3[:, 3, :], in0=E3[:, :, U - 1], scalar=float(PAD - 1), in1=Z3[:, 2, :],
                                           op0=ALU.mult, op1=ALU.add).then_inc(sem("f_z3"), 1)
                    need(dve, ("f_z3", at(i, 5, 4)))
                    v.reciprocal(Z3[:, 0, :], Z3[:, 3, :]).then_inc(sem("f_z3"), 1)
                    need(dve, ("f_z3", at(i, 5, 5)))
                    v.tensor_scalar(Z3[:, 1, :], Z3[:, 0, :], CO[0:NL, C_DV:C_DV + 1], None, ALU.mult).then_inc(sem("f_r3"), 1)
                    need(dve, ("f_w", at(i, 1, 1)), ("f_r3", at(i, 1, 1)), ("f_um", at(i, 1, 0)))
                    v.tensor_tensor(ST[:, :, NL:SW], PS[0:NL, 3, 0:H * DH].rearrange("p (g n) -> p g n", g=H),
                                    Z3[:, 1, :].unsqueeze(2).broadcast_to([NL, H, DH]), ALU.mult).then_inc(sem("f_w0"), 1)
                    need(dve, ("f_e1", at(i, 1, 1)), ("f_p1", at(i, 1, 0)))
                    v.tensor_reduce(Z1[:, 0, :], E1_[:, :, :], AX.X, ALU.add).then_inc(sem("f_z1"), 1)
                    need(dve, ("f_z1", at(i, 3, 1)))
                    v.scalar_tensor_tensor(out=Z1[:, 1, :], in0=E1_[:, :, 0], scalar=float(ZL - 1), in1=Z1[:, 0, :],
                                           op0=ALU.mult, op1=ALU.add).then_inc(sem("f_z1"), 1)
                    need(dve, ("f_z1", at(i, 3, 2)))
                    v.reciprocal(Z1[:, 2, :], Z1[:, 1, :]).then_inc(sem("f_z1"), 1)
                    v.tensor_scalar(E1_[:, :, 0], E1_[:, :, 0], ROOT, None, ALU.mult).then_inc(sem("f_e10"), 1)
                    kappa = 1.0
                    for it in range(ITERS):
                        for q in range(2):
                            need(dve, ("f_ta", at(i, 2 * ITERS, 2 * it + q + 1)))
                            v.scalar_tensor_tensor(out=TX[:, 4 * q:4 * q + 4, :], in0=ST[:, 4 * q:4 * q + 4, :],
                                                   scalar=7.0 * 15.0 / 13.0, in1=TA[:, 4 * q:4 * q + 4, :],
                                                   op0=ALU.mult, op1=ALU.subtract).then_inc(sem("f_tx"), 1)
                        for q in range(2):
                            c0 = 0 if it < ITERS - 1 else NL
                            need(dve, ("f_m2", at(i, 2 * ITERS, 2 * it + q + 1)), ("f_td", at(i, 2 * ITERS, 2 * it + q + 1)))
                            v.scalar_tensor_tensor(
                                out=ST[:, 4 * q:4 * q + 4, c0:SW],
                                in0=PS[0:NL, 6 + q, 0:4 * SW].rearrange("p (g n) -> p g n", g=4)[:, :, c0:SW],
                                scalar=kappa * 13.0 / 225.0, in1=TD[:, 4 * q:4 * q + 4, c0:SW],
                                op0=ALU.mult, op1=ALU.add).then_inc(sem("f_st"), 1)
                        kappa *= 13.0 / 4.0
                    need(dve, ("f_out", at(i, 1, 1)))
                    v.tensor_tensor(HT[:, i, 0:COPIES * NI].rearrange("p (r n) -> p r n", r=COPIES),
                                    PS[0:D, 3, 0:COPIES * NI].rearrange("p (r n) -> p r n", r=COPIES),
                                    HX[:, i, 0:NI].unsqueeze(1).broadcast_to([D, COPIES, NI]), ALU.add
                                    ).then_inc(sem("f_res"), 1)
                    v.tensor_tensor(HT[:, i, COPIES * NI:N], PS[0:D, 3, COPIES * NI:N], HX[:, i, NI:NI + NX], ALU.add
                                    ).then_inc(sem("f_res"), 1)
        phase_over()
        S.close()

        XR = sb("XR", [D, B, NP])
        XN = sb("XN", [D, B, NP])
        WR = sb("WR", [TT, B * NT, E0])
        WT = sb("WT", [E0, B, NP])

        def chunk(t, c):
            return t[:, :, :].rearrange("p b n -> p (b n)")[:, CH * c:CH * (c + 1)]

        def router_pe(pe, tag, weights, n, ready):
            pe.wait_ge(*ready)
            for k in range(B * NT):
                last = nc.tensor.matmul(PS[0:TT, 0, k * n:(k + 1) * n], XR[:, k // NT, k % NT * TT:(k % NT + 1) * TT],
                                        weights, start=True, stop=True)
            last.then_inc(sem(tag + "_logit"), 1)

        def router_turn(pe, tag, m):
            pe.wait_ge(sem(tag + "_w"), 1)
            for k in range(B * NT):
                last = nc.tensor.transpose(PS[0:m, 1 + k // 5, k % 5 * TT:(k % 5 + 1) * TT], WR[:, k, 0:m],
                                           ident[0:TT, 0:TT])
            last.then_inc(sem(tag + "_turned"), 1)

        def router_act(act, tag, n, m, gates):
            act.wait_ge(sem(tag + "_sub"), 1)
            nc.scalar.activation(RE[:, :, 0:n], RD[:, :, 0:n], ACT.Exp).then_inc(sem(tag + "_exp"), 1)
            if gates:
                act.wait_ge(sem(tag + "_gsub"), 1)
                nc.scalar.activation(RE[:, :, 0:n], RD[:, :, 0:n], ACT.Exp).then_inc(sem(tag + "_gexp"), 1)
            act.wait_ge(sem(tag + "_turned"), 1)
            for q in range(5):
                w = min(5, B * NT - 5 * q) * TT
                last = nc.scalar.copy(WT[0:m, :, :].rearrange("p b n -> p (b n)")[:, 5 * TT * q:5 * TT * q + w],
                                      PS[0:m, 1 + q, 0:w])
            last.then_inc(sem(tag + "_wt"), 1)

        def router_dve(dve, tag, bias, n, gates):
            v = nc.vector
            K = B * NT
            steps = [0]

            def step(ins):
                ins.then_inc(sem(tag + "_step"), 1)
                steps[0] += 1
                dve.wait_ge(sem(tag + "_step"), steps[0])

            wide = lambda x: x.unsqueeze(2).broadcast_to([TT, K, n])
            iota = CO[0:TT, C_IOTA:C_IOTA + n].unsqueeze(1).broadcast_to([TT, K, n])
            L, D_, T, O1, O2 = (x[:, :, 0:n] for x in (RL, RD, RT, R1, R2))
            dve.wait_ge(sem(tag + "_logit"), 1)
            step(v.tensor_tensor(L, PS[0:TT, 0, 0:K * n].rearrange("p (k n) -> p k n", n=n),
                                 bias.unsqueeze(1).broadcast_to([TT, K, n]), ALU.add))
            step(v.tensor_reduce(RM[:, 0, :], L, AX.X, ALU.max))
            v.tensor_tensor(D_, L, wide(RM[:, 0, :]), ALU.subtract).then_inc(sem(tag + "_sub"), 1)
            top = RM[:, 0, :]
            for k, hot in enumerate((O1, O2)):
                step(v.tensor_tensor(T, L, wide(top), ALU.is_lt))
                step(v.scalar_tensor_tensor(out=T, in0=T, scalar=100.0, in1=iota, op0=ALU.mult, op1=ALU.add))
                step(v.tensor_reduce(RM[:, 1, :], T, AX.X, ALU.min))
                step(v.tensor_tensor(hot, iota, wide(RM[:, 1, :]), ALU.is_equal))
                if k == 0:
                    step(v.scalar_tensor_tensor(out=L, in0=hot, scalar=-1e30, in1=L, op0=ALU.mult, op1=ALU.add))
                    step(v.tensor_reduce(RM[:, 2, :], L, AX.X, ALU.max))
                    top = RM[:, 2, :]
            step(v.tensor_tensor(O1, O1, O2, ALU.add))
            dve.wait_ge(sem(tag + "_exp"), 1)
            if gates:
                step(v.tensor_reduce(RM[:, 1, :], RE[:, :, 0:n], AX.X, ALU.add))
                step(v.reciprocal(RM[:, 2, :], RM[:, 1, :]))
                step(v.tensor_tensor(T, RE[:, :, 0:n], wide(RM[:, 2, :]), ALU.mult))
                v.tensor_tensor(D_, T, wide(RM[:, 2, :]), ALU.subtract).then_inc(sem(tag + "_gsub"), 1)
                dve.wait_ge(sem(tag + "_gexp"), 1)
            step(v.tensor_tensor(T, RE[:, :, 0:n], O1, ALU.mult))
            step(v.tensor_reduce(RM[:, 1, :], T, AX.X, ALU.add))
            step(v.reciprocal(RM[:, 2, :], RM[:, 1, :]))
            v.tensor_tensor(WR[:, :, 0:n], T, wide(RM[:, 2, :]), ALU.mult).then_inc(sem(tag + "_w"), 1)

        RL, RD, RT, R1, R2, RE = (sb(n, [TT, B * NT, E0]) for n in ("RL", "RD", "RT", "R1", "R2", "RE"))
        RM = sb("RM", [TT, 3, B * NT])
        CH = 432
        NCH = B * NP // CH

        with nc.Block() as block:
            @block.tensor
            def _(pe):
                ln_pe(pe, "b", lambda c: chunk(HT, c), (s_load, 16), NCH, CH)
                router_pe(pe, "r", MA[:, W_R:W_R + E0], E0, (sem("b_done"), 2 * NCH))
                router_turn(pe, "r", E0)

            @block.scalar
            def _(act):
                ln_act(act, "b", NCH, CH, [False, True])
                router_act(act, "r", E0, E0, False)

            @block.vector
            def _(dve):
                ln_dve(dve, "b", NCH, CH, [lambda c: chunk(XR, c), lambda c: chunk(XN, c)])
                router_dve(dve, "r", WI[0:TT, X_BR:X_BR + E0], E0, False)
        phase_over()

        S = ExitStack()
        GE = ts("GE", [128, 2 * E0, NP])
        XM = ts("XM", [D, NP])
        WS = ts("WS", [E0, NP])
        YW = ts("YW", [TT, E0, D])
        AC = ts("AC", [TT, NT, D])
        with nc.Block() as block:
            @block.sync
            def _(sp):
                started(sp, LOOP3)

            AHEAD = 4

            @block.gpsimd
            def _(pool):
                with pool.Fori(0, B) as i:
                    need(pool, ("m_h", at(i, 2 * E0, 0)))
                    nc.gpsimd.tensor_copy(XM[:, :], XN[:, i, :]).then_inc(sem("m_x"), 1)
                    need(pool, ("m_o", at(i, 1, 0)))
                    nc.gpsimd.tensor_copy(WS[:, :], WT[:, i, :]).then_inc(sem("m_ws"), 1)

            @block.tensor
            def _(pe):
                with pe.Fori(0, B) as i:
                    def hidden(j):
                        need(pe, ("m_g", at(i, 2 * E0, j - 3)) if j >= 4 else ("m_g", at(i, 2 * E0, 0)))
                        nc.tensor.matmul(PS[:, j % 4, 0:NP], FW1[:, j // 2, (j % 2) * 128:(j % 2 + 1) * 128],
                                         XM[:, :], start=True, stop=True).then_inc(sem("m_h"), 1)

                    need(pe, ("m_x", at(i, 1, 1)))
                    for j in range(AHEAD):
                        hidden(j)
                    for e in range(E0):
                        need(pe, ("m_g", at(i, 2 * E0, 2 * e + 2)), ("m_yw", at(i, NT, 0)))
                        for t in range(NT):
                            for k in range(2):
                                last = nc.tensor.matmul(PS[0:TT, 4 + t, e * D:(e + 1) * D],
                                                        GE[:, 2 * e + k, t * TT:(t + 1) * TT],
                                                        WI[:, X_F2 + (2 * e + k) * D:X_F2 + (2 * e + k + 1) * D],
                                                        start=k == 0, stop=k == 1)
                        last.then_inc(sem("m_y"), 1)
                        for j in range(2 * e + AHEAD, min(2 * e + AHEAD + 2, 2 * E0)):
                            hidden(j)
                    need(pe, ("m_ws", at(i, 1, 1)), ("m_ac", at(i, NT, NT)), ("m_res", at(i, 1, 0)))
                    nc.tensor.matmul(PS[0:D, 7, 0:NP], B2[:, :], WS[:, :], start=True, stop=False)
                    for t in range(NT):
                        last = nc.tensor.matmul(PS[0:D, 7, t * TT:(t + 1) * TT], AC[:, t, :], ident[0:TT, 0:TT],
                                                start=False, stop=t == NT - 1)
                    last.then_inc(sem("m_o"), 1)

            @block.scalar
            def _(act):
                with act.Fori(0, B) as i:
                    for j in range(2 * E0):
                        need(act, ("m_h", at(i, 2 * E0, j + 1)), ("m_y", at(i, E0, 0)))
                        nc.scalar.activation(GE[:, j, :], PS[:, j % 4, 0:NP], ACT.Gelu, bias=FB1[:, j:j + 1]
                                             ).then_inc(sem("m_g"), 1)

            @block.vector
            def _(dve):
                v = nc.vector
                with dve.Fori(0, B) as i:
                    need(dve, ("m_y", at(i, E0, E0)), ("m_o", at(i, 1, 0)))
                    for t in range(NT):
                        if t:
                            need(dve, ("m_ac", at(i, NT, t)))
                        v.tensor_tensor(YW[:, :, :], PS[0:TT, 4 + t, :].rearrange("p (e d) -> p e d", e=E0),
                                        WR[:, bass.ds(i * NT + t, 1), :].rearrange("p a e -> p (a e)").unsqueeze(2).broadcast_to([TT, E0, D]),
                                        ALU.mult).then_inc(sem("m_yw"), 1)
                        need(dve, ("m_yw", at(i, NT, t + 1)))
                        v.tensor_reduce(AC[:, t, :], YW[:, :, :].rearrange("p e d -> p d e"), AX.X, ALU.add
                                        ).then_inc(sem("m_ac"), 1)
                    need(dve, ("m_o", at(i, 1, 1)))
                    v.tensor_tensor(HT[:, i, 0:N], PS[0:D, 7, 0:N], HT[:, i, 0:N], ALU.add).then_inc(sem("m_res"), 1)
        phase_over()
        S.close()

        with nc.Block() as block:
            @block.tensor
            def _(pe):
                ln_pe(pe, "c", lambda c: chunk(HT, c), (s_load, 16), NCH, CH)

            @block.scalar
            def _(act):
                ln_act(act, "c", NCH, CH, [True])

            @block.vector
            def _(dve):
                ln_dve(dve, "c", NCH, CH, [lambda c: chunk(XN, c)])
        phase_over()

        S = ExitStack()
        NK = 288
        XK = ts("XK", [D, NK])
        QA = ts("QA", [66, H, NP])
        KA = ts("KA", [66, H, NK])
        SQ = ts("SQ", [128, 4, NK])
        NQ = ts("NQ", [H, NP])
        NKY = ts("NKY", [H, NK])
        VM = ts("VM", [128, 2, H, D])
        VR = ts("VR", [128, 2, D])
        CL = ts("CL", [128, 3, 2, NP])
        EX = ts("EX", [128, 3, 2, NP])
        UN = H + 1
        with nc.Block() as block:
            @block.sync
            def _(sp):
                started(sp, LOOP4)
                sp.wait_ge(sem("d_ones"), 4)
                with sp.Fori(0, B) as i:
                    need(sp, ("d_n", at(i, 2, 2)), ("d_s", at(i, UN, 0)))
                    for h in range(H):
                        sp.dma_start(QA[64:65, h, :], NQ[h:h + 1, :]).then_inc(sem("d_row"), 16)
                        sp.dma_start(KA[65:66, h, :], NKY[h:h + 1, :]).then_inc(sem("d_row"), 16)

            @block.gpsimd
            def _(pool):
                for k, (rows, value) in enumerate(((XK[:, :], 0.0), (QA[64:66, :, :], 1.0), (KA[64:66, :, :], 1.0),
                                                   (SQ[:, :, :], 0.0))):
                    nc.gpsimd.memset(rows, value).then_inc(sem("d_ones"), 1)
                    pool.wait_ge(sem("d_ones"), k + 1)
                with pool.Fori(0, B) as i:
                    need(pool, ("d_v", at(i, 1, 0)))
                    nc.gpsimd.tensor_copy(XK[:, 0:NP], XN[:, i, :]).then_inc(sem("d_x"), 1)

            @block.tensor
            def _(pe):
                with pe.Fori(0, B) as i:
                    need(pe, ("d_x", at(i, 1, 1)), ("d_res", at(i, 1, 0)), ("d_cl", at(i, UN, 0)))
                    for p in range(4):
                        last = nc.tensor.matmul(PS[:, p, 0:NP], MA[:, W_Q + p * 128:W_Q + (p + 1) * 128], XK[:, 0:NP],
                                                start=True, stop=True)
                    last.then_inc(sem("d_q"), 1)
                    for p in range(4):
                        last = nc.tensor.matmul(PS[:, 4 + p, 0:NK], MA[:, W_K + p * 128:W_K + (p + 1) * 128], XK[:, :],
                                                start=True, stop=True)
                    last.then_inc(sem("d_k"), 1)
                    need(pe, ("d_qa", at(i, 2, 2)), ("d_sq", at(i, 2, 1)))
                    for p in range(4):
                        last = nc.tensor.matmul(PS[0:H, 0, 0:NP], CO[:, C_BS + 8 * p:C_BS + 8 * p + 8], SQ[:, p, 0:NP],
                                                start=p == 0, stop=p == 3)
                    last.then_inc(sem("d_nq"), 1)
                    for t in range(2):
                        nc.tensor.matmul(PS[:, 2 + t, :], XK[:, t * 128:(t + 1) * 128],
                                         WVO[:, :, :].rearrange("p h o -> p (h o)"), start=True, stop=True)
                    for h in range(H):
                        r = h % 4
                        last = nc.tensor.matmul(PS[32 * r:32 * r + 32, 1, (h // 4) * D:(h // 4 + 1) * D], XK[:, 256:288],
                                                WVO[:, h, :], start=True, stop=True)
                    last.then_inc(sem("d_v"), 1)
                    need(pe, ("d_sq", at(i, 2, 2)), ("d_ka", at(i, 2, 2)))
                    for p in range(4):
                        last = nc.tensor.matmul(PS[0:H, 4, 0:NK], CO[:, C_BS + 8 * p:C_BS + 8 * p + 8], SQ[:, p, :],
                                                start=p == 0, stop=p == 3)
                    last.then_inc(sem("d_nk"), 1)

                    def scores(u):
                        if u < H:
                            for t in range(2):
                                last = nc.tensor.matmul(PS[:, 2 + 2 * (u % 3) + t, 0:NP], KA[:, u, t * 128:(t + 1) * 128],
                                                        QA[:, u, :], start=True, stop=True)
                        else:
                            for h in range(H):
                                r = h % 4
                                last = nc.tensor.matmul(PS[32 * r:32 * r + 32, 2 + 2 * (u % 3) + h // 4, 0:NP],
                                                        KA[:, h, 256:288], QA[:, h, :], start=True, stop=True)
                        last.then_inc(sem("d_s"), 1)

                    need(pe, ("d_row", at(i, 32 * H, 32 * H)), ("d_n", at(i, 2, 2)), ("d_vm", at(i, 2, 2)))
                    for u in range(3):
                        scores(u)
                    for u in range(UN):
                        need(pe, ("d_e", at(i, UN, u + 1)))
                        for t in range(2):
                            last = nc.tensor.matmul(PS[0:D, 1, 0:NP], VM[:, t, u, :] if u < H else VR[:, t, :],
                                                    EX[:, u % 3, t, :], start=u == 0 and t == 0,
                                                    stop=u == UN - 1 and t == 1)
                        last.then_inc(sem("d_pv"), 1)
                        if u + 3 < UN:
                            need(pe, ("d_cl", at(i, UN, u + 1)))
                            scores(u + 3)

            @block.scalar
            def _(act):
                act.wait_ge(sem("d_ones"), 4)
                with act.Fori(0, B) as i:
                    need(act, ("d_q", at(i, 1, 1)), ("d_nk", at(i, 1, 0)), ("d_s", at(i, UN, 0)))
                    nc.scalar.activation(SQ[:, :, 0:NP], PS[:, 0:4, 0:NP], ACT.Square).then_inc(sem("d_sq"), 1)
                    for o in range(2):
                        nc.scalar.mul(QA[0:D, o::2, :], PS[o * D:(o + 1) * D, 0:4, 0:NP], -2.0).then_inc(sem("d_qa"), 1)
                    need(act, ("d_ka", at(i, 2, 2)), ("d_nq", at(i, 1, 1)))
                    nc.scalar.activation(SQ[:, :, :], PS[:, 4:8, 0:NK], ACT.Square).then_inc(sem("d_sq"), 1)
                    nc.scalar.copy(NQ[:, :], PS[0:H, 0, 0:NP]).then_inc(sem("d_n"), 1)
                    need(act, ("d_v", at(i, 1, 1)))
                    nc.scalar.copy(VR[:, :, :], PS[:, 1, 0:2 * D].rearrange("p (q d) -> p q d", q=2)
                                   ).then_inc(sem("d_vm"), 1)
                    need(act, ("d_nk", at(i, 1, 1)))
                    nc.scalar.copy(NKY[:, :], PS[0:H, 4, 0:NK]).then_inc(sem("d_n"), 1)
                    for u in range(UN):
                        need(act, ("d_cl", at(i, UN, u + 1)), ("d_pv", at(i, UN, max(u - 2, 0))))
                        if u < H:
                            nc.scalar.activation(EX[:, u % 3, :, :], CL[:, u % 3, :, :], ACT.Exp,
                                                 scale=NG[:, u:u + 1]).then_inc(sem("d_e"), 1)
                        else:
                            nc.scalar.activation(EX[:, u % 3, 0, :], CL[:, u % 3, 0, :], ACT.Exp, scale=NG[:, H:H + 1])
                            nc.scalar.activation(EX[:, u % 3, 1, :], CL[:, u % 3, 1, :], ACT.Exp,
                                                 scale=NG[:, H + 1:H + 2]).then_inc(sem("d_e"), 1)

            @block.vector
            def _(dve):
                v = nc.vector
                with dve.Fori(0, B) as i:
                    need(dve, ("d_k", at(i, 1, 1)), ("d_s", at(i, UN, 0)))
                    for o in range(2):
                        v.tensor_copy(KA[0:D, o::2, :], PS[o * D:(o + 1) * D, 4:8, 0:NK]).then_inc(sem("d_ka"), 1)
                    need(dve, ("d_v", at(i, 1, 1)))
                    v.tensor_copy(VM[:, :, :, :].rearrange("p t h d -> p t (h d)"), PS[:, 2:4, :]).then_inc(sem("d_vm"), 1)
                    for u in range(UN):
                        need(dve, ("d_s", at(i, UN, u + 1)), ("d_e", at(i, UN, max(u - 2, 0))))
                        s = 2 + 2 * (u % 3)
                        v.tensor_scalar(CL[:, u % 3, :, :], PS[:, s:s + 2, 0:NP], 0.0, None, ALU.max
                                        ).then_inc(sem("d_cl"), 1)
                    need(dve, ("d_pv", at(i, UN, UN)))
                    v.tensor_tensor(HT[:, i, 0:N], PS[0:D, 1, 0:N], HT[:, i, 0:N], ALU.add).then_inc(sem("d_res"), 1)
        phase_over()
        S.close()

        with nc.Block() as block:
            @block.gpsimd
            def _(pool):
                nc.gpsimd.memset(WR[:, :, E1:E1 + 1], 1.0).then_inc(sem("one_col"), 1)

            @block.tensor
            def _(pe):
                ln_pe(pe, "d", lambda c: chunk(HT, c), (s_load, 16), NCH, CH)
                router_pe(pe, "g", MA[:, W_G:W_G + E1], E1, (sem("d_done"), NCH))
                pe.wait_ge(sem("one_col"), 1)
                router_turn(pe, "g", E1 + 1)

            @block.scalar
            def _(act):
                ln_act(act, "d", NCH, CH, [False])
                router_act(act, "g", E1, E1 + 1, True)

            @block.vector
            def _(dve):
                ln_dve(dve, "d", NCH, CH, [lambda c: chunk(XR, c)])
                router_dve(dve, "g", WI[0:TT, X_GB:X_GB + E1], E1, True)
        phase_over()

        S = ExitStack()
        XF = ts("XF", [D, NP])
        HF = ts("HF", [D, NP])
        WF = ts("WF", [E1 + 1, NP])
        H1 = ts("H1", [128, E1, NP])
        S1 = ts("S1", [D, NP])
        H2 = ts("H2", [128, 2, NP])
        S2 = ts("S2", [128, NP])
        GW = ts("GW", [TT, NT, E1, D])
        GS = ts("GS", [TT, NT, D])
        OS = ts("OS", [TT, NT, D])
        with nc.Block() as block:
            @block.sync
            def _(sp):
                started(sp, LOOP5)
                with sp.Fori(0, B) as i:
                    need(sp, ("g_fin", at(i, 1, 1)))
                    sp.dma_start(out[bass.ds(i, 1), 0:2 * TT, :].rearrange("b (t p) d -> p (b t) d", p=TT),
                                 OS[:, 0:2, :]).then_inc(sem("g_put"), 16)
                    sp.dma_start(out[bass.ds(i, 1), 2 * TT:N, :].rearrange("b p d -> p (b d)"), OS[0:N - 2 * TT, 2, :]
                                 ).then_inc(sem("g_put"), 16)
                sp.wait_ge(sem("g_put"), 32 * B + 1)

            @block.gpsimd
            def _(pool):
                with pool.Fori(0, B) as i:
                    need(pool, ("g_l3", at(i, NT, 0)))
                    nc.gpsimd.tensor_copy(XF[:, :], XR[:, i, :]).then_inc(sem("g_x"), 1)
                    nc.gpsimd.tensor_copy(HF[:, :], HT[:, i, :]).then_inc(sem("g_x"), 1)
                    nc.gpsimd.tensor_copy(WF[:, :], WT[0:E1 + 1, i, :]).then_inc(sem("g_x"), 1)

            @block.tensor
            def _(pe):
                with pe.Fori(0, B) as i:
                    need(pe, ("g_x", at(i, 3, 1)), ("g_h1", at(i, 4, 0)), ("g_s1", at(i, 1, 0)), ("g_gw", at(i, NT, 0)), ("g_fin", at(i, 1, 0)))
                    for e in range(E1):
                        nc.tensor.matmul(PS[:, e, 0:NP], MA[:, W_E1 + e * 128:W_E1 + (e + 1) * 128], XF[:, :],
                                         start=True, stop=True).then_inc(sem("g_l1"), 1)
                        if e == 0:
                            nc.tensor.matmul(PS[0:D, 4, 0:NP], MA[:, W_S1:W_S1 + D], XF[:, :], start=True, stop=True
                                             ).then_inc(sem("g_l1"), 1)
                    need(pe, ("g_s1", at(i, 1, 1)), ("g_h2", at(i, 3, 0)))
                    nc.tensor.matmul(PS[:, 7, 0:NP], MA[:, W_S2:W_S2 + 128], S1[:, :], start=True, stop=True
                                     ).then_inc(sem("g_l2"), 1)
                    need(pe, ("g_h1", at(i, 4, 4)))
                    for e in range(E1):
                        last = nc.tensor.matmul(PS[e % 2 * D:(e % 2 + 1) * D, 5 + e // 2, 0:NP],
                                                WI[:, X_E2 + e * D:X_E2 + (e + 1) * D], H1[:, e, :],
                                                start=True, stop=True)
                        if e % 2:
                            last.then_inc(sem("g_l2"), 1)
                    need(pe, ("g_h2", at(i, 3, 3)), ("g_x", at(i, 3, 3)))
                    for t in range(NT):
                        tok = slice(t * TT, (t + 1) * TT)
                        for e in (0, 2, 1, 3):
                            o = e % 2 * D
                            nc.tensor.matmul(PS[0:TT, t + 3 * (e % 2), e // 2 * D:(e // 2 + 1) * D],
                                             H2[o:o + D, e // 2, tok],
                                             WI[o:o + D, X_E3 + e // 2 * D:X_E3 + (e // 2 + 1) * D], start=True, stop=True)
                        fin = PS[0:TT, t, 2 * D:3 * D]
                        nc.tensor.matmul(fin, HF[:, tok], ident[0:D, 0:D], start=True, stop=False)
                        nc.tensor.matmul(fin, S2[:, tok], WI[:, X_S3:X_S3 + D], start=False, stop=False)
                        nc.tensor.matmul(fin, WF[:, tok], B3[:, :], start=False, stop=True).then_inc(sem("g_l3"), 1)

            @block.scalar
            def _(act):
                with act.Fori(0, B) as i:
                    need(act, ("g_l1", at(i, 5, 2)), ("g_l2", at(i, 3, 0)))
                    nc.scalar.activation(S1[:, :], PS[0:D, 4, 0:NP], ACT.Relu, bias=VE[:, V_SB1:V_SB1 + 1]
                                         ).then_inc(sem("g_s1"), 1)
                    for e in range(2):
                        need(act, ("g_l1", at(i, 5, 2 + e)))
                        nc.scalar.activation(H1[:, e, :], PS[:, e, 0:NP], ACT.Relu, bias=WI[:, X_EB1 + e:X_EB1 + e + 1]
                                             ).then_inc(sem("g_h1"), 1)
                    need(act, ("g_l2", at(i, 3, 1)), ("g_l3", at(i, NT, 0)))
                    nc.scalar.activation(S2[:, :], PS[:, 7, 0:NP], ACT.Relu, bias=WI[:, X_SB2:X_SB2 + 1]
                                         ).then_inc(sem("g_h2"), 1)
                    need(act, ("g_l2", at(i, 3, 2)))
                    nc.scalar.activation(H2[:, 0, :], PS[:, 5, 0:NP], ACT.Relu, bias=WI[:, X_EB2:X_EB2 + 1]
                                         ).then_inc(sem("g_h2"), 1)

            @block.vector
            def _(dve):
                v = nc.vector
                with dve.Fori(0, B) as i:
                    for e in range(2, 4):
                        need(dve, ("g_l1", at(i, 5, 2 + e)), ("g_l2", at(i, 3, 0)))
                        v.tensor_scalar(H1[:, e, :], PS[:, e, 0:NP], WI[:, X_EB1 + e:X_EB1 + e + 1], 0.0, ALU.add, ALU.max
                                        ).then_inc(sem("g_h1"), 1)
                    need(dve, ("g_l2", at(i, 3, 3)), ("g_l3", at(i, NT, 0)))
                    v.tensor_scalar(H2[:, 1, :], PS[:, 6, 0:NP], WI[:, X_EB2 + 1:X_EB2 + 2], 0.0, ALU.add, ALU.max
                                    ).then_inc(sem("g_h2"), 1)
                    need(dve, ("g_l3", at(i, NT, NT)))
                    for t in range(NT):
                        v.tensor_tensor(GW[:, t, :, :].rearrange("p (o k) d -> p o k d", o=2),
                                        PS[0:TT, t:t + 4:3, 0:2 * D].rearrange("p o (k d) -> p o k d", k=2),
                                        WR[:, bass.ds(i * NT + t, 1), 0:E1].rearrange("p a (k o) -> p o (a k)", o=2)
                                        .unsqueeze(3).broadcast_to([TT, 2, 2, D]), ALU.mult).then_inc(sem("g_gw"), 1)
                    need(dve, ("g_gw", at(i, NT, NT)))
                    v.tensor_reduce(GS[:, :, :], GW[:, :, :, :].rearrange("p t e d -> p t d e"), AX.X, ALU.add
                                    ).then_inc(sem("g_sum"), 1)
                    need(dve, ("g_sum", at(i, 1, 1)), ("g_put", at(i, 32, 0)))
                    v.tensor_tensor(OS[:, :, :], PS[0:TT, 0:NT, 2 * D:3 * D], GS[:, :, :], ALU.add).then_inc(sem("g_fin"), 1)
        phase_over()
        S.close()

_OUT = (B, N, D)


def kernel(**inputs):
    import concourse.bacc as bacc
    from concourse.bass_utils import run_bass_kernel_spmd as run

    a = {k: np.asarray(v) for k, v in inputs.items()}
    t = lambda m: np.ascontiguousarray(m)
    x = a["x"].reshape(B, 3, 8, 8, 8, 8).transpose(3, 5, 1, 0, 2, 4).reshape(PF, B * NI)
    txt = a["txt"].transpose(2, 0, 1).reshape(D, B * NX)
    ln1 = np.stack([a["L0_tok_ln1_g"], a["L0_tok_ln1_b"]], 1)
    names = ["L0_tok_b1", "L0_tok_ln2_g", "L0_tok_ln2_b", "L0_tok_bp1", "L0_tok_lnp_g", "L0_tok_lnp_b", "L0_tok_bp2",
             "L0_attn_ln_g", "L0_attn_ln_b", "L0_attn_b_out", "L1_attn_ln_scale", "L1_ffn_sb1"]
    vec = np.concatenate([np.stack([a[n] for n in names], 1), a["L0_ffn_ln_g"].T, a["L0_ffn_ln_b"].T], 1)
    side = lambda w: w.transpose(1, 0, 2).reshape(w.shape[1], -1)
    w_qkv = a["L0_attn_w_qkv"]
    mat = np.concatenate([
        a["L0_tok_Wp1"], a["L0_tok_Wp2"], w_qkv, a["L0_ffn_Wr"], a["L1_ffn_gW"], a["L1_ffn_sW1"], a["L1_ffn_sW2"],
        side(a["L1_ffn_eW1"]), side(a["L1_attn_W_q"]), side(a["L1_attn_W_k"]),
        side(a["L1_attn_W_v"].transpose(0, 2, 1)),
        a["L1_attn_W_o"].reshape(D, H, D).transpose(2, 1, 0).reshape(D, H * D),
        side(a["L0_ffn_W1"])], 1)
    rows = lambda r: np.broadcast_to(r[None, :], (128, r.shape[0]))
    halves = lambda w: w.reshape(2, 128, -1).transpose(1, 0, 2)
    kd = halves(np.repeat(a["L0_attn_res_kernel"].reshape(H, TAPS), DH, 0)).reshape(128, -1)
    wvt = halves(w_qkv[:, 512:768].T)
    e3 = a["L1_ffn_eW3"].reshape(2, 2, D, D).transpose(1, 2, 0, 3).reshape(128, 2 * D)
    wide = np.concatenate([
        a["L0_ffn_b1"].reshape(E0 * 2, 128).T, a["L1_ffn_sb2"][:, None], a["L1_ffn_eb1"].T,
        a["L1_ffn_eb2"].reshape(2, 128).T, rows(a["L1_attn_gamma"].reshape(H)),
        np.repeat(a["L1_attn_gamma"].reshape(2, 4), 32, 1).T, rows(a["L0_ffn_br"]),
        rows(a["L1_ffn_gb"]), kd, a["L1_ffn_sW3"], side(a["L1_ffn_eW2"]), e3,
        np.concatenate([wvt, wvt], 2).reshape(128, -1), halves(a["L0_attn_w_out"]).reshape(128, -1),
        a["L0_ffn_W2"].reshape(E0 * 2, 128, D).transpose(1, 0, 2).reshape(128, -1)], 1)
    b3 = np.concatenate([a["L1_ffn_eb3"], a["L1_ffn_sb3"][None, :]], 0)
    arrays = {"xpatch": x, "txt": txt, "w1": a["L0_tok_W1"], "ln1": ln1, "vec": vec, "mat": mat, "wide": wide,
              "b2": a["L0_ffn_b2"], "b3": b3, "const": shape_constants()}
    arrays = {k: t(v) for k, v in arrays.items()}
    nc = bacc.Bacc("TRN2", target_bir_lowering=False, num_devices=1)
    args = [nc.dram_tensor(k, v.shape, F32, kind="ExternalInput").ap() for k, v in arrays.items()]
    args.append(nc.dram_tensor("out_0", _OUT, F32, kind="ExternalOutput").ap())
    program(nc, *args)
    return run(nc, [arrays], core_ids=[0]).results[0]["out_0"]
```

```python
from contextlib import ExitStack

import numpy as np

import concourse.bass as bass
from concourse import mybir

F32 = mybir.dt.float32
F32R = mybir.dt.float32r
ALU = mybir.AluOpType
ACT = mybir.ActivationFunctionType
AX = mybir.AxisListType

B = 8
D = 64
NI = 64
NX = 77
COPIES = 3
N = COPIES * NI + NX
LM = 128
PAD = -N % LM
GRP = (N + PAD) // LM
ZL = PAD // GRP
NL = LM - ZL + 1
U = NI + NX + 1
UT = U // 2
KP = 96
UL = U + KP
H = 8
DH = 32
SC = DH ** -0.5
TAPS = 33
HALO = TAPS // 2
CW = 304
NP = 270
TT = 90
NT = 3
SW = NL + DH
ITERS = 6
EPS = 1e-5
PF = 192
E0 = 8
EH = 256
E1 = 4
ROOT = float(np.sqrt(ZL))

C_ID, C_CEN, C_AVG, C_AVP, C_D, C_NS, C_IOTA, C_EPS, C_EPS2, C_DV, C_KW, C_II, C_SEL = (
    0, 128, 192, 320, 448, 539, 571, 579, 580, 581, 582, 584, 648)
C_W = 648 + E0 // 2 * 128


def shape_constants():
    c = np.zeros((128, C_W), np.float32)
    c[:, C_ID:C_ID + 128] = np.eye(128)
    c[:D, C_CEN:C_CEN + D] = np.eye(D) - 1.0 / D
    c[:D, C_AVG:C_AVG + D] = 1.0 / D
    c[D:, C_AVG + D:C_AVG + 2 * D] = 1.0 / D
    c[:, C_AVP:C_AVP + 128] = 1.0 / PF
    c[:NL, C_D:C_D + NL] = 1.0
    c[0, C_D:C_D + NL] = ROOT
    c[:D, C_NS] = 1.0
    c[D:, C_NS + 1] = 1.0
    c[:, C_IOTA:C_IOTA + 8] = np.arange(8)
    c[:, C_EPS] = EPS
    c[:, C_EPS2] = EPS * EPS
    c[:, C_DV] = 1.0
    c[0, C_DV] = ROOT
    c[:, C_KW:C_KW + 2] = 1.0
    c[:NI, C_KW] = COPIES
    c[:D, C_II:C_II + D] = np.eye(D)
    c[D:, C_II:C_II + D] = np.eye(D)
    for e in range(E0):
        for row in (e, 32 + e):
            c[row, C_SEL + e * D:C_SEL + (e + 1) * D] = 1.0
    return c


V_B1, V_G2, V_B2, V_BP1, V_GP, V_BP, V_BP2, V_GA, V_BA, V_BO, V_LS, V_SB1 = range(12)
V_FG, V_FB = 12, 20
V_W = 28
W_P1, W_P2, W_QKV, W_R, W_G, W_S1, W_S2, W_E1, W_Q, W_K, W_VT, W_OT, W_F1 = (
    0, 64, 128, 896, 904, 908, 972, 1100, 1612, 2124, 2636, 3148, 3660)
W_W = 3660 + E0 * EH
Y_S1, Y_S2, Y_E1, Y_Q, Y_K, Y_F1, Y_VO = 0, 64, 192, 704, 1216, 1728, 1728 + E0 * EH
Y_W = Y_VO + H * D
X_B1, X_SB2, X_EB1, X_EB2, X_GAM, X_GAR, X_BR, X_GB, X_KD, X_S3, X_E2, X_E3, X_WVT, X_WO, X_F2, X_B2, X_SB3, X_EB3 = (
    0, 16, 17, 21, 23, 31, 33, 41, 45, 111, 175, 431, 687, 943, 1071, 2095, 2099, 2100)
X_W = 2102


LOOP1 = ["n_proj", "n_qk", "n_score", "n_max", "n_sub", "n_exp", "n_z", "n_e0", "n_a", "n_cs", "n_c1", "n_cm"]
LOOP2 = ["f_x", "f_u", "f_res", "f_qk", "f_v", "f_qks", "f_s3", "f_s1", "f_vu", "f_e3", "f_t3", "f_p3", "f_as",
         "f_t2", "f_d1", "f_w", "f_at", "f_aa", "f_y0", "f_w0", "f_st", "f_m1", "f_m2", "f_p1", "f_t1", "f_ta",
         "f_tx", "f_td", "f_pt", "f_um", "f_o", "f_oo", "f_out", "f_sub3", "f_m3", "f_mm1", "f_e1", "f_z1",
         "f_e10", "f_z3", "f_r3", "f_hx", "f_xw"]
LOOP3 = ["m_h", "m_g", "m_w", "m_wb", "m_y", "m_yw", "m_s"]
LOOP4 = ["d_x", "d_q", "d_k", "d_qa", "d_ka", "d_sq", "d_v", "d_vm", "d_s", "d_cl", "d_e", "d_pv", "d_half", "d_res"]
LOOP5 = ["g_l1", "g_s1", "g_h1", "g_l2", "g_s2", "g_h2", "g_gate", "g_gb", "g_l3", "g_yg", "g_ga", "g_hf", "g_fin", "g_os", "g_put"]


def program(nc, xpatch, txt, w1, ln1, vec, mat, wide, const, out):
    with ExitStack() as ctx:
        def sb(name, shape, dt=F32):
            return ctx.enter_context(nc.sbuf_tensor(name, shape, dt))

        sems = {}

        def sem(name):
            if name not in sems:
                sems[name] = nc.alloc_semaphore(name=name)
            return sems[name]

        def phase_over():
            done = [sems.pop(name) for name in list(sems) if name != "loaded"]
            nc.clear_and_free_semaphores(done)
            nc.all_engine_barrier()

        PS = ctx.enter_context(nc.psum_tensor("PS", [128, 8, 512], F32))
        CO = sb("CO", [128, C_W])
        VE = sb("VE", [128, V_W])
        MA = sb("MA", [128, W_W])
        WI = sb("WI", [128, X_W])
        W1A = sb("W1A", [128, D])
        W1B = sb("W1B", [D, D])
        G1A = sb("G1A", [128, 2])
        G1B = sb("G1B", [D, 2])
        ident = CO[:, C_ID:C_ID + 128]
        NG = sb("NG", [128, H + 2])
        FB1 = sb("FB1", [128, 2 * E0])
        WH = sb("WH", [128, Y_W], F32R)
        WL = sb("WL", [128, Y_W], F32R)
        SEL = sb("SEL", [128, E0 // 2 * 128], F32R)
        RC = sb("RC", [NL, 1])
        RCK = sb("RCK", [NL, 1])
        HT = sb("HT", [KP, B, NP])
        first = ExitStack()

        def fs(name, shape, dt=F32):
            return first.enter_context(nc.sbuf_tensor(name, shape, dt))

        TAP = fs("TAP", [128, HALO + 1, D])
        HU = fs("HU", [KP, B, U])
        XL = fs("XL", [D, B, U])
        HX = fs("HX", [D, B, U])
        XAP = fs("XAP", [KP, B, UL])
        XC = fs("XC", [128, B, CW])
        AA = fs("AA", [KP, B, H, NL])
        CM = fs("CM", [NL, B, H])

        s_load = sem("loaded")

        def col(t, c, p=128, n=1):
            return t[0:p, c:c + n]

        def at(i, n, k):
            return i * n + (k + 1)

        def started(eng, names):
            for name in names:
                eng.sem_inc(sem(name), 1)

        def need(eng, *waits):
            for name, value in waits:
                eng.wait_ge(sem(name), value)
            eng.wait_ge(s_load, 16)

        def ln_pe(pe, tag, src, ready, chunks, width):
            pe.wait_ge(*ready)
            for c in range(chunks):
                o = c % 2 * D
                last = nc.tensor.matmul(PS[o:o + D, c // 2, 0:width], CO[0:KP, C_CEN:C_CEN + D], src(c),
                                        start=True, stop=True)
                if c % 2:
                    last.then_inc(sem(tag + "_centred"), 1)
            for p in range(chunks // 2):
                pe.wait_ge(sem(tag + "_squared"), p + 1)
                nc.tensor.matmul(PS[:, 4 + p, 0:width], CO[:, C_AVG:C_AVG + 128], LSQ[:, p, 0:width],
                                 start=True, stop=True).then_inc(sem(tag + "_var"), 1)

        def ln_act(act, tag, chunks, width, twice):
            for p in range(chunks // 2):
                act.wait_ge(sem(tag + "_centred"), p + 1)
                nc.scalar.activation(LSQ[:, p, 0:width], PS[:, p, 0:width],
                                     ACT.Square).then_inc(sem(tag + "_squared"), 1)
            for p in range(chunks // 2):
                act.wait_ge(sem(tag + "_var"), p + 1)
                for n, t in enumerate(twice):
                    nc.scalar.activation(LST[:, p, n, 0:width], PS[:, 4 + p, 0:width],
                                         ACT.Sqrt, scale=1.0 + EPS if t else 1.0,
                                         bias=col(CO, C_EPS2 if t else C_EPS)).then_inc(sem(tag + "_rooted"), 1)

        def ln_dve(dve, tag, chunks, width, outs):
            k = len(outs)
            for p in range(chunks // 2):
                for n, dst in enumerate(outs):
                    dve.wait_ge(sem(tag + "_rooted"), p * k + n + 1)
                    nc.vector.reciprocal(LST[:, p, n, 0:width],
                                         LST[:, p, n, 0:width]).then_inc(sem(tag + "_inv"), 1)
                    dve.wait_ge(sem(tag + "_inv"), p * k + n + 1)
                    for o in range(2):
                        half = slice(o * D, (o + 1) * D)
                        nc.vector.tensor_tensor(dst(2 * p + o), PS[half, p, 0:width], LST[half, p, n, 0:width],
                                                ALU.mult).then_inc(sem(tag + "_done"), 1)

        S = ExitStack()

        def ts(name, shape, dt=F32):
            return S.enter_context(nc.sbuf_tensor(name, shape, dt))

        XA0 = ts("XA0", [128, 512])
        XA1 = ts("XA1", [D, 512])
        XC0 = ts("XC0", [128, 512])
        XC1 = ts("XC1", [D, 512])
        XQ0 = ts("XQ0", [128, 512])
        XQ1 = ts("XQ1", [D, 512])
        XS = ts("XS", [128, 512])
        TK = ts("TK", [KP, 512])
        TN = ts("TN", [D, 512])
        WVO = ts("WVO", [128, H, D])
        LSQ = ts("LSQ", [128, 2, 2 * U])
        LST = ts("LST", [128, 2, 2, 2 * U])
        WOK = ts("WOK", [128, 2, (TAPS + 1) * D])
        TS = B * NI
        assert TS == 512

        def half_tk(c):
            return TK[:, c * TS // 2:(c + 1) * TS // 2]

        with nc.Block() as block:
            @block.sync
            def _(sp):
                sp.dma_start(CO[:, :], const).then_inc(s_load, 16)
                sp.dma_start(XA0[:, :], xpatch[0:128, :]).then_inc(s_load, 16)
                sp.dma_start(XA1[:, :], xpatch[128:PF, :]).then_inc(s_load, 16)
                sp.dma_start(G1A[:, :], ln1[0:128, :]).then_inc(s_load, 16)
                sp.dma_start(G1B[:, :], ln1[128:PF, :]).then_inc(s_load, 16)
                sp.dma_start(W1A[:, :], w1[0:128, :]).then_inc(s_load, 16)
                sp.dma_start(W1B[:, :], w1[128:PF, :]).then_inc(s_load, 16)
                sp.dma_start(VE[:, :], vec).then_inc(s_load, 16)
                sp.dma_start(HU[0:D, :, NI:NI + NX], txt.rearrange("f (b n) -> f b n", b=B)).then_inc(s_load, 16)
                sp.wait_ge(sem("seq_built"), 2)
                flat = XC[:, :, :].rearrange("p b w -> p (b w)")
                sp.dma_start(flat[D:128, 0:B * CW - 1], flat[0:D, 1:B * CW]).then_inc(sem("seq_shift"), 16)
                sp.wait_ge(sem("seq_shift"), 16)

            @block.scalar
            def _(act):
                act.dma_start(MA[:, :], mat).then_inc(sem("mats"), 16)
                act.dma_start(WI[:, :], wide).then_inc(sem("wides"), 16)
                act.wait_ge(sem("p_cent"), 2)
                nc.scalar.activation(XQ0[:, :], XC0[:, :], ACT.Square)
                nc.scalar.activation(XQ1[:, :], XC1[:, :], ACT.Square).then_inc(sem("p_sq"), 1)
                act.wait_ge(sem("p_var"), 1)
                nc.scalar.activation(XS[:, :], PS[:, 1, :], ACT.Sqrt, bias=col(CO, C_EPS)).then_inc(sem("p_std"), 1)
                ln_act(act, "t2", 2, TS // 2, [False])
                ln_act(act, "tp", 2, TS // 2, [False])
                act.wait_ge(sem("tp_aff"), 1)
                nc.scalar.activation(TN[:, :], XA1[:, :], ACT.Silu).then_inc(sem("silu"), 1)
                ln_act(act, "a", 4, 2 * U, [False, True])
                act.wait_ge(sem("pool_raw"), 2)
                nc.scalar.mul(XAP[0:D, :, U + 1:U + NL], XAP[0:D, :, U + 1:U + NL], 1.0 / GRP).then_inc(sem("pooled"), 1)
                for c in range(5):
                    act.wait_ge(sem("tap_mm"), c + 1)
                    k = 8 if c < 4 else 2
                    src = PS[:, 5 + c % 3, 0:k * D].rearrange("p (j e o) -> p j e o", e=2, o=D)
                    nc.scalar.copy(TAP[0:D, 4 * c:4 * c + k // 2, :], src[0:D, :, 0, :])
                    nc.scalar.copy(TAP[D:128, 4 * c:4 * c + k // 2, :],
                                   src[D:128, :, 1, :]).then_inc(sem("tap_out"), 1)
                act.wait_ge(sem("wvo_mm"), 1)
                nc.scalar.mul(WVO[:, :, :], PS[:, 0, :].rearrange("p (h o) -> p h o", h=H),
                              VE[:, V_LS:V_LS + 1]).then_inc(sem("wvo"), 1)

            FILL_HU, FILL_XC = 3, 4

            @block.gpsimd
            def _(pool):
                for k, pad in enumerate((TK[D:KP, :], HU[D:KP, :, :], HU[0:D, :, U - 1:U], XC[:, :, :],
                                         XAP[D:KP, :, :], XAP[0:D, :, U - 1:U + 1], XAP[0:D, :, U + NL:UL],
                                         AA[D:KP, :, :, :], HT[0:D, :, N:NP], HT[D:KP, :, :],
                                         WOK[:, :, TAPS * D:])):
                    nc.gpsimd.memset(pad, 0.0).then_inc(sem("zeroed"), 1)
                    pool.wait_ge(sem("zeroed"), k + 1)
                pool.wait_ge(sem("wides"), 16)
                for t in range(2):
                    wo = WI[:, X_WO + t * D:X_WO + (t + 1) * D].unsqueeze(1).broadcast_to([128, TAPS, D])
                    kd = WI[:, X_KD + t * TAPS:X_KD + (t + 1) * TAPS].unsqueeze(2).broadcast_to([128, TAPS, D])
                    nc.gpsimd.tensor_tensor(WOK[:, t, 0:TAPS * D].rearrange("p (k o) -> p k o", o=D),
                                            wo, kd, ALU.mult).then_inc(sem("wok"), 1)
                pool.wait_ge(sem("mats"), 16)
                pool.wait_ge(s_load, 16 * 9)
                pool.wait_ge(sem("fb1_mm"), 2 * E0)
                nc.gpsimd.tensor_copy(SEL[:, :], CO[:, C_SEL:C_SEL + E0 // 2 * 128])
                for o in range(0, 2 * E0, 4):
                    w = MA[:, W_F1 + o * 128:W_F1 + (o + 4) * 128].rearrange("p (e n) -> p e n", e=2)
                    nc.gpsimd.tensor_tensor(w, w, VE[:, V_FG + o // 2:V_FG + o // 2 + 2].unsqueeze(2)
                                            .broadcast_to([128, 2, EH]), ALU.mult)
                nc.gpsimd.tensor_scalar(MA[:, W_Q:W_Q + 2 * H * D], MA[:, W_Q:W_Q + 2 * H * D],
                                        VE[:, V_LS:V_LS + 1], None, ALU.mult).then_inc(sem("wqk"), 1)
                for k, (y, w, n) in enumerate(((Y_S1, W_S1, Y_Q), (Y_Q, W_Q, Y_F1 - Y_Q), (Y_F1, W_F1, E0 * EH))):
                    pool.wait_ge(sem("wqk"), 1 + k)
                    nc.gpsimd.tensor_copy(WH[:, y:y + n], MA[:, w:w + n]).then_inc(sem("w_high"), 1)
                    pool.wait_ge(sem("w_high"), k + 1)
                    nc.gpsimd.tensor_tensor(WL[:, y:y + n], MA[:, w:w + n], WH[:, y:y + n], ALU.subtract
                                            ).then_inc(sem("wqk"), 1)
                pool.wait_ge(sem("wvo"), 1)
                wvo = WVO[:, :, :].rearrange("p h o -> p (h o)")
                nc.gpsimd.tensor_copy(WH[:, Y_VO:Y_W], wvo).then_inc(sem("w_high"), 1)
                pool.wait_ge(sem("w_high"), 4)
                nc.gpsimd.tensor_tensor(WL[:, Y_VO:Y_W], wvo, WH[:, Y_VO:Y_W], ALU.subtract).then_inc(sem("wqk"), 1)

            @block.tensor
            def _(pe):
                pe.wait_ge(s_load, 16 * 9)
                avp = CO[:, C_AVP:C_AVP + 128]
                nc.tensor.matmul(PS[:, 0, :], avp, XA0[:, :], start=True, stop=False)
                nc.tensor.matmul(PS[:, 0, :], avp[0:D, :], XA1[:, :], start=False, stop=True).then_inc(sem("p_mean"), 1)
                pe.wait_ge(sem("p_sq"), 1)
                nc.tensor.matmul(PS[:, 1, :], avp, XQ0[:, :], start=True, stop=False)
                nc.tensor.matmul(PS[:, 1, :], avp[0:D, :], XQ1[:, :], start=False, stop=True).then_inc(sem("p_var"), 1)
                pe.wait_ge(sem("p_aff"), 2)
                nc.tensor.matmul(PS[0:D, 2, :], W1A[:, :], XC0[:, :], start=True, stop=False)
                nc.tensor.matmul(PS[0:D, 2, :], W1B[:, :], XC1[:, :], start=False, stop=True).then_inc(sem("tok1"), 1)
                pe.wait_ge(sem("zeroed"), FILL_HU)
                ln_pe(pe, "t2", half_tk, (sem("tok1_b"), 1), 2, TS // 2)
                pe.wait_ge(sem("t2_aff"), 1)
                pe.wait_ge(sem("mats"), 16)
                nc.tensor.matmul(PS[0:D, 3, :], MA[0:D, W_P1:W_P1 + D], TN[:, :], start=True, stop=True).then_inc(sem("tok2"), 1)
                ln_pe(pe, "tp", half_tk, (sem("tok2_b"), 1), 2, TS // 2)
                pe.wait_ge(sem("silu"), 1)
                nc.tensor.matmul(PS[0:D, 4, :], MA[0:D, W_P2:W_P2 + D], TN[:, :], start=True, stop=True).then_inc(sem("tok3"), 1)
                ln_pe(pe, "a", lambda c: HU[:, 2 * c:2 * c + 2, :].rearrange("p b n -> p (b n)"), (sem("stream"), 1), 4, 2 * U)
                pe.wait_ge(sem("a_done"), 8)
                for j in range(2 * E0):
                    nc.tensor.matmul(PS[:, 4, j:j + 1], MA[0:D, W_F1 + j * 128:W_F1 + (j + 1) * 128],
                                     VE[0:D, V_FB + j // 2:V_FB + j // 2 + 1], start=True, stop=True
                                     ).then_inc(sem("fb1_mm"), 1)
                pe.wait_ge(sem("wok"), 2)
                for c in range(5):
                    w = 512 if c < 4 else 2 * D
                    if c >= 3:
                        pe.wait_ge(sem("tap_out"), c - 2)
                    for t in range(2):
                        last = nc.tensor.matmul(PS[:, 5 + c % 3, 0:w], WI[:, X_WVT + t * 128:X_WVT + (t + 1) * 128],
                                                WOK[:, t, c * 512:c * 512 + w], start=t == 0, stop=t == 1)
                    last.then_inc(sem("tap_mm"), 1)
                for h in range(H):
                    for o in range(2):
                        last = nc.tensor.matmul(PS[o * D:(o + 1) * D, 0, h * D:(h + 1) * D],
                                                MA[0:D, W_VT + h * D:W_VT + (h + 1) * D],
                                                MA[0:D, W_OT + h * D:W_OT + (h + 1) * D], start=True, stop=True)
                last.then_inc(sem("wvo_mm"), 1)

            @block.vector
            def _(dve):
                v = nc.vector
                dve.wait_ge(sem("p_mean"), 1)
                v.tensor_tensor(XC0[:, :], XA0[:, :], PS[:, 0, :], ALU.subtract).then_inc(sem("p_cent"), 1)
                v.tensor_tensor(XC1[:, :], XA1[:, :], PS[0:D, 0, :], ALU.subtract).then_inc(sem("p_cent"), 1)
                dve.wait_ge(sem("p_std"), 1)
                v.reciprocal(XQ0[:, :], XS[:, :]).then_inc(sem("p_rstd"), 1)
                dve.wait_ge(sem("p_rstd"), 1)
                v.tensor_tensor(XA0[:, :], XC0[:, :], XQ0[:, :], ALU.mult).then_inc(sem("p_norm"), 1)
                v.tensor_tensor(XA1[:, :], XC1[:, :], XQ0[0:D, :], ALU.mult).then_inc(sem("p_norm"), 1)
                dve.wait_ge(sem("p_norm"), 2)
                v.tensor_scalar(XC0[:, :], XA0[:, :], G1A[:, 0:1], G1A[:, 1:2], ALU.mult, ALU.add).then_inc(sem("p_aff"), 1)
                v.tensor_scalar(XC1[:, :], XA1[:, :], G1B[:, 0:1], G1B[:, 1:2], ALU.mult, ALU.add).then_inc(sem("p_aff"), 1)
                dve.wait_ge(sem("tok1"), 1)
                v.tensor_scalar(TK[0:D, :], PS[0:D, 2, :], VE[0:D, V_B1:V_B1 + 1], None, ALU.add).then_inc(sem("tok1_b"), 1)
                ln_dve(dve, "t2", 2, TS // 2, [lambda c: TN[:, c * TS // 2:(c + 1) * TS // 2]])
                dve.wait_ge(sem("t2_done"), 2)
                v.tensor_scalar(TN[:, :], TN[:, :], VE[0:D, V_G2:V_G2 + 1], VE[0:D, V_B2:V_B2 + 1], ALU.mult, ALU.add
                                ).then_inc(sem("t2_aff"), 1)
                dve.wait_ge(sem("tok2"), 1)
                v.tensor_scalar(TK[0:D, :], PS[0:D, 3, :], VE[0:D, V_BP1:V_BP1 + 1], None, ALU.add).then_inc(sem("tok2_b"), 1)
                ln_dve(dve, "tp", 2, TS // 2, [lambda c: TN[:, c * TS // 2:(c + 1) * TS // 2]])
                dve.wait_ge(sem("tp_done"), 2)
                v.tensor_scalar(XA1[:, :], TN[:, :], VE[0:D, V_GP:V_GP + 1], VE[0:D, V_BP:V_BP + 1], ALU.mult, ALU.add
                                ).then_inc(sem("tp_aff"), 1)
                dve.wait_ge(sem("tok3"), 1)
                dve.wait_ge(sem("zeroed"), FILL_HU)
                v.tensor_scalar(HU[0:D, :, 0:NI], PS[0:D, 4, :].rearrange("p (b n) -> p b n", b=B),
                                VE[0:D, V_BP2:V_BP2 + 1], None, ALU.add).then_inc(sem("stream"), 1)
                flat = lambda t, c: t[:, 2 * c:2 * c + 2, :].rearrange("p b n -> p (b n)")
                ln_dve(dve, "a", 4, 2 * U, [lambda c: flat(XL, c), lambda c: flat(HX, c)])
                dve.wait_ge(sem("a_done"), 8)
                v.tensor_scalar(XAP[0:D, :, 0:U - 1], HX[:, :, 0:U - 1], VE[0:D, V_GA:V_GA + 1], VE[0:D, V_BA:V_BA + 1],
                                ALU.mult, ALU.add).then_inc(sem("a_in"), 1)
                dve.wait_ge(sem("a_in"), 1)
                dve.wait_ge(sem("zeroed"), FILL_XC)
                v.tensor_copy(XC[0:D, :, HALO:HALO + COPIES * NI].rearrange("p b (r n) -> p b r n", r=COPIES),
                              XAP[0:D, :, 0:NI].unsqueeze(2).broadcast_to([D, B, COPIES, NI])).then_inc(sem("seq_built"), 1)
                v.tensor_copy(XC[0:D, :, HALO + COPIES * NI:HALO + N], XAP[0:D, :, NI:NI + NX]).then_inc(sem("seq_built"), 1)
                dve.wait_ge(sem("seq_built"), 2)
                first = GRP - PAD % GRP
                v.tensor_reduce(XAP[0:D, :, U + 1:U + 2], XC[0:D, :, HALO:HALO + first], AX.X, ALU.add
                                ).then_inc(sem("pool_raw"), 1)
                v.tensor_reduce(XAP[0:D, :, U + 2:U + NL],
                                XC[0:D, :, HALO + first:HALO + N].rearrange("p b (j t) -> p b j t", t=GRP),
                                AX.X, ALU.add).then_inc(sem("pool_raw"), 1)
                v.scalar_tensor_tensor(out=HX[:, :, :], in0=HU[0:D, :, :], scalar=VE[0:D, V_BO:V_BO + 1], in1=XL[:, :, :],
                                       op0=ALU.add, op1=ALU.add).then_inc(sem("resid"), 1)
                dve.wait_ge(sem("fb1_mm"), 2 * E0)
                dve.wait_ge(sem("wides"), 16)
                v.tensor_scalar(NG[:, :], WI[:, X_GAM:X_GAM + H + 2], -1.0, None, ALU.mult)
                v.tensor_tensor(FB1[:, :], PS[:, 4, 0:2 * E0], WI[:, X_B1:X_B1 + 2 * E0], ALU.add).then_inc(sem("fb1"), 1)
        phase_over()
        S.close()


        S = ExitStack()
        QL = ts("QL", [128, 4, KP])
        DD = ts("DD", [NL, H, NL])
        EE = ts("EE", [NL, H, NL])
        MX = ts("MX", [NL, H])
        MX2 = ts("MX2", [NL, 2, H])
        ZZ = ts("ZZ", [NL, 4, H])
        with nc.Block() as block:
            @block.sync
            def _(sp):
                started(sp, LOOP1)

            @block.tensor
            def _(pe):
                with pe.Fori(0, B) as i:
                    need(pe, ("n_qk", at(i, 1, 0)))
                    for j in range(4):
                        last = nc.tensor.matmul(PS[:, 0, j * KP:(j + 1) * KP],
                                                MA[0:KP, W_QKV + j * 128:W_QKV + (j + 1) * 128],
                                                XAP[:, i, U:UL], start=True, stop=True)
                    last.then_inc(sem("n_proj"), 1)
                    need(pe, ("n_qk", at(i, 1, 1)), ("n_sub", at(i, 1, 0)))
                    for g in range(H):
                        r, hh = g // 2, g % 2
                        last = nc.tensor.matmul(PS[0:KP, 1 + r, hh * KP:(hh + 1) * KP],
                                                QL[32 * r:32 * r + 32, hh, :], QL[32 * r:32 * r + 32, 2 + hh, :],
                                                start=True, stop=True)
                    last.then_inc(sem("n_score"), 1)
                pe.wait_ge(sem("n_sub"), B + 1)
                with pe.Fori(0, B // 2) as i:
                    for o in range(2):
                        need(pe, ("n_a", i * 2 + (o + 2)), ("n_cm", at(i, 2, o)))
                        for q in range(2):
                            last = nc.tensor.matmul(PS[0:NL, 4 + 2 * o + q, 0:4 * NL], CO[0:KP, C_D:C_D + NL],
                                                    AA[:, bass.ds(i * 2 + o, 1), 4 * q:4 * q + 4, :].rearrange("p a h n -> p (a h n)"),
                                                    start=True, stop=True)
                        last.then_inc(sem("n_cs"), 1)

            @block.scalar
            def _(act):
                with act.Fori(0, B) as i:
                    need(act, ("n_proj", at(i, 1, 1)), ("n_score", at(i, 1, 0)))
                    nc.scalar.copy(QL[:, :, :], PS[:, 0, 0:4 * KP].rearrange("p (j n) -> p j n", j=4)
                                   ).then_inc(sem("n_qk"), 1)
                    need(act, ("n_sub", at(i, 1, 1)), ("n_a", at(i, 1, 0)))
                    nc.scalar.activation(EE[:, :, :], DD[:, :, :], ACT.Exp, scale=SC).then_inc(sem("n_exp"), 1)

            @block.vector
            def _(dve):
                v = nc.vector
                score = PS[0:NL, 1:5, 0:2 * KP].rearrange("p r (k n) -> p r k n", k=2)[:, :, :, 0:NL]
                with dve.Fori(0, B) as i:
                    need(dve, ("n_score", at(i, 1, 1)))
                    v.tensor_reduce(MX[:, :].rearrange("p (r k) -> p r k", k=2), score, AX.X, ALU.max
                                    ).then_inc(sem("n_max"), 1)
                    need(dve, ("n_max", at(i, 1, 1)), ("n_exp", at(i, 1, 0)))
                    v.tensor_tensor(DD[:, :, :].rearrange("p (r k) n -> p r k n", k=2), score,
                                    MX[:, :].rearrange("p (r k) -> p r k", k=2).unsqueeze(3).broadcast_to([NL, 4, 2, NL]),
                                    ALU.subtract).then_inc(sem("n_sub"), 1)
                    need(dve, ("n_exp", at(i, 1, 1)))
                    v.tensor_reduce(ZZ[:, 0, :], EE[:, :, :], AX.X, ALU.add).then_inc(sem("n_z"), 1)
                    need(dve, ("n_z", at(i, 4, 1)))
                    v.scalar_tensor_tensor(out=ZZ[:, 1, :], in0=EE[:, :, 0], scalar=float(ZL - 1), in1=ZZ[:, 0, :],
                                           op0=ALU.mult, op1=ALU.add).then_inc(sem("n_z"), 1)
                    need(dve, ("n_z", at(i, 4, 2)))
                    v.reciprocal(ZZ[:, 2, :], ZZ[:, 1, :]).then_inc(sem("n_z"), 1)
                    v.tensor_scalar(EE[:, :, 0], EE[:, :, 0], ROOT, None, ALU.mult).then_inc(sem("n_e0"), 1)
                    need(dve, ("n_z", at(i, 4, 3)))
                    v.tensor_scalar(ZZ[:, 3, :], ZZ[:, 2, :], CO[0:NL, C_DV:C_DV + 1], None, ALU.mult
                                    ).then_inc(sem("n_z"), 1)
                    need(dve, ("n_z", at(i, 4, 4)), ("n_e0", at(i, 1, 1)))
                    v.tensor_tensor(AA[0:NL, i, :, :], EE[:, :, :], ZZ[:, 3, :].unsqueeze(2).broadcast_to([NL, H, NL]),
                                    ALU.mult).then_inc(sem("n_a"), 1)
                with dve.Fori(0, B // 2) as i:
                    for o in range(2):
                        need(dve, ("n_cs", at(i, 2, o + 1)))
                        sums = PS[0:NL, 4 + 2 * o:6 + 2 * o, 0:4 * NL].rearrange("p q (k n) -> p q k n", k=4)
                        top = MX2[:, o, :].rearrange("p (q k) -> p q k", k=4)
                        v.tensor_reduce(top, sums[:, :, :, 1:NL], AX.X, ALU.max).then_inc(sem("n_c1"), 1)
                        need(dve, ("n_c1", at(i, 2, o + 1)))
                        v.scalar_tensor_tensor(out=CM[:, bass.ds(i * 2 + o, 1), :].rearrange("p a (q k) -> p q (a k)", k=4),
                                               in0=sums[:, :, :, 0], scalar=1.0 / ROOT, in1=top,
                                               op0=ALU.mult, op1=ALU.max).then_inc(sem("n_cm"), 1)
                dve.wait_ge(sem("n_cm"), B + 1)
                v.tensor_reduce(MX2[:, 0, 0:1], CM[:, :, :], AX.XY, ALU.max).then_inc(sem("n_top"), 1)
                dve.wait_ge(sem("n_top"), 1)
                v.reciprocal(RC[:, :], MX2[:, 0, 0:1]).then_inc(sem("n_rc"), 1)
                dve.wait_ge(sem("n_rc"), 1)
                v.tensor_scalar(RCK[:, :], RC[:, :], (13.0 / 4.0) ** ITERS, None, ALU.mult)
        phase_over()
        S.close()

        S = ExitStack()
        XS = ts("XS_", [KP, UL])
        XW = ts("XW", [128, CW])
        QK = ts("QK", [128, 2, 2, UL])
        VU = ts("VU", [UT, 2, H * DH])
        AS = ts("AS", [KP, H, NL])
        AT = ts("AT", [KP, H, KP])
        M3 = ts("M3", [NL, H])
        E3 = ts("E3", [KP, H, U])
        Z3 = ts("Z3", [NL, 4, H])
        P3 = ts("P3", [UT, H, 2, KP])
        M1 = ts("M1", [UT, 2 * H])
        E1_ = ts("E1_", [UT, 2 * H, NL])
        P1 = ts("P1", [KP, 2 * H, NL])
        Z1 = ts("Z1", [UT, 3, 2 * H])
        PT = ts("PT", [KP, H, U])
        ST = ts("ST", [KP, H, SW])
        TA = ts("TA", [KP, H, SW])
        TX = ts("TX", [KP, H, SW])
        TD = ts("TD", [NL, H, SW])
        UU = ts("UU", [KP, H, DH])
        OO = ts("OO", [128, 2, U])
        with nc.Block() as block:
            @block.sync
            def _(sp):
                started(sp, LOOP2)

            def taps(j0, j1):
                for j in range(j0, j1):
                    o = j % 2 * D
                    nc.tensor.matmul(PS[o:o + D, 3, 0:NP], TAP[:, j, :], XW[:, 2 * j:2 * j + NP],
                                     start=j < 2, stop=j == 15, skip_group_check=True)

            @block.tensor
            def _(pe):
                with pe.Fori(0, B) as i:
                    need(pe, ("f_x", at(i, 1, 1)), ("f_u", at(i, 1, 0)), ("f_res", at(i, 1, 0)), ("f_oo", at(i, 1, 0)))
                    for j in range(4):
                        last = nc.tensor.matmul(PS[:, j // 2, (j % 2) * UL:(j % 2 + 1) * UL],
                                                MA[0:KP, W_QKV + j * 128:W_QKV + (j + 1) * 128],
                                                XS[:, :], start=True, stop=True)
                    last.then_inc(sem("f_qk"), 1)
                    for t in range(2):
                        last = nc.tensor.matmul(PS[0:UT, 2, t * 256:(t + 1) * 256], XS[:, t * UT:(t + 1) * UT],
                                                MA[0:KP, W_QKV + 512:W_QKV + 768], start=True, stop=True)
                    last.then_inc(sem("f_v"), 1)
                    need(pe, ("f_qks", at(i, 2, 2)), ("f_st", at(i, 2 * ITERS, 0)))
                    for g in range(H):
                        r, hh = g // 2, g % 2
                        last = nc.tensor.matmul(PS[0:KP, 4 + r, hh * U:(hh + 1) * U],
                                                QK[32 * r:32 * r + 32, 0, hh, U:UL], QK[32 * r:32 * r + 32, 1, hh, 0:U],
                                                start=True, stop=True)
                    last.then_inc(sem("f_s3"), 1)
                    need(pe, ("f_vu", at(i, 1, 1)))
                    for g in range(H):
                        r, hh = g // 2, g % 2
                        for t in range(2):
                            c = (2 * hh + t) * KP
                            last = nc.tensor.matmul(PS[0:UT, r, c:c + KP],
                                                    QK[32 * r:32 * r + 32, 0, hh, t * UT:(t + 1) * UT],
                                                    QK[32 * r:32 * r + 32, 1, hh, U:UL], start=True, stop=True)
                    last.then_inc(sem("f_s1"), 1)
                    need(pe, ("f_e3", at(i, 1, 1)))
                    for g in range(H):
                        for t in range(2):
                            c = ((g % 2) * 2 + t) * KP
                            last = nc.tensor.transpose(PS[0:UT, 4 + g // 2, c:c + KP], E3[:, g, t * UT:(t + 1) * UT],
                                                       ident[0:KP, 0:KP])
                    last.then_inc(sem("f_t3"), 1)
                    need(pe, ("f_p3", at(i, 1, 1)), ("f_as", at(i, 1, 1)))
                    for g in range(H):
                        last = nc.tensor.transpose(PS[0:NL, 4 + g // 4, (g % 4) * KP:(g % 4 + 1) * KP], AS[:, g, :],
                                                   ident[0:KP, 0:KP])
                    last.then_inc(sem("f_t2"), 1)
                    need(pe, ("f_d1", at(i, 1, 1)))
                    for g in range(H):
                        h = g % 2 * 4 + g // 2
                        for t in range(2):
                            last = nc.tensor.matmul(PS[0:NL, 3, g * DH:(g + 1) * DH], P3[:, g, t, 0:NL],
                                                    VU[:, t, h * DH:(h + 1) * DH], start=t == 0, stop=t == 1)
                    last.then_inc(sem("f_w"), 1)
                    need(pe, ("f_at", at(i, 1, 1)))
                    for g in range(H):
                        last = nc.tensor.matmul(PS[0:NL, 6 + g // 4, (g % 4) * KP:(g % 4 + 1) * KP], AT[:, g, 0:NL],
                                                AT[:, g, :], start=True, stop=True)
                    last.then_inc(sem("f_aa"), 1)
                    for it in range(ITERS):
                        for q in range(2):
                            if it == 0:
                                need(pe, ("f_y0", at(i, 2, 2)), ("f_w0", at(i, 1, 1)))
                            else:
                                need(pe, ("f_st", at(i, 2 * ITERS, 2 * it - 1 + q)))
                            for g in range(4 * q, 4 * q + 4):
                                last = nc.tensor.matmul(PS[0:NL, 4 + q, (g % 4) * SW:(g % 4 + 1) * SW],
                                                        ST[:, g, 0:NL], ST[:, g, :], start=True, stop=True)
                            last.then_inc(sem("f_m1"), 1)
                        if it == 0:
                            need(pe, ("f_p1", at(i, 1, 1)))
                            for g in range(H):
                                for t in range(2):
                                    c = g % 3 * U + t * UT
                                    last = nc.tensor.transpose(PS[0:NL, g // 3, c:c + KP], P1[:, 2 * g + t, :],
                                                               ident[0:KP, 0:KP])
                            last.then_inc(sem("f_t1"), 1)
                        else:
                            if it == 1:
                                need(pe, ("f_xw", at(i, 1, 1)))
                            taps((it - 1) * 3, min(it * 3, 17))
                        for q in range(2):
                            need(pe, ("f_ta", at(i, 2 * ITERS, 2 * it + q + 1)), ("f_tx", at(i, 2 * ITERS, 2 * it + q + 1)))
                            for g in range(4 * q, 4 * q + 4):
                                c0 = 0 if it < ITERS - 1 else NL
                                last = nc.tensor.matmul(PS[0:NL, 6 + q, (g % 4) * SW + c0:(g % 4 + 1) * SW],
                                                        TA[:, g, 0:NL], TX[:, g, c0:SW], start=True, stop=True)
                            last.then_inc(sem("f_m2"), 1)
                    taps(15, 17)
                    need(pe, ("f_st", at(i, 2 * ITERS, 2 * ITERS)), ("f_pt", at(i, 1, 1)))
                    for g in range(H):
                        last = nc.tensor.matmul(PS[0:NL, 0, g * DH:(g + 1) * DH], AS[:, g, :], ST[:, g, NL:SW],
                                                start=True, stop=True)
                    last.then_inc(sem("f_um"), 1)
                    need(pe, ("f_u", at(i, 1, 1)))
                    for g in range(H):
                        r, hh = g // 2, g % 2
                        last = nc.tensor.matmul(PS[32 * r:32 * r + 32, 1, hh * U:(hh + 1) * U], UU[:, g, :], PT[:, g, :],
                                                start=True, stop=True)
                    last.then_inc(sem("f_o"), 1)
                    need(pe, ("f_oo", at(i, 1, 1)))
                    for t in range(2):
                        wo = WI[:, X_WO + t * D:X_WO + (t + 1) * D]
                        nc.tensor.matmul(PS[0:D, 3, 0:COPIES * NI], wo,
                                         OO[:, t, 0:NI].unsqueeze(1).broadcast_to([128, COPIES, NI]),
                                         start=False, stop=False, skip_group_check=True)
                        last = nc.tensor.matmul(PS[0:D, 3, COPIES * NI:N], wo, OO[:, t, NI:NI + NX],
                                                start=False, stop=t == 1, skip_group_check=True)
                    last.then_inc(sem("f_out"), 1)

            @block.scalar
            def _(act):
                act.wait_ge(sem("f_pad"), 8)
                with act.Fori(0, B) as i:
                    need(act, ("f_qk", at(i, 1, 1)), ("f_s1", at(i, 1, 0)))
                    nc.scalar.copy(QK[:, 0, :, :], PS[:, 0, 0:2 * UL].rearrange("p (j n) -> p j n", j=2)
                                   ).then_inc(sem("f_qks"), 1)
                    need(act, ("f_sub3", at(i, 1, 1)))
                    nc.scalar.activation(E3[0:NL, :, :], E3[0:NL, :, :], ACT.Exp, scale=SC).then_inc(sem("f_e3"), 1)
                    need(act, ("f_t3", at(i, 1, 1)))
                    nc.scalar.copy(P3[:, :, :, :].rearrange("p (b g) t n -> p b (g t n)", b=4), PS[0:UT, 4:8, 0:4 * KP]
                                   ).then_inc(sem("f_p3"), 1)
                    need(act, ("f_t2", at(i, 1, 1)))
                    nc.scalar.copy(AT[0:NL, :, :].rearrange("p (b g) n -> p b (g n)", b=2), PS[0:NL, 4:6, 0:4 * KP]
                                   ).then_inc(sem("f_at"), 1)
                    need(act, ("f_d1", at(i, 1, 1)))
                    nc.scalar.activation(E1_[:, :, :], E1_[:, :, :], ACT.Exp, scale=SC).then_inc(sem("f_e1"), 1)
                    need(act, ("f_aa", at(i, 1, 1)))
                    for q in range(2):
                        nc.scalar.mul(ST[0:NL, 4 * q:4 * q + 4, 0:NL],
                                      PS[0:NL, 6 + q, 0:4 * KP].rearrange("p (g n) -> p g n", g=4)[:, :, 0:NL],
                                      RC[:, 0:1]).then_inc(sem("f_y0"), 1)
                    kappa = 1.0
                    for it in range(ITERS):
                        for q in range(2):
                            need(act, ("f_m1", at(i, 2 * ITERS, 2 * it + q + 1)))
                            nc.scalar.mul(TA[0:NL, 4 * q:4 * q + 4, :],
                                          PS[0:NL, 4 + q, 0:4 * SW].rearrange("p (g n) -> p g n", g=4),
                                          15.0 / 13.0 * kappa).then_inc(sem("f_ta"), 1)
                        if it == 0:
                            need(act, ("f_t1", at(i, 1, 1)))
                            nc.scalar.copy(PT[0:NL, 0:6, :].rearrange("p (b g) n -> p b (g n)", b=2),
                                           PS[0:NL, 0:2, 0:3 * U])
                            nc.scalar.copy(PT[0:NL, 6:8, :].rearrange("p g n -> p (g n)"),
                                           PS[0:NL, 2, 0:2 * U]).then_inc(sem("f_pt"), 1)
                        kappa *= 13.0 / 4.0
                    need(act, ("f_um", at(i, 1, 1)))
                    nc.scalar.mul(UU[0:NL, :, :], PS[0:NL, 0, 0:H * DH].rearrange("p (g n) -> p g n", g=H), RCK[:, 0:1]
                                  ).then_inc(sem("f_u"), 1)
                    need(act, ("f_o", at(i, 1, 1)))
                    nc.scalar.copy(OO[:, :, :], PS[:, 1, 0:2 * U].rearrange("p (t n) -> p t n", t=2)).then_inc(sem("f_oo"), 1)

            @block.gpsimd
            def _(pool):
                with pool.Fori(0, B) as i:
                    need(pool, ("f_v", at(i, 1, 0)))
                    nc.gpsimd.tensor_copy(XS[:, :], XAP[:, i, :]).then_inc(sem("f_x"), 1)
                    need(pool, ("f_out", at(i, 1, 0)))
                    nc.gpsimd.tensor_copy(XW[:, :], XC[:, i, :]).then_inc(sem("f_xw"), 1)
                    need(pool, ("f_um", at(i, 1, 0)))
                    nc.gpsimd.tensor_copy(AS[:, :, :], AA[:, i, :, :]).then_inc(sem("f_as"), 1)
                    need(pool, ("f_z1", at(i, 3, 3)), ("f_e10", at(i, 1, 1)), ("f_t1", at(i, 1, 0)))
                    nc.gpsimd.tensor_tensor(P1[0:UT, :, :], E1_[:, :, :],
                                            Z1[:, 2, :].unsqueeze(2).broadcast_to([UT, 2 * H, NL]),
                                            ALU.mult).then_inc(sem("f_p1"), 1)
                    for it in range(ITERS):
                        for q in range(2):
                            need(pool, ("f_ta", at(i, 2 * ITERS, 2 * it + q + 1)))
                            nc.gpsimd.tensor_tensor(TD[:, 4 * q:4 * q + 4, :], ST[0:NL, 4 * q:4 * q + 4, :],
                                                    TA[0:NL, 4 * q:4 * q + 4, :], ALU.subtract).then_inc(sem("f_td"), 1)

            @block.vector
            def _(dve):
                v = nc.vector
                s3 = PS[0:NL, 4:8, 0:2 * U].rearrange("p r (k n) -> p r k n", k=2)
                s1 = PS[0:UT, 0:4, 0:4 * KP].rearrange("p r (k n) -> p r k n", k=4)[:, :, :, 0:NL]
                for pad in (AT, E3, P1, PT, ST, TA, TX, UU):
                    v.memset(pad[D:KP, :, :], 0.0).then_inc(sem("f_pad"), 1)
                dve.wait_ge(sem("f_pad"), 8)
                with dve.Fori(0, B) as i:
                    need(dve, ("f_qk", at(i, 1, 1)), ("f_s1", at(i, 1, 0)))
                    v.tensor_copy(QK[:, 1, :, :], PS[:, 1, 0:2 * UL].rearrange("p (j n) -> p j n", j=2)
                                  ).then_inc(sem("f_qks"), 1)
                    need(dve, ("f_v", at(i, 1, 1)), ("f_w", at(i, 1, 0)))
                    v.tensor_tensor(VU[:, :, :], PS[0:UT, 2, :].rearrange("p (t n) -> p t n", t=2),
                                    CO[0:UT, C_KW:C_KW + 2].unsqueeze(2).broadcast_to([UT, 2, H * DH]),
                                    ALU.mult).then_inc(sem("f_vu"), 1)
                    need(dve, ("f_s3", at(i, 1, 1)))
                    v.tensor_reduce(M3[:, :].rearrange("p (r k) -> p r k", k=2), s3, AX.X, ALU.max).then_inc(sem("f_m3"), 1)
                    need(dve, ("f_m3", at(i, 1, 1)), ("f_t3", at(i, 1, 0)))
                    v.tensor_tensor(E3[0:NL, :, :].rearrange("p (r k) n -> p r k n", k=2), s3,
                                    M3[:, :].rearrange("p (r k) -> p r k", k=2).unsqueeze(3).broadcast_to([NL, 4, 2, U]),
                                    ALU.subtract).then_inc(sem("f_sub3"), 1)
                    need(dve, ("f_s1", at(i, 1, 1)))
                    v.tensor_reduce(M1[:, :].rearrange("p (r k) -> p r k", k=4), s1, AX.X, ALU.max).then_inc(sem("f_mm1"), 1)
                    need(dve, ("f_mm1", at(i, 1, 1)), ("f_p1", at(i, 1, 0)))
                    v.tensor_tensor(E1_[:, :, :].rearrange("p (r k) n -> p r k n", k=4), s1,
                                    M1[:, :].rearrange("p (r k) -> p r k", k=4).unsqueeze(3).broadcast_to([UT, 4, 4, NL]),
                                    ALU.subtract).then_inc(sem("f_d1"), 1)
                    need(dve, ("f_e3", at(i, 1, 1)))
                    v.tensor_reduce(Z3[:, 0, :], E3[0:NL, :, 0:NI], AX.X, ALU.add).then_inc(sem("f_z3"), 1)
                    v.tensor_reduce(Z3[:, 1, :], E3[0:NL, :, :], AX.X, ALU.add).then_inc(sem("f_z3"), 1)
                    need(dve, ("f_z3", at(i, 5, 2)))
                    v.scalar_tensor_tensor(out=Z3[:, 2, :], in0=Z3[:, 0, :], scalar=float(COPIES - 1), in1=Z3[:, 1, :],
                                           op0=ALU.mult, op1=ALU.add).then_inc(sem("f_z3"), 1)
                    need(dve, ("f_z3", at(i, 5, 3)))
                    v.scalar_tensor_tensor(out=Z3[:, 3, :], in0=E3[0:NL, :, U - 1], scalar=float(PAD - 1), in1=Z3[:, 2, :],
                                           op0=ALU.mult, op1=ALU.add).then_inc(sem("f_z3"), 1)
                    need(dve, ("f_z3", at(i, 5, 4)))
                    v.reciprocal(Z3[:, 0, :], Z3[:, 3, :]).then_inc(sem("f_z3"), 1)
                    need(dve, ("f_z3", at(i, 5, 5)))
                    v.tensor_scalar(Z3[:, 1, :], Z3[:, 0, :], CO[0:NL, C_DV:C_DV + 1], None, ALU.mult).then_inc(sem("f_r3"), 1)
                    need(dve, ("f_w", at(i, 1, 1)), ("f_r3", at(i, 1, 1)), ("f_um", at(i, 1, 0)))
                    v.tensor_tensor(ST[0:NL, :, NL:SW], PS[0:NL, 3, 0:H * DH].rearrange("p (g n) -> p g n", g=H),
                                    Z3[:, 1, :].unsqueeze(2).broadcast_to([NL, H, DH]), ALU.mult).then_inc(sem("f_w0"), 1)
                    need(dve, ("f_e1", at(i, 1, 1)), ("f_p1", at(i, 1, 0)))
                    v.tensor_reduce(Z1[:, 0, :], E1_[:, :, :], AX.X, ALU.add).then_inc(sem("f_z1"), 1)
                    need(dve, ("f_z1", at(i, 3, 1)))
                    v.scalar_tensor_tensor(out=Z1[:, 1, :], in0=E1_[:, :, 0], scalar=float(ZL - 1), in1=Z1[:, 0, :],
                                           op0=ALU.mult, op1=ALU.add).then_inc(sem("f_z1"), 1)
                    need(dve, ("f_z1", at(i, 3, 2)))
                    v.reciprocal(Z1[:, 2, :], Z1[:, 1, :]).then_inc(sem("f_z1"), 1)
                    v.tensor_scalar(E1_[:, :, 0], E1_[:, :, 0], ROOT, None, ALU.mult).then_inc(sem("f_e10"), 1)
                    kappa = 1.0
                    for it in range(ITERS):
                        for q in range(2):
                            need(dve, ("f_ta", at(i, 2 * ITERS, 2 * it + q + 1)))
                            v.scalar_tensor_tensor(out=TX[0:NL, 4 * q:4 * q + 4, :], in0=ST[0:NL, 4 * q:4 * q + 4, :],
                                                   scalar=7.0 * 15.0 / 13.0, in1=TA[0:NL, 4 * q:4 * q + 4, :],
                                                   op0=ALU.mult, op1=ALU.subtract).then_inc(sem("f_tx"), 1)
                        for q in range(2):
                            c0 = 0 if it < ITERS - 1 else NL
                            need(dve, ("f_m2", at(i, 2 * ITERS, 2 * it + q + 1)), ("f_td", at(i, 2 * ITERS, 2 * it + q + 1)))
                            v.scalar_tensor_tensor(
                                out=ST[0:NL, 4 * q:4 * q + 4, c0:SW],
                                in0=PS[0:NL, 6 + q, 0:4 * SW].rearrange("p (g n) -> p g n", g=4)[:, :, c0:SW],
                                scalar=kappa * 13.0 / 225.0, in1=TD[:, 4 * q:4 * q + 4, c0:SW],
                                op0=ALU.mult, op1=ALU.add).then_inc(sem("f_st"), 1)
                        kappa *= 13.0 / 4.0
                    need(dve, ("f_out", at(i, 1, 1)))
                    v.tensor_tensor(HT[0:D, i, 0:COPIES * NI].rearrange("p (r n) -> p r n", r=COPIES),
                                    PS[0:D, 3, 0:COPIES * NI].rearrange("p (r n) -> p r n", r=COPIES),
                                    HX[:, i, 0:NI].unsqueeze(1).broadcast_to([D, COPIES, NI]), ALU.add
                                    ).then_inc(sem("f_hx"), 1)
                    v.tensor_tensor(HT[0:D, i, COPIES * NI:N], PS[0:D, 3, COPIES * NI:N], HX[:, i, NI:NI + NX], ALU.add
                                    ).then_inc(sem("f_hx"), 1)
                    need(dve, ("f_hx", at(i, 2, 2)))
                    v.tensor_tensor(HT[0:D, i, 0:N], PS[D:128, 3, 0:N], HT[0:D, i, 0:N], ALU.add).then_inc(sem("f_res"), 1)
        phase_over()
        S.close()

        first.close()
        XM = sb("XM", [128, B + 1, NP], F32R)
        XR = sb("XR", [D, B, NP])
        XN = sb("XN", [D, B, NP])
        WR = sb("WR", [TT, B * NT, E0])
        WT = sb("WT", [128, B, NP], F32R)

        def chunk(t, c, p=D):
            return t[0:p, :, :].rearrange("p b n -> p (b n)")[:, CH * c:CH * (c + 1)]

        def router_pe(pe, tag, weights, n, ready):
            pe.wait_ge(*ready)
            for k in range(B * NT):
                last = nc.tensor.matmul(PS[0:TT, 0, k * n:(k + 1) * n], XR[:, k // NT, k % NT * TT:(k % NT + 1) * TT],
                                        weights, start=True, stop=True)
            last.then_inc(sem(tag + "_logit"), 1)

        def router_turn(pe, tag, n):
            pe.wait_ge(sem(tag + "_w"), 1)
            for k in range(B * NT):
                last = nc.tensor.transpose(PS[0:n, 1 + k // 5, k % 5 * TT:(k % 5 + 1) * TT], WR[:, k, 0:n],
                                           ident[0:TT, 0:TT])
            last.then_inc(sem(tag + "_turned"), 1)

        def router_act(act, tag, n, gates):
            act.wait_ge(sem(tag + "_sub"), 1)
            nc.scalar.activation(RE[:, :, 0:n], RD[:, :, 0:n], ACT.Exp).then_inc(sem(tag + "_exp"), 1)
            if gates:
                act.wait_ge(sem(tag + "_gsub"), 1)
                nc.scalar.activation(RE[:, :, 0:n], RD[:, :, 0:n], ACT.Exp).then_inc(sem(tag + "_gexp"), 1)
            act.wait_ge(sem(tag + "_turned"), 1)
            for q in range(5):
                w = min(5, B * NT - 5 * q) * TT
                nc.scalar.copy(WT[0:n, :, :].rearrange("p b n -> p (b n)")[:, 5 * TT * q:5 * TT * q + w],
                               PS[0:n, 1 + q, 0:w]).then_inc(sem(tag + "_wt"), 1)

        def router_dve(dve, tag, bias, n, gates):
            v = nc.vector
            K = B * NT
            steps = [0]

            def step(ins):
                ins.then_inc(sem(tag + "_step"), 1)
                steps[0] += 1
                dve.wait_ge(sem(tag + "_step"), steps[0])

            wide = lambda x: x.unsqueeze(2).broadcast_to([TT, K, n])
            iota = CO[0:TT, C_IOTA:C_IOTA + n].unsqueeze(1).broadcast_to([TT, K, n])
            L, D_, T, O1, O2 = (x[:, :, 0:n] for x in (RL, RD, RT, R1, R2))
            dve.wait_ge(sem(tag + "_logit"), 1)
            step(v.tensor_tensor(L, PS[0:TT, 0, 0:K * n].rearrange("p (k n) -> p k n", n=n),
                                 bias.unsqueeze(1).broadcast_to([TT, K, n]), ALU.add))
            step(v.tensor_reduce(RM[:, 0, :], L, AX.X, ALU.max))
            v.tensor_tensor(D_, L, wide(RM[:, 0, :]), ALU.subtract).then_inc(sem(tag + "_sub"), 1)
            top = RM[:, 0, :]
            for k, hot in enumerate((O1, O2)):
                step(v.tensor_tensor(T, L, wide(top), ALU.is_lt))
                step(v.scalar_tensor_tensor(out=T, in0=T, scalar=100.0, in1=iota, op0=ALU.mult, op1=ALU.add))
                step(v.tensor_reduce(RM[:, 1, :], T, AX.X, ALU.min))
                step(v.tensor_tensor(hot, iota, wide(RM[:, 1, :]), ALU.is_equal))
                if k == 0:
                    step(v.scalar_tensor_tensor(out=L, in0=hot, scalar=-1e30, in1=L, op0=ALU.mult, op1=ALU.add))
                    step(v.tensor_reduce(RM[:, 2, :], L, AX.X, ALU.max))
                    top = RM[:, 2, :]
            step(v.tensor_tensor(O1, O1, O2, ALU.add))
            dve.wait_ge(sem(tag + "_exp"), 1)
            if gates:
                step(v.tensor_reduce(RM[:, 1, :], RE[:, :, 0:n], AX.X, ALU.add))
                step(v.reciprocal(RM[:, 2, :], RM[:, 1, :]))
                step(v.tensor_tensor(T, RE[:, :, 0:n], wide(RM[:, 2, :]), ALU.mult))
                v.tensor_tensor(D_, T, wide(RM[:, 2, :]), ALU.subtract).then_inc(sem(tag + "_gsub"), 1)
                dve.wait_ge(sem(tag + "_gexp"), 1)
            step(v.tensor_tensor(T, RE[:, :, 0:n], O1, ALU.mult))
            step(v.tensor_reduce(RM[:, 1, :], T, AX.X, ALU.add))
            step(v.reciprocal(RM[:, 2, :], RM[:, 1, :]))
            v.tensor_tensor(WR[:, :, 0:n], T, wide(RM[:, 2, :]), ALU.mult).then_inc(sem(tag + "_w"), 1)
            for q in range(5):
                dve.wait_ge(sem(tag + "_wt"), q + 1)
                w = min(5, K - 5 * q) * TT
                part = WT[:, :, :].rearrange("p b n -> p (b n)")[:, 5 * TT * q:5 * TT * q + w]
                v.tensor_tensor(part[32:32 + n, :], PS[0:n, 1 + q, 0:w], part[0:n, :], ALU.subtract)

        def split_pool(pool, tag, src, done):
            for c in range(NCH):
                pool.wait_ge(sem(tag + "_done"), done(c))
                nc.gpsimd.tensor_copy(chunk(XM, c), chunk(src, c)).then_inc(sem(tag + "_high"), 1)
                pool.wait_ge(sem(tag + "_high"), c + 1)
                nc.gpsimd.tensor_tensor(XM[D:128, :, :].rearrange("p b n -> p (b n)")[:, CH * c:CH * (c + 1)],
                                        chunk(src, c), chunk(XM, c), ALU.subtract).then_inc(sem(tag + "_low"), 1)
                pool.wait_ge(sem(tag + "_low"), c + 1)

        RL, RD, RT, R1, R2, RE = (sb(n, [TT, B * NT, E0]) for n in ("RL", "RD", "RT", "R1", "R2", "RE"))
        RM = sb("RM", [TT, 3, B * NT])
        CH = 360
        NCH = B * NP // CH
        LSQ = sb("LSQb", [128, NCH // 2, CH])
        LST = sb("LSTb", [128, NCH // 2, 2, CH])

        def add_halves(t):
            with nc.Block() as block:
                @block.tensor
                def _(pe):
                    for c in range(NCH):
                        nc.tensor.matmul(PS[0:D, c, 0:CH], CO[:, C_II:C_II + D], chunk(t, c, 128),
                                         start=True, stop=True).then_inc(sem("halves"), 1)

                @block.vector
                def _(dve):
                    for c in range(NCH):
                        dve.wait_ge(sem("halves"), c + 1)
                        nc.vector.tensor_tensor(chunk(HT, c), PS[0:D, c, 0:CH], chunk(HT, c), ALU.add)
            phase_over()

        with nc.Block() as block:
            @block.tensor
            def _(pe):
                ln_pe(pe, "b", lambda c: chunk(HT, c, KP), (s_load, 16), NCH, CH)
                router_pe(pe, "r", MA[0:D, W_R:W_R + E0], E0, (sem("b_done"), 2 * NCH))
                router_turn(pe, "r", E0)

            @block.gpsimd
            def _(pool):
                nc.gpsimd.memset(WT[:, :, :].bitcast(F32), 0.0).then_inc(sem("clear"), 1)
                pool.wait_ge(sem("clear"), 1)
                nc.gpsimd.memset(XM[:, B, :].bitcast(F32), 0.0).then_inc(sem("clear"), 1)
                pool.wait_ge(sem("clear"), 2)
                split_pool(pool, "b", XN, lambda c: 4 * (c // 2) + 2 + c % 2 + 1)

            @block.scalar
            def _(act):
                ln_act(act, "b", NCH, CH, [False, True])
                act.wait_ge(sem("clear"), 1)
                router_act(act, "r", E0, False)

            @block.vector
            def _(dve):
                ln_dve(dve, "b", NCH, CH, [lambda c: chunk(XR, c), lambda c: chunk(XN, c)])
                router_dve(dve, "r", WI[0:TT, X_BR:X_BR + E0], E0, False)
        phase_over()

        S = ExitStack()
        GE = ts("GE", [128, 2 * E0, NP])
        YW = ts("YW", [128, 4, NP])
        WB = ts("WB", [128, 2, NP])
        YS = ts("YS", [128, 2, NP])
        YA = ts("YA", [128, B, NP])
        PAIRS = E0 // 2
        AHEAD = 4
        with nc.Block() as block:
            @block.sync
            def _(sp):
                started(sp, LOOP3)
                sp.sem_inc(sem("m_y"), PAIRS)
                sp.sem_inc(sem("m_started"), 1)

            def y_at(i, k):
                return at(i, PAIRS, k) + PAIRS

            @block.tensor
            def _(pe):
                def hidden(x, j):
                    nc.tensor.matmul(PS[:, j % AHEAD, 0:NP], WH[:, Y_F1 + j * 128:Y_F1 + (j + 1) * 128], x,
                                     start=True, stop=False)
                    nc.tensor.matmul(PS[:, j % AHEAD, 0:NP], WL[:, Y_F1 + j * 128:Y_F1 + (j + 1) * 128], x,
                                     start=False, stop=True).then_inc(sem("m_h"), 1)

                pe.wait_ge(sem("m_started"), 1)
                for j in range(AHEAD):
                    hidden(XM[:, 0, :], j)
                with pe.Fori(0, B) as i:
                    for q in range(PAIRS):
                        need(pe, ("m_yw", at(i, PAIRS, max(q - 1, 0))))
                        nc.tensor.matmul(PS[:, 6 + q % 2, 0:NP], SEL[:, q * 128:(q + 1) * 128], WT[:, i, :],
                                         start=True, stop=True).then_inc(sem("m_w"), 1)
                        for k in range(4):
                            need(pe, ("m_g", at(i, 2 * E0, 4 * q + k + 1)))
                            j = 4 * q + k + AHEAD
                            hidden(XM[:, i, :] if j < 2 * E0 else XM[:, bass.ds(i + 1, 1), :].rearrange("p a n -> p (a n)"),
                                   j % (2 * E0))
                            if k >= 2:
                                for o in range(2):
                                    g = 4 * q + 2 * o + k - 2
                                    last = nc.tensor.matmul(PS[o * D:(o + 1) * D, 4 + q % 2, 0:NP],
                                                            WI[:, X_F2 + g * D:X_F2 + (g + 1) * D], GE[:, g, :],
                                                            start=k == 2, stop=k == 3)
                        last.then_inc(sem("m_y"), 1)

            @block.scalar
            def _(act):
                with act.Fori(0, B) as i:
                    for j in range(2 * E0):
                        need(act, ("m_h", at(i, 2 * E0, j + 1)), ("m_y", y_at(i, j // 4 + 1 - PAIRS)))
                        nc.scalar.activation(GE[:, j, :], PS[:, j % AHEAD, 0:NP], ACT.Gelu, bias=FB1[:, j:j + 1]
                                             ).then_inc(sem("m_g"), 1)

            @block.vector
            def _(dve):
                v = nc.vector
                with dve.Fori(0, B) as i:
                    for q in range(PAIRS):
                        need(dve, ("m_w", at(i, PAIRS, q + 1)))
                        v.tensor_copy(WB[:, q % 2, :], PS[:, 6 + q % 2, 0:NP]).then_inc(sem("m_wb"), 1)
                        need(dve, ("m_wb", at(i, PAIRS, q + 1)), ("m_y", y_at(i, q + 1)), ("m_s", at(i, 3, 0 if q < 2 else 1)))
                        v.scalar_tensor_tensor(out=YW[:, q, :], in0=PS[:, 4 + q % 2, 0:NP],
                                               scalar=WI[:, X_B2 + q:X_B2 + q + 1], in1=WB[:, q % 2, :],
                                               op0=ALU.add, op1=ALU.mult).then_inc(sem("m_yw"), 1)

            @block.gpsimd
            def _(pool):
                with pool.Fori(0, B) as i:
                    for o in range(2):
                        need(pool, ("m_yw", at(i, PAIRS, 2 * o + 2)), ("m_s", at(i, 3, 0)))
                        nc.gpsimd.tensor_tensor(YS[:, o, :], YW[:, 2 * o, :], YW[:, 2 * o + 1, :], ALU.add
                                                ).then_inc(sem("m_s"), 1)
                    need(pool, ("m_s", at(i, 3, 2)))
                    nc.gpsimd.tensor_tensor(YA[:, i, :], YS[:, 0, :], YS[:, 1, :], ALU.add).then_inc(sem("m_s"), 1)
        phase_over()
        add_halves(YA)
        S.close()

        with nc.Block() as block:
            @block.tensor
            def _(pe):
                ln_pe(pe, "c", lambda c: chunk(HT, c, KP), (s_load, 16), NCH, CH)

            @block.scalar
            def _(act):
                ln_act(act, "c", NCH, CH, [True])

            @block.gpsimd
            def _(pool):
                split_pool(pool, "c", XN, lambda c: c + 1)

            @block.vector
            def _(dve):
                ln_dve(dve, "c", NCH, CH, [lambda c: chunk(XN, c)])
        phase_over()

        S = ExitStack()
        NK = 288
        XK = ts("XK", [128, NK], F32R)
        QR = ts("QR", [128, 2, H, NP])
        KA = ts("KA", [128, 2, H, NK])
        SQ = ts("SQ", [128, 4, NK])
        K2 = ts("K2", [128, 2, 2 * H + 2])
        VM = ts("VM", [128, 2, 2, H * D])
        VR = ts("VR", [128, 2, 2, D])
        CL = ts("CL", [128, 3, 2, NP])
        EX = ts("EX", [128, 3, 2, NP])
        UN = H + 1
        PAIRS = H // 2
        VT0, VT1, VLAST = PAIRS, PAIRS + 1, PAIRS + 2
        FREE = {"d_cl": 4, "d_e": 3, "d_pv": 3, "d_res": 1}

        def atb(name, i, o, n, k):
            return i * (2 * n) + (o * n + k + 1 + FREE.get(name, 0))

        def batches(eng, body):
            with eng.Fori(0, B // 2 - 1) as i:
                body(i, 0, True)
                body(i, 1, True)
            body(B // 2 - 1, 0, True)
            body(B // 2 - 1, 1, False)

        with nc.Block() as block:
            @block.sync
            def _(sp):
                started(sp, LOOP4)
                for name, count in FREE.items():
                    sp.sem_inc(sem(name), count)
                sp.sem_inc(sem("d_started"), 1)

            @block.gpsimd
            def _(pool):
                for k, (rows, value) in enumerate(((XK[:, :].bitcast(F32), 0.0), (KA[D:128, :, :, :], 1.0))):
                    nc.gpsimd.memset(rows, value).then_inc(sem("d_ones"), 1)
                    pool.wait_ge(sem("d_ones"), k + 1)
                pool.wait_ge(sem("d_started"), 1)
                with pool.Fori(0, B) as i:
                    need(pool, ("d_v", at(i, 3, 0)))
                    nc.gpsimd.tensor_copy(XK[:, 0:N], XM[:, i, 0:N]).then_inc(sem("d_x"), 1)

            @block.tensor
            def _(pe):
                def split_product(out_, y, m, x, swap=False):
                    for k, w in enumerate((WH, WL)):
                        last = nc.tensor.matmul(out_, x if swap else w[:, y:y + m], w[:, y:y + m] if swap else x,
                                                start=k == 0, stop=k == 1)
                    return last

                def front(i, o, s):
                    if s < PAIRS:
                        if s == 0:
                            need(pe, ("d_x", atb("d_x", i, o, 1, 1)), ("d_vm", atb("d_vm", i, o, 4, 0)))
                        else:
                            need(pe, ("d_qa", atb("d_qa", i, o, PAIRS, s)))
                        split_product(PS[:, 5, 0:NP], Y_Q + s * 128, 128, XK[:, 0:NP]).then_inc(sem("d_q"), 1)
                        if s:
                            need(pe, ("d_sq", atb("d_sq", i, o, PAIRS, s)))
                        split_product(PS[:, 6, 0:NK], Y_K + s * 128, 128, XK[:, :]).then_inc(sem("d_k"), 1)
                    elif s == VT0:
                        need(pe, ("d_qa", atb("d_qa", i, o, PAIRS, PAIRS)))
                        split_product(PS[:, 5, :], Y_VO, H * D, XK[:, 0:128], True).then_inc(sem("d_v"), 1)
                    elif s == VT1:
                        need(pe, ("d_sq", atb("d_sq", i, o, PAIRS, PAIRS)))
                        split_product(PS[:, 6, :], Y_VO, H * D, XK[:, 128:256], True).then_inc(sem("d_v"), 1)
                    elif s == VLAST:
                        need(pe, ("d_vm", atb("d_vm", i, o, 4, 2)))
                        split_product(PS[0:32, 5, :], Y_VO, H * D, XK[:, 256:288], True)
                        for p in range(PAIRS):
                            for t in range(2):
                                c = t * H + 2 * p
                                nc.tensor.matmul(PS[:, 6, c:c + 2], SQ[:, p, t * 128:(t + 1) * 128], CO[:, C_NS:C_NS + 2],
                                                 start=True, stop=True)
                        for h in range(H):
                            r = h % 4
                            last = nc.tensor.matmul(PS[32 * r:32 * r + 32, 6, 2 * H + h // 4:2 * H + h // 4 + 1],
                                                    SQ[:, h // 2, 256:288], CO[:, C_NS + h % 2:C_NS + h % 2 + 1],
                                                    start=True, stop=True)
                        last.then_inc(sem("d_v"), 1)

                def scores(i, o, u):
                    a = o % 2
                    if u == 0:
                        need(pe, ("d_vm", atb("d_vm", i, o, 4, 4)))
                    for t in range(2):
                        bank = 1 + (2 * UN * a + 2 * u + t) % 4
                        need(pe, ("d_cl", atb("d_cl", i, o, 2 * UN, 2 * u + t - 3)))
                        if u < H:
                            last = nc.tensor.matmul(PS[:, bank, 0:NP], KA[:, a, u, t * 128:(t + 1) * 128],
                                                    QR[:, a, u, :], start=True, stop=True)
                        else:
                            for r in range(4):
                                last = nc.tensor.matmul(PS[32 * r:32 * r + 32, bank, 0:NP],
                                                        KA[:, a, 4 * t + r, 256:288], QR[:, a, 4 * t + r, :],
                                                        start=True, stop=True)
                        last.then_inc(sem("d_s"), 1)

                def body(i, o, ahead):
                    for u in range(UN):
                        need(pe, ("d_e", atb("d_e", i, o, UN, u + 1)))
                        if u == 0:
                            need(pe, ("d_res", atb("d_res", i, o, 1, -1)))
                        for t in range(2):
                            last = nc.tensor.matmul(PS[t * D:(t + 1) * D, 7 * o, 0:NP],
                                                    VM[:, o, t, u * D:(u + 1) * D] if u < H else VR[:, o, t, :],
                                                    EX[:, u % 3, t, :], start=u == 0, stop=u == UN - 1)
                        last.then_inc(sem("d_pv"), 1)
                        if u + 2 < UN:
                            scores(i, o, u + 2)
                        elif ahead:
                            scores(i, o + 1, u + 2 - UN)
                        if ahead:
                            front(i, o + 1, u)

                pe.wait_ge(sem("d_started"), 1)
                pe.wait_ge(sem("d_ones"), 2)
                for s in range(VLAST + 1):
                    front(0, 0, s)
                for u in range(2):
                    scores(0, 0, u)
                batches(pe, body)

            @block.scalar
            def _(act):
                def front(i, o, s):
                    if s >= PAIRS:
                        return
                    a = o % 2
                    need(act, ("d_q", atb("d_q", i, o, PAIRS, s + 1)))
                    for k in range(2):
                        half = PS[k * D:(k + 1) * D, 5, 0:NP]
                        nc.scalar.mul(QR[0:D, a, 2 * s + k, :], half, -2.0)
                        last = nc.scalar.activation(QR[D:128, a, 2 * s + k, :], half, ACT.Square)
                    last.then_inc(sem("d_qa"), 1)
                    need(act, ("d_ka", atb("d_ka", i, o, PAIRS, s + 1)))
                    nc.scalar.activation(SQ[:, s, :], PS[:, 6, 0:NK], ACT.Square).then_inc(sem("d_sq"), 1)

                def exps(i, o, u):
                    need(act, ("d_cl", atb("d_cl", i, o, 2 * UN, 2 * u + 2)), ("d_pv", atb("d_pv", i, o, UN, u - 2)))
                    if u < H:
                        nc.scalar.activation(EX[:, u % 3, :, :], CL[:, u % 3, :, :], ACT.Exp,
                                             scale=NG[:, u:u + 1]).then_inc(sem("d_e"), 1)
                    else:
                        nc.scalar.activation(EX[:, u % 3, 0, :], CL[:, u % 3, 0, :], ACT.Exp, scale=NG[:, H:H + 1])
                        nc.scalar.activation(EX[:, u % 3, 1, :], CL[:, u % 3, 1, :], ACT.Exp,
                                             scale=NG[:, H + 1:H + 2]).then_inc(sem("d_e"), 1)

                def body(i, o, ahead):
                    for u in range(UN):
                        if u + 1 < UN:
                            exps(i, o, u + 1)
                        elif ahead:
                            exps(i, o + 1, 0)
                        if ahead:
                            front(i, o + 1, u)

                act.wait_ge(sem("d_started"), 1)
                for s in range(PAIRS):
                    front(0, 0, s)
                exps(0, 0, 0)
                batches(act, body)

            @block.vector
            def _(dve):
                v = nc.vector

                def front(i, o, s):
                    a = o % 2
                    if s < PAIRS:
                        need(dve, ("d_k", atb("d_k", i, o, PAIRS, s + 1)))
                        for k in range(2):
                            last = v.tensor_copy(KA[0:D, a, 2 * s + k, :], PS[k * D:(k + 1) * D, 6, 0:NK])
                        last.then_inc(sem("d_ka"), 1)
                    elif s in (VT0, VT1):
                        need(dve, ("d_v", atb("d_v", i, o, 3, s - VT0 + 1)))
                        v.tensor_copy(VM[:, a, s - VT0, :], PS[:, 5 + s - VT0, :]).then_inc(sem("d_vm"), 1)
                    elif s == VLAST:
                        need(dve, ("d_v", atb("d_v", i, o, 3, 3)))
                        for r in range(4):
                            last = v.tensor_copy(VR[32 * r:32 * r + 32, a, :, :],
                                                 PS[0:32, 5, :].rearrange("p (t r d) -> p t r d", t=2, r=4)[:, :, r, :])
                        last.then_inc(sem("d_vm"), 1)
                        v.tensor_copy(K2[:, a, :], PS[:, 6, 0:2 * H + 2]).then_inc(sem("d_vm"), 1)

                def clamp(i, o, u):
                    a = o % 2
                    if u == 0:
                        need(dve, ("d_vm", atb("d_vm", i, o, 4, 4)))
                    for t in range(2):
                        bank = 1 + (2 * UN * a + 2 * u + t) % 4
                        c = t * H + u if u < H else 2 * H + t
                        need(dve, ("d_s", atb("d_s", i, o, 2 * UN, 2 * u + t + 1)),
                             ("d_e", atb("d_e", i, o, UN, u - 2)))
                        v.tensor_scalar(CL[:, u % 3, t, :], PS[:, bank, 0:NP], K2[:, a, c:c + 1], 0.0, ALU.add, ALU.max
                                        ).then_inc(sem("d_cl"), 1)

                def body(i, o, ahead):
                    for u in range(UN):
                        if u + 2 < UN:
                            clamp(i, o, u + 2)
                        elif ahead:
                            clamp(i, o + 1, u + 2 - UN)
                        if ahead:
                            front(i, o + 1, u)
                    need(dve, ("d_pv", atb("d_pv", i, o, UN, UN)))
                    mine = HT[0:D, bass.ds(i * 2 + o, 1), 0:N].rearrange("p a n -> p (a n)")
                    v.tensor_tensor(mine, PS[0:D, 7 * o, 0:N], mine, ALU.add).then_inc(sem("d_half"), 1)
                    need(dve, ("d_half", atb("d_half", i, o, 1, 1)))
                    v.tensor_tensor(mine, PS[D:128, 7 * o, 0:N], mine, ALU.add).then_inc(sem("d_res"), 1)

                dve.wait_ge(sem("d_started"), 1)
                for s in range(VLAST + 1):
                    front(0, 0, s)
                for u in range(2):
                    clamp(0, 0, u)
                batches(dve, body)
        phase_over()
        S.close()

        with nc.Block() as block:
            @block.tensor
            def _(pe):
                ln_pe(pe, "d", lambda c: chunk(HT, c, KP), (s_load, 16), NCH, CH)
                router_pe(pe, "g", MA[0:D, W_G:W_G + E1], E1, (sem("d_done"), NCH))
                router_turn(pe, "g", E1)

            @block.gpsimd
            def _(pool):
                split_pool(pool, "d", XR, lambda c: c + 1)

            @block.scalar
            def _(act):
                ln_act(act, "d", NCH, CH, [False])
                router_act(act, "g", E1, True)

            @block.vector
            def _(dve):
                ln_dve(dve, "d", NCH, CH, [lambda c: chunk(XR, c)])
                router_dve(dve, "g", WI[0:TT, X_GB:X_GB + E1], E1, True)
        phase_over()

        S = ExitStack()
        H1 = ts("H1", [128, E1, NP])
        S1 = ts("S1", [KP, NP])
        H2 = ts("H2", [128, 2, NP])
        S2 = ts("S2", [128, NP])
        GB = ts("GB", [128, 2, NP])
        YG = ts("YG", [128, 2, NP])
        GA = ts("GA", [128, NP])
        HF = ts("HF", [KP, NP])
        OS = ts("OS", [TT, NT, D])

        def nxt(i, o, n, k):
            return i * n + (o * n + k + 1)

        with nc.Block() as block:
            @block.sync
            def _(sp):
                started(sp, LOOP5)
                sp.sem_inc(sem("g_started"), 1)
                with sp.Fori(0, B) as i:
                    need(sp, ("g_os", at(i, 1, 1)))
                    sp.dma_start(out[bass.ds(i, 1), 0:2 * TT, :].rearrange("b (t p) d -> p (b t) d", p=TT),
                                 OS[:, 0:2, :]).then_inc(sem("g_put"), 16)
                    sp.dma_start(out[bass.ds(i, 1), 2 * TT:N, :].rearrange("b p d -> p (b d)"), OS[0:N - 2 * TT, 2, :]
                                 ).then_inc(sem("g_put"), 16)
                sp.wait_ge(sem("g_put"), 32 * B + 1)

            @block.gpsimd
            def _(pool):
                for k, pad in enumerate((S1[D:KP, :], HF[D:KP, :])):
                    nc.gpsimd.memset(pad, 0.0).then_inc(sem("g_pad"), 1)
                    pool.wait_ge(sem("g_pad"), k + 1)
                with pool.Fori(0, B) as i:
                    need(pool, ("g_fin", at(i, 1, 0)))
                    nc.gpsimd.tensor_tensor(HF[0:D, :], HT[0:D, i, :], WI[0:D, X_SB3:X_SB3 + 1].broadcast_to([D, NP]),
                                            ALU.add).then_inc(sem("g_hf"), 1)
                    need(pool, ("g_yg", at(i, 2, 2)))
                    nc.gpsimd.tensor_tensor(GA[:, :], YG[:, 0, :], YG[:, 1, :], ALU.add).then_inc(sem("g_ga"), 1)

            @block.tensor
            def _(pe):
                def first_layer(i, o):
                    x = XM[:, bass.ds(i + o, 1), :].rearrange("p a n -> p (a n)")
                    need(pe, ("g_h1", nxt(i, o, 4, 0)), ("g_s2", nxt(i, o, 1, 0)), ("g_os", at(i, 1, 0)))
                    for bank, y, m in ((0, Y_E1, 128), (1, Y_E1 + 128, 128), (4, Y_S1, D),
                                       (2, Y_E1 + 256, 128), (3, Y_E1 + 384, 128)):
                        for k, w in enumerate((WH, WL)):
                            last = nc.tensor.matmul(PS[0:m, bank, 0:NP], w[:, y:y + m], x, start=k == 0, stop=k == 1)
                        last.then_inc(sem("g_l1"), 1)

                def second_layer(i, o):
                    need(pe, ("g_s1", nxt(i, o, 1, 1)))
                    nc.tensor.matmul(PS[:, 4, 0:NP], MA[0:KP, W_S2:W_S2 + 128], S1[:, :], start=True, stop=True
                                     ).then_inc(sem("g_l2"), 1)
                    need(pe, ("g_h1", nxt(i, o, 4, 4)), ("g_yg", nxt(i, o, 2, 0)))
                    for e in range(E1):
                        last = nc.tensor.matmul(PS[e % 2 * D:(e % 2 + 1) * D, 5 + e // 2, 0:NP],
                                                WI[:, X_E2 + e * D:X_E2 + (e + 1) * D], H1[:, e, :],
                                                start=True, stop=True)
                        if e % 2:
                            last.then_inc(sem("g_l2"), 1)

                def third_layer(i):
                    for q in range(2):
                        need(pe, ("g_gb", at(i, 2, q)))
                        nc.tensor.matmul(PS[:, 7, 0:NP], SEL[:, q * 128:(q + 1) * 128],
                                         WT[:, bass.ds(i + 0, 1), :].rearrange("p a n -> p (a n)"),
                                         start=True, stop=True).then_inc(sem("g_gate"), 1)
                        if q == 0:
                            need(pe, ("g_h2", at(i, 2, 2)))
                        nc.tensor.matmul(PS[:, 5 + q, 0:NP], WI[:, X_E3 + q * 128:X_E3 + (q + 1) * 128],
                                         H2[:, q, :], start=True, stop=True).then_inc(sem("g_l3"), 1)

                def output(i, ahead):
                    need(pe, ("g_ga", at(i, 1, 1)), ("g_hf", at(i, 1, 1)), ("g_s2", at(i, 1, 1)))
                    if ahead:
                        need(pe, ("g_h1", nxt(i, 1, 4, 4)))
                    for t in range(NT):
                        tok = slice(t * TT, (t + 1) * TT)
                        fin = PS[0:TT, 3, t * D:(t + 1) * D]
                        nc.tensor.matmul(fin, GA[:, tok], CO[:, C_II:C_II + D], start=True, stop=False)
                        nc.tensor.matmul(fin, S2[:, tok], WI[:, X_S3:X_S3 + D], start=False, stop=False)
                        last = nc.tensor.matmul(fin, HF[:, tok], ident[0:KP, 0:D], start=False, stop=True)
                    last.then_inc(sem("g_fin"), 1)

                pe.wait_ge(sem("g_started"), 1)
                pe.wait_ge(sem("g_pad"), 2)
                first_layer(0, 0)
                second_layer(0, 0)
                with pe.Fori(0, B - 1) as i:
                    first_layer(i, 1)
                    third_layer(i)
                    second_layer(i, 1)
                    output(i, True)
                third_layer(B - 1)
                output(B - 1, False)

            @block.scalar
            def _(act):
                def layers(i, o):
                    need(act, ("g_l1", nxt(i, o, 5, 1)), ("g_l2", nxt(i, o, 3, 0)))
                    nc.scalar.activation(H1[:, 0, :], PS[:, 0, 0:NP], ACT.Relu, bias=WI[:, X_EB1:X_EB1 + 1]
                                         ).then_inc(sem("g_h1"), 1)
                    need(act, ("g_l1", nxt(i, o, 5, 3)))
                    nc.scalar.activation(S1[0:D, :], PS[0:D, 4, 0:NP], ACT.Relu, bias=VE[0:D, V_SB1:V_SB1 + 1]
                                         ).then_inc(sem("g_s1"), 1)
                    need(act, ("g_l1", nxt(i, o, 5, 4)))
                    nc.scalar.activation(H1[:, 2, :], PS[:, 2, 0:NP], ACT.Relu, bias=WI[:, X_EB1 + 2:X_EB1 + 3]
                                         ).then_inc(sem("g_h1"), 1)

                def layers2(i, o):
                    need(act, ("g_l2", nxt(i, o, 3, 2)), ("g_l3", nxt(i, o, 2, 0)))
                    nc.scalar.activation(H2[:, 0, :], PS[:, 5, 0:NP], ACT.Relu, bias=WI[:, X_EB2:X_EB2 + 1]
                                         ).then_inc(sem("g_h2"), 1)
                    need(act, ("g_l2", nxt(i, o, 3, 1)), ("g_fin", nxt(i, o, 1, 0)))
                    nc.scalar.activation(S2[:, :], PS[:, 4, 0:NP], ACT.Relu, bias=WI[:, X_SB2:X_SB2 + 1]
                                         ).then_inc(sem("g_s2"), 1)

                def gates(i):
                    for q in range(2):
                        need(act, ("g_gate", at(i, 2, q + 1)), ("g_yg", at(i, 2, 0)))
                        nc.scalar.copy(GB[:, q, :], PS[:, 7, 0:NP]).then_inc(sem("g_gb"), 1)

                layers(0, 0)
                layers2(0, 0)
                with act.Fori(0, B - 1) as i:
                    layers(i, 1)
                    gates(i)
                    layers2(i, 1)
                gates(B - 1)

            @block.vector
            def _(dve):
                v = nc.vector

                def layers(i, o):
                    for e in (1, 3):
                        need(dve, ("g_l1", nxt(i, o, 5, 2 if e == 1 else 5)), ("g_l2", nxt(i, o, 3, 0)))
                        v.tensor_scalar(H1[:, e, :], PS[:, e, 0:NP], WI[:, X_EB1 + e:X_EB1 + e + 1], 0.0, ALU.add, ALU.max
                                        ).then_inc(sem("g_h1"), 1)

                def layers2(i, o):
                    need(dve, ("g_l2", nxt(i, o, 3, 3)), ("g_l3", nxt(i, o, 2, 0)))
                    v.tensor_scalar(H2[:, 1, :], PS[:, 6, 0:NP], WI[:, X_EB2 + 1:X_EB2 + 2], 0.0, ALU.add, ALU.max
                                    ).then_inc(sem("g_h2"), 1)

                def gated(i):
                    for q in range(2):
                        need(dve, ("g_l3", at(i, 2, q + 1)), ("g_gb", at(i, 2, q + 1)), ("g_ga", at(i, 1, 0)))
                        v.scalar_tensor_tensor(out=YG[:, q, :], in0=PS[:, 5 + q, 0:NP],
                                               scalar=WI[:, X_EB3 + q:X_EB3 + q + 1], in1=GB[:, q, :],
                                               op0=ALU.add, op1=ALU.mult).then_inc(sem("g_yg"), 1)

                def output(i):
                    need(dve, ("g_fin", at(i, 1, 1)), ("g_put", at(i, 32, 0)))
                    v.tensor_copy(OS[:, :, :], PS[0:TT, 3, 0:NT * D].rearrange("p (t d) -> p t d", t=NT)
                                  ).then_inc(sem("g_os"), 1)

                layers(0, 0)
                layers2(0, 0)
                with dve.Fori(0, B - 1) as i:
                    layers(i, 1)
                    gated(i)
                    layers2(i, 1)
                    output(i)
                gated(B - 1)
                output(B - 1)
        phase_over()
        S.close()


_OUT = (B, N, D)


def kernel(**inputs):
    import concourse.bacc as bacc
    from concourse.bass_utils import run_bass_kernel_spmd as run

    a = {k: np.asarray(v) for k, v in inputs.items()}
    t = lambda m: np.ascontiguousarray(m)
    x = a["x"].reshape(B, 3, 8, 8, 8, 8).transpose(3, 5, 1, 0, 2, 4).reshape(PF, B * NI)
    txt = a["txt"].transpose(2, 0, 1).reshape(D, B * NX)
    ln1 = np.stack([a["L0_tok_ln1_g"], a["L0_tok_ln1_b"]], 1)
    names = ["L0_tok_b1", "L0_tok_ln2_g", "L0_tok_ln2_b", "L0_tok_bp1", "L0_tok_lnp_g", "L0_tok_lnp_b", "L0_tok_bp2",
             "L0_attn_ln_g", "L0_attn_ln_b", "L0_attn_b_out", "L1_attn_ln_scale", "L1_ffn_sb1"]
    vec = np.concatenate([np.stack([a[n] for n in names], 1), a["L0_ffn_ln_g"].T, a["L0_ffn_ln_b"].T], 1)
    side = lambda w: w.transpose(1, 0, 2).reshape(w.shape[1], -1)
    w_qkv = a["L0_attn_w_qkv"]
    mat = np.concatenate([
        a["L0_tok_Wp1"], a["L0_tok_Wp2"], w_qkv, a["L0_ffn_Wr"], a["L1_ffn_gW"], a["L1_ffn_sW1"], a["L1_ffn_sW2"],
        side(a["L1_ffn_eW1"]), side(a["L1_attn_W_q"]), side(a["L1_attn_W_k"]),
        side(a["L1_attn_W_v"].transpose(0, 2, 1)),
        a["L1_attn_W_o"].reshape(D, H, D).transpose(2, 1, 0).reshape(D, H * D),
        side(a["L0_ffn_W1"])], 1)
    rows = lambda r: np.broadcast_to(r[None, :], (128, r.shape[0]))
    halves = lambda w: w.reshape(2, 128, -1).transpose(1, 0, 2)
    kd = halves(np.repeat(a["L0_attn_res_kernel"].reshape(H, TAPS), DH, 0)).reshape(128, -1)
    wvt = halves(w_qkv[:, 512:768].T)
    e3 = np.zeros((2, D, 2, 2, D), np.float32)
    for o in range(2):
        e3[o, :, :, o, :] = a["L1_ffn_eW3"][o::2].transpose(1, 0, 2)
    e3 = e3.reshape(128, 2 * 128)
    wide = np.concatenate([
        a["L0_ffn_b1"].reshape(E0 * 2, 128).T, a["L1_ffn_sb2"][:, None], a["L1_ffn_eb1"].T,
        a["L1_ffn_eb2"].reshape(2, 128).T, rows(a["L1_attn_gamma"].reshape(H)),
        np.repeat(a["L1_attn_gamma"].reshape(2, 4), 32, 1).T, rows(a["L0_ffn_br"]),
        rows(a["L1_ffn_gb"]), kd, a["L1_ffn_sW3"], side(a["L1_ffn_eW2"]), e3,
        np.concatenate([wvt, wvt], 2).reshape(128, -1), halves(a["L0_attn_w_out"]).reshape(128, -1),
        a["L0_ffn_W2"].reshape(E0 * 2, 128, D).transpose(1, 0, 2).reshape(128, -1),
        a["L0_ffn_b2"].reshape(4, 128).T, np.concatenate([a["L1_ffn_sb3"]] * 2)[:, None],
        a["L1_ffn_eb3"].reshape(2, 128).T], 1)
    arrays = {"xpatch": x, "txt": txt, "w1": a["L0_tok_W1"], "ln1": ln1, "vec": np.concatenate([vec, vec], 0), "mat": np.concatenate([mat, mat], 0), "wide": wide,
              "const": shape_constants()}
    arrays = {k: t(v) for k, v in arrays.items()}
    nc = bacc.Bacc("TRN2", target_bir_lowering=False, num_devices=1)
    args = [nc.dram_tensor(k, v.shape, F32, kind="ExternalInput").ap() for k, v in arrays.items()]
    args.append(nc.dram_tensor("out_0", _OUT, F32, kind="ExternalOutput").ap())
    program(nc, *args)
    return run(nc, [arrays], core_ids=[0]).results[0]["out_0"]
```

```python
from contextlib import ExitStack

import numpy as np

import concourse.bass as bass
from concourse import mybir

F32 = mybir.dt.float32
F32R = mybir.dt.float32r
ALU = mybir.AluOpType
ACT = mybir.ActivationFunctionType
AX = mybir.AxisListType

B = 8
D = 64
NI = 64
NX = 77
COPIES = 3
N = COPIES * NI + NX
LM = 128
PAD = -N % LM
GRP = (N + PAD) // LM
ZL = PAD // GRP
NL = LM - ZL + 1
U = NI + NX + 1
UT = U // 2
KP = 96
UL = U + KP
H = 8
DH = 32
SC = DH ** -0.5
TAPS = 33
HALO = TAPS // 2
CW = 304
NP = 270
TT = 90
NT = 3
SW = NL + DH
ITERS = 6
EPS = 1e-5
PF = 192
E0 = 8
EH = 256
E1 = 4
ROOT = float(np.sqrt(ZL))

C_ID, C_CEN, C_AVG, C_AVP, C_D, C_NS, C_IOTA, C_EPS, C_EPS2, C_DV, C_KW, C_II, C_SEL = (
    0, 128, 192, 320, 448, 539, 571, 579, 580, 581, 582, 584, 648)
C_W = 648 + E0 // 2 * 128


def shape_constants():
    c = np.zeros((128, C_W), np.float32)
    c[:, C_ID:C_ID + 128] = np.eye(128)
    c[:D, C_CEN:C_CEN + D] = np.eye(D) - 1.0 / D
    c[:D, C_AVG:C_AVG + D] = 1.0 / D
    c[D:, C_AVG + D:C_AVG + 2 * D] = 1.0 / D
    c[:, C_AVP:C_AVP + 128] = 1.0 / PF
    c[:NL, C_D:C_D + NL] = 1.0
    c[0, C_D:C_D + NL] = ROOT
    c[:D, C_NS] = 1.0
    c[D:, C_NS + 1] = 1.0
    c[:, C_IOTA:C_IOTA + 8] = np.arange(8)
    c[:, C_EPS] = EPS
    c[:, C_EPS2] = EPS * EPS
    c[:, C_DV] = 1.0
    c[0, C_DV] = ROOT
    c[:, C_KW:C_KW + 2] = 1.0
    c[:NI, C_KW] = COPIES
    c[:D, C_II:C_II + D] = np.eye(D)
    c[D:, C_II:C_II + D] = np.eye(D)
    for e in range(E0):
        for row in (e, 32 + e):
            c[row, C_SEL + e * D:C_SEL + (e + 1) * D] = 1.0
    return c


V_B1, V_G2, V_B2, V_BP1, V_GP, V_BP, V_BP2, V_GA, V_BA, V_BO, V_LS, V_SB1 = range(12)
V_FG, V_FB = 12, 20
V_W = 28
W_P1, W_P2, W_QKV, W_R, W_G, W_S1, W_S2, W_E1, W_Q, W_K, W_VT, W_OT, W_F1 = (
    0, 64, 128, 896, 904, 908, 972, 1100, 1612, 2124, 2636, 3148, 3660)
W_W = 3660 + E0 * EH
M_Q, M_VT, M_OT, M_F1 = W_Q - W_E1, W_VT - W_E1, W_OT - W_E1, W_F1 - W_E1
Y_S1, Y_S2, Y_E1, Y_Q, Y_K, Y_F1, Y_VO = 0, 64, 192, 704, 1216, 1728, 1728 + E0 * EH
Y_W = Y_VO + H * D
X_B1, X_SB2, X_EB1, X_EB2, X_GAM, X_GAR, X_BR, X_GB, X_KD, X_S3, X_E2, X_E3, X_WVT, X_WO, X_F2, X_B2, X_SB3, X_EB3 = (
    0, 16, 17, 21, 23, 31, 33, 41, 45, 111, 175, 431, 687, 943, 1071, 2095, 2099, 2100)
X_W = 2102


LOOP1 = ["n_proj", "n_qk", "n_score", "n_max", "n_sub", "n_exp", "n_z", "n_e0", "n_a", "n_cs", "n_c1", "n_cm"]
LOOP2 = ["f_x", "f_xw", "f_as", "f_pq", "f_pk", "f_v", "f_s3", "f_s1", "f_t3", "f_w", "f_t1", "f_q", "f_ka", "f_kd",
         "f_vu", "f_m3", "f_nm3", "f_mm1", "f_sub1", "f_e3", "f_e1", "f_p3", "f_z3", "f_r3", "f_w0", "f_z1", "f_e10",
         "f_p1", "f_pt", "f_m0", "f_y0", "f_m1", "f_m2", "f_ta", "f_tx", "f_td", "f_st", "f_u", "f_o", "f_oo", "f_out",
         "f_hx", "f_res"]
LOOP3 = ["m_h", "m_g", "m_w", "m_wb", "m_y", "m_yw", "m_s"]
LOOP4 = ["d_x", "d_norm", "d_q2", "d_q", "d_k", "d_qa", "d_ka", "d_sq", "d_v", "d_vm", "d_s", "d_cl", "d_e", "d_pv", "d_half", "d_res"]
LOOP5 = ["g_l1", "g_s1", "g_h1", "g_l2", "g_s2", "g_h2", "g_gate", "g_gb", "g_l3", "g_yg", "g_ga", "g_hf", "g_fin", "g_os", "g_put"]


def program(nc, xpatch, txt, w1, ln1, vec, mat, wide, const, out):
    with ExitStack() as ctx:
        def sb(name, shape, dt=F32):
            return ctx.enter_context(nc.sbuf_tensor(name, shape, dt))

        sems = {}

        def sem(name):
            if name not in sems:
                sems[name] = nc.alloc_semaphore(name=name)
            return sems[name]

        def phase_over():
            done = [sems.pop(name) for name in list(sems) if name != "loaded"]
            nc.clear_and_free_semaphores(done)
            nc.all_engine_barrier()

        PS = ctx.enter_context(nc.psum_tensor("PS", [128, 8, 512], F32))
        CO = sb("CO", [128, C_W])
        VE = sb("VE", [128, V_W])
        MA = sb("MA", [128, W_E1])
        WI = sb("WI", [128, X_W])
        W1A = sb("W1A", [128, D])
        W1B = sb("W1B", [D, D])
        G1A = sb("G1A", [128, 2])
        G1B = sb("G1B", [D, 2])
        ident = CO[:, C_ID:C_ID + 128]
        NG = sb("NG", [128, H + 2])
        FB1 = sb("FB1", [128, 2 * E0])
        WU = sb("WU", [1, 1])
        WH = sb("WH", [128, Y_W], F32R)
        WL = sb("WL", [128, Y_W], F32R)
        SEL = sb("SEL", [128, E0 // 2 * 128], F32R)
        RC = sb("RC", [NL, 1])
        RCK = sb("RCK", [NL, 1])
        HT = sb("HT", [KP, B, NP])
        first = ExitStack()

        def fs(name, shape, dt=F32):
            return first.enter_context(nc.sbuf_tensor(name, shape, dt))

        TAP = fs("TAP", [128, HALO + 1, D])
        HU = fs("HU", [KP, B, U])
        XL = fs("XL", [D, B, U])
        HX = fs("HX", [D, B, U])
        XAP = fs("XAP", [KP, B, UL])
        XC = fs("XC", [128, B, CW])
        AA = fs("AA", [KP, B, H, NL])
        CM = fs("CM", [NL, B, H])

        s_load = sem("loaded")

        def col(t, c, p=128, n=1):
            return t[0:p, c:c + n]

        def at(i, n, k):
            return i * n + (k + 1)

        def started(eng, names):
            for name in names:
                eng.sem_inc(sem(name), 1)

        def nxt(i, o, n, k):
            return i * n + (o * n + k + 1)

        FREE = {"d_cl": 4, "d_e": 3, "d_pv": 3, "d_res": 1}

        def atb(name, i, o, n, k):
            return i * (2 * n) + (o * n + k + 1 + FREE.get(name, 0))

        def batches(eng, body):
            with eng.Fori(0, B // 2 - 1) as i:
                body(i, 0, True)
                body(i, 1, True)
            body(B // 2 - 1, 0, True)
            body(B // 2 - 1, 1, False)

        def warm(function):
            nc.scalar.activation(WU[:, :], CO[0:1, 0:1], function)

        def need(eng, *waits):
            for name, value in waits:
                eng.wait_ge(sem(name), value)
            eng.wait_ge(s_load, 16)

        def groups(width):
            n = -(-width // 128)
            size = -(-width // n)
            return size, [min(g * size, width - size) for g in range(n)]

        def ln_pe(pe, tag, src, ready, chunks, width, norms=1):
            size, firsts = groups(width)
            pairs, G = chunks // 2, len(firsts)
            pe.wait_ge(*ready)
            for c in range(chunks):
                o = c % 2 * D
                last = nc.tensor.matmul(PS[o:o + D, c // 2, 0:width], CO[0:KP, C_CEN:C_CEN + D], src(c),
                                        start=True, stop=True)
                if c % 2:
                    last.then_inc(sem(tag + "_centred"), 1)
            for p in range(pairs):
                pe.wait_ge(sem(tag + "_squared"), p + 1)
                for g, first in enumerate(firsts):
                    k = 2 * (p * G + g)
                    last = nc.tensor.matmul(PS[0:size, 4, k:k + 2], LSQ[:, p, first:first + size],
                                            CO[:, C_AVG:C_AVG + 2 * D:D], start=True, stop=True)
            last.then_inc(sem(tag + "_var"), 1)
            for n in range(norms):
                for p in range(pairs):
                    pe.wait_ge(sem(tag + "_widened"), n * pairs + p + 1)
                    if n:
                        pe.wait_ge(sem(tag + "_done"), 2 * ((n - 1) * pairs + p + 1))
                    for g, first in enumerate(firsts):
                        k = 2 * (p * G + g)
                        last = nc.tensor.matmul(
                            PS[:, 4 + p, first:first + size],
                            LSW[0:size, n, k:k + 2, :].rearrange("p a d -> p (a d)"),
                            ident[0:size, 0:size], start=True, stop=True)
                    last.then_inc(sem(tag + "_spread"), 1)

        def ln_act(act, tag, chunks, width, twice):
            size, firsts = groups(width)
            K = chunks * len(firsts)
            for p in range(chunks // 2):
                act.wait_ge(sem(tag + "_centred"), p + 1)
                nc.scalar.activation(LSQ[:, p, 0:width], PS[:, p, 0:width],
                                     ACT.Square).then_inc(sem(tag + "_squared"), 1)
            act.wait_ge(sem(tag + "_var"), 1)
            for n, t in enumerate(twice):
                nc.scalar.activation(LST[0:size, n, 0:K], PS[0:size, 4, 0:K],
                                     ACT.Sqrt, scale=1.0 + EPS if t else 1.0,
                                     bias=col(CO, C_EPS2 if t else C_EPS, size)).then_inc(sem(tag + "_rooted"), 1)
            act.wait_ge(sem(tag + "_inv"), 1)
            for n in range(len(twice)):
                for p in range(chunks // 2):
                    k = slice(2 * p * len(firsts), 2 * (p + 1) * len(firsts))
                    m = 2 * len(firsts)
                    nc.scalar.copy(LSW[0:size, n, k, :], LST[0:size, n, k].unsqueeze(2).broadcast_to([size, m, D])
                                   ).then_inc(sem(tag + "_widened"), 1)

        def ln_dve(dve, tag, chunks, width, outs):
            size, firsts = groups(width)
            pairs, k = chunks // 2, len(outs)
            for p in range(pairs):
                dve.wait_ge(sem(tag + "_squared"), p + 1)
                nc.vector.tensor_copy(LCE[:, p, 0:width], PS[:, p, 0:width]).then_inc(sem(tag + "_kept"), 1)
            dve.wait_ge(sem(tag + "_rooted"), k)
            roots = LST[0:size, 0:k, 0:chunks * len(firsts)]
            nc.vector.reciprocal(roots, roots).then_inc(sem(tag + "_inv"), 1)
            for n, dst in enumerate(outs):
                for p in range(pairs):
                    dve.wait_ge(sem(tag + "_spread"), n * pairs + p + 1)
                    if n == 0:
                        dve.wait_ge(sem(tag + "_kept"), p + 1)
                    for o in range(2):
                        half = slice(o * D, (o + 1) * D)
                        nc.vector.tensor_tensor(dst(2 * p + o), LCE[half, p, 0:width], PS[half, 4 + p, 0:width],
                                                ALU.mult).then_inc(sem(tag + "_done"), 1)

        def short_ln_pe(pe, tag, src, ready, chunks, width):
            pe.wait_ge(*ready)
            for c in range(chunks):
                o = c % 2 * D
                last = nc.tensor.matmul(PS[o:o + D, c // 2, 0:width], CO[0:KP, C_CEN:C_CEN + D], src(c),
                                        start=True, stop=True)
                if c % 2:
                    last.then_inc(sem(tag + "_centred"), 1)
            for p in range(chunks // 2):
                pe.wait_ge(sem(tag + "_squared"), p + 1)
                nc.tensor.matmul(PS[:, 4 + p, 0:width], CO[:, C_AVG:C_AVG + 128], LSQ[:, p, 0:width],
                                 start=True, stop=True).then_inc(sem(tag + "_var"), 1)

        def short_ln_act(act, tag, chunks, width, twice):
            for p in range(chunks // 2):
                act.wait_ge(sem(tag + "_centred"), p + 1)
                nc.scalar.activation(LSQ[:, p, 0:width], PS[:, p, 0:width],
                                     ACT.Square).then_inc(sem(tag + "_squared"), 1)
            for p in range(chunks // 2):
                act.wait_ge(sem(tag + "_var"), p + 1)
                for n, t in enumerate(twice):
                    nc.scalar.activation(LST[:, p, n, 0:width], PS[:, 4 + p, 0:width],
                                         ACT.Sqrt, scale=1.0 + EPS if t else 1.0,
                                         bias=col(CO, C_EPS2 if t else C_EPS)).then_inc(sem(tag + "_rooted"), 1)

        def short_ln_dve(dve, tag, chunks, width, outs):
            k = len(outs)
            for n, dst in enumerate(outs):
                for p in range(chunks // 2):
                    dve.wait_ge(sem(tag + "_rooted"), p * k + n + 1)
                    nc.vector.reciprocal(LST[:, p, n, 0:width],
                                         LST[:, p, n, 0:width]).then_inc(sem(tag + "_inv"), 1)
                    dve.wait_ge(sem(tag + "_inv"), n * (chunks // 2) + p + 1)
                    for o in range(2):
                        half = slice(o * D, (o + 1) * D)
                        nc.vector.tensor_tensor(dst(2 * p + o), PS[half, p, 0:width], LST[half, p, n, 0:width],
                                                ALU.mult).then_inc(sem(tag + "_done"), 1)

        S = ExitStack()

        def ts(name, shape, dt=F32):
            return S.enter_context(nc.sbuf_tensor(name, shape, dt))

        XA0 = ts("XA0", [128, 512])
        XA1 = ts("XA1", [D, 512])
        XC0 = ts("XC0", [128, 512])
        XC1 = ts("XC1", [D, 512])
        XQ0 = ts("XQ0", [128, 512])
        XQ1 = ts("XQ1", [D, 512])
        XS = ts("XS", [128, 512])
        TK = ts("TK", [KP, 512])
        TN = ts("TN", [D, 512])
        MB = ts("MB", [128, W_W - W_E1])
        MF = ts("MF", [128, E0 * EH])
        WVO = ts("WVO", [128, H, D])
        LSQ = ts("LSQ", [128, 2, 2 * U])
        LST = ts("LST", [128, 2, 2, 2 * U])
        WOK = ts("WOK", [128, 2, (TAPS + 1) * D])
        TS = B * NI
        assert TS == 512

        def half_tk(c):
            return TK[:, c * TS // 2:(c + 1) * TS // 2]

        FILL_HU, FILL_XC = 3, 4
        TAP_BANKS = (6, 7, 2)
        with nc.Block() as block:
            @block.sync
            def _(sp):
                sp.dma_start(XA0[:, :], xpatch[0:128, :]).then_inc(sem("patches"), 16)
                sp.dma_start(XA1[:, :], xpatch[128:PF, :]).then_inc(sem("patches"), 16)
                sp.dma_start(CO[:, 0:C_SEL], const[:, 0:C_SEL]).then_inc(sem("patches"), 16)
                sp.dma_start(G1A[:, :], ln1[0:128, :]).then_inc(s_load, 16)
                sp.dma_start(G1B[:, :], ln1[128:PF, :]).then_inc(s_load, 16)
                sp.dma_start(W1A[:, :], w1[0:128, :]).then_inc(s_load, 16)
                sp.dma_start(W1B[:, :], w1[128:PF, :]).then_inc(s_load, 16)
                sp.dma_start(VE[:, :], vec).then_inc(s_load, 16)
                sp.dma_start(CO[:, C_SEL:C_W], const[:, C_SEL:C_W]).then_inc(s_load, 16)
                sp.dma_start(HU[0:D, :, NI:NI + NX], txt.rearrange("f (b n) -> f b n", b=B)).then_inc(s_load, 16)
                sp.wait_ge(sem("seq_built"), 2)
                flat = XC[:, :, :].rearrange("p b w -> p (b w)")
                sp.dma_start(flat[D:128, 0:B * CW - 1], flat[0:D, 1:B * CW]).then_inc(sem("seq_shift"), 16)
                sp.wait_ge(sem("seq_shift"), 16)

            @block.scalar
            def _(act):
                act.wait_ge(sem("patches"), 48)
                act.dma_start(WI[:, :], wide).then_inc(sem("wides"), 16)
                act.dma_start(MA[:, :], mat[:, 0:W_E1]).then_inc(sem("mats"), 16)
                act.dma_start(MB[:, :], mat[:, W_E1:W_W]).then_inc(sem("more_mats"), 16)
                act.wait_ge(sem("p_cent"), 2)
                nc.scalar.activation(XQ0[:, :], XC0[:, :], ACT.Square)
                nc.scalar.activation(XQ1[:, :], XC1[:, :], ACT.Square).then_inc(sem("p_sq"), 1)
                act.wait_ge(sem("p_var"), 1)
                nc.scalar.activation(XS[:, :], PS[:, 1, :], ACT.Sqrt, bias=col(CO, C_EPS)).then_inc(sem("p_std"), 1)
                short_ln_act(act, "t2", 2, TS // 2, [False])
                short_ln_act(act, "tp", 2, TS // 2, [False])
                act.wait_ge(sem("tp_aff"), 1)
                nc.scalar.activation(TN[:, :], XA1[:, :], ACT.Silu).then_inc(sem("silu"), 1)
                short_ln_act(act, "a", 4, 2 * U, [False, True])
                act.wait_ge(sem("wvo_mm"), 1)
                nc.scalar.mul(WVO[:, :, :], PS[:, 5, :].rearrange("p (h o) -> p h o", h=H),
                              VE[:, V_LS:V_LS + 1]).then_inc(sem("wvo"), 1)
                for c in range(5):
                    act.wait_ge(sem("tap_mm"), c + 1)
                    k = 8 if c < 4 else 2
                    src = PS[:, TAP_BANKS[c % 3], 0:k * D].rearrange("p (j e o) -> p j e o", e=2, o=D)
                    nc.scalar.copy(TAP[0:D, 4 * c:4 * c + k // 2, :], src[0:D, :, 0, :])
                    nc.scalar.copy(TAP[D:128, 4 * c:4 * c + k // 2, :],
                                   src[D:128, :, 1, :]).then_inc(sem("tap_out"), 1)
                act.wait_ge(sem("pool_raw"), 2)
                nc.scalar.mul(XAP[0:D, :, U + 1:U + NL], XAP[0:D, :, U + 1:U + NL], 1.0 / GRP).then_inc(sem("pooled"), 1)

            @block.gpsimd
            def _(pool):
                for k, pad in enumerate((TK[D:KP, :], HU[D:KP, :, :], HU[0:D, :, U - 1:U], XC[:, :, :],
                                         XAP[D:KP, :, :], XAP[0:D, :, U - 1:U + 1], XAP[0:D, :, U + NL:UL],
                                         AA[D:KP, :, :, :], HT[0:D, :, N:NP], HT[D:KP, :, :],
                                         WOK[:, :, TAPS * D:])):
                    nc.gpsimd.memset(pad, 0.0).then_inc(sem("zeroed"), 1)
                    pool.wait_ge(sem("zeroed"), k + 1)
                pool.wait_ge(sem("wides"), 16)
                for t in range(2):
                    wo = WI[:, X_WO + t * D:X_WO + (t + 1) * D].unsqueeze(1).broadcast_to([128, TAPS, D])
                    kd = WI[:, X_KD + t * TAPS:X_KD + (t + 1) * TAPS].unsqueeze(2).broadcast_to([128, TAPS, D])
                    nc.gpsimd.tensor_tensor(WOK[:, t, 0:TAPS * D].rearrange("p (k o) -> p k o", o=D),
                                            wo, kd, ALU.mult).then_inc(sem("wok"), 1)
                pool.wait_ge(sem("mats"), 16)
                pool.wait_ge(sem("more_mats"), 16)
                pool.wait_ge(s_load, 16 * 7)
                nc.gpsimd.tensor_copy(SEL[:, :], CO[:, C_SEL:C_SEL + E0 // 2 * 128])
                for o in range(0, 2 * E0, 4):
                    nc.gpsimd.tensor_tensor(MF[:, o * 128:(o + 4) * 128].rearrange("p (e n) -> p e n", e=2),
                                            MB[:, M_F1 + o * 128:M_F1 + (o + 4) * 128].rearrange("p (e n) -> p e n", e=2), VE[:, V_FG + o // 2:V_FG + o // 2 + 2].unsqueeze(2)
                                            .broadcast_to([128, 2, EH]), ALU.mult)
                nc.gpsimd.tensor_scalar(MB[:, M_Q:M_Q + 2 * H * D], MB[:, M_Q:M_Q + 2 * H * D],
                                        VE[:, V_LS:V_LS + 1], None, ALU.mult).then_inc(sem("wqk"), 1)
                for k, (y, w, n) in enumerate(((Y_S1, MA[:, W_S1:W_E1], Y_E1), (Y_E1, MB[:, 0:Y_F1 - Y_E1], Y_F1 - Y_E1),
                                               (Y_F1, MF[:, :], E0 * EH))):
                    pool.wait_ge(sem("wqk"), 1 + k)
                    nc.gpsimd.tensor_copy(WH[:, y:y + n], w).then_inc(sem("w_high"), 1)
                    pool.wait_ge(sem("w_high"), k + 1)
                    nc.gpsimd.tensor_tensor(WL[:, y:y + n], w, WH[:, y:y + n], ALU.subtract
                                            ).then_inc(sem("wqk"), 1)
                pool.wait_ge(sem("wvo"), 1)
                wvo = WVO[:, :, :].rearrange("p h o -> p (h o)")
                nc.gpsimd.tensor_copy(WH[:, Y_VO:Y_W], wvo).then_inc(sem("w_high"), 1)
                pool.wait_ge(sem("w_high"), 4)
                nc.gpsimd.tensor_tensor(WL[:, Y_VO:Y_W], wvo, WH[:, Y_VO:Y_W], ALU.subtract).then_inc(sem("wqk"), 1)

            @block.tensor
            def _(pe):
                pe.wait_ge(sem("patches"), 48)
                avp = CO[:, C_AVP:C_AVP + 128]
                nc.tensor.matmul(PS[:, 0, :], avp, XA0[:, :], start=True, stop=False)
                nc.tensor.matmul(PS[:, 0, :], avp[0:D, :], XA1[:, :], start=False, stop=True).then_inc(sem("p_mean"), 1)
                pe.wait_ge(sem("p_sq"), 1)
                nc.tensor.matmul(PS[:, 1, :], avp, XQ0[:, :], start=True, stop=False)
                nc.tensor.matmul(PS[:, 1, :], avp[0:D, :], XQ1[:, :], start=False, stop=True).then_inc(sem("p_var"), 1)
                pe.wait_ge(sem("p_aff"), 2)
                pe.wait_ge(s_load, 16 * 7)
                nc.tensor.matmul(PS[0:D, 2, :], W1A[:, :], XC0[:, :], start=True, stop=False)
                nc.tensor.matmul(PS[0:D, 2, :], W1B[:, :], XC1[:, :], start=False, stop=True).then_inc(sem("tok1"), 1)
                pe.wait_ge(sem("zeroed"), FILL_HU)
                short_ln_pe(pe, "t2", half_tk, (sem("tok1_b"), 1), 2, TS // 2)
                pe.wait_ge(sem("t2_aff"), 1)
                pe.wait_ge(sem("mats"), 16)
                nc.tensor.matmul(PS[0:D, 3, :], MA[0:D, W_P1:W_P1 + D], TN[:, :], start=True, stop=True).then_inc(sem("tok2"), 1)
                short_ln_pe(pe, "tp", half_tk, (sem("tok2_b"), 1), 2, TS // 2)
                pe.wait_ge(sem("silu"), 1)
                nc.tensor.matmul(PS[0:D, 4, :], MA[0:D, W_P2:W_P2 + D], TN[:, :], start=True, stop=True).then_inc(sem("tok3"), 1)
                short_ln_pe(pe, "a", lambda c: HU[:, 2 * c:2 * c + 2, :].rearrange("p b n -> p (b n)"), (sem("stream"), 1), 4, 2 * U)
                pe.wait_ge(sem("a_rooted"), 4)
                pe.wait_ge(sem("more_mats"), 16)
                for h in range(H):
                    for o in range(2):
                        last = nc.tensor.matmul(PS[o * D:(o + 1) * D, 5, h * D:(h + 1) * D],
                                                MB[0:D, M_VT + h * D:M_VT + (h + 1) * D],
                                                MB[0:D, M_OT + h * D:M_OT + (h + 1) * D], start=True, stop=True)
                last.then_inc(sem("wvo_mm"), 1)
                pe.wait_ge(sem("wok"), 2)
                for c in range(5):
                    w = 512 if c < 4 else 2 * D
                    if c >= 3:
                        pe.wait_ge(sem("tap_out"), c - 2)
                    for t in range(2):
                        last = nc.tensor.matmul(PS[:, TAP_BANKS[c % 3], 0:w], WI[:, X_WVT + t * 128:X_WVT + (t + 1) * 128],
                                                WOK[:, t, c * 512:c * 512 + w], start=t == 0, stop=t == 1)
                    last.then_inc(sem("tap_mm"), 1)
                for j in range(2 * E0):
                    last = nc.tensor.matmul(PS[:, 3, j:j + 1], MB[0:D, M_F1 + j * 128:M_F1 + (j + 1) * 128],
                                            VE[0:D, V_FB + j // 2:V_FB + j // 2 + 1], start=True, stop=True)
                last.then_inc(sem("fb1_mm"), 1)

            @block.vector
            def _(dve):
                v = nc.vector
                dve.wait_ge(sem("p_mean"), 1)
                v.tensor_tensor(XC0[:, :], XA0[:, :], PS[:, 0, :], ALU.subtract).then_inc(sem("p_cent"), 1)
                v.tensor_tensor(XC1[:, :], XA1[:, :], PS[0:D, 0, :], ALU.subtract).then_inc(sem("p_cent"), 1)
                dve.wait_ge(sem("p_std"), 1)
                v.reciprocal(XQ0[:, :], XS[:, :]).then_inc(sem("p_rstd"), 1)
                dve.wait_ge(sem("p_rstd"), 1)
                v.tensor_tensor(XA0[:, :], XC0[:, :], XQ0[:, :], ALU.mult).then_inc(sem("p_norm"), 1)
                v.tensor_tensor(XA1[:, :], XC1[:, :], XQ0[0:D, :], ALU.mult).then_inc(sem("p_norm"), 1)
                dve.wait_ge(sem("p_norm"), 2)
                dve.wait_ge(s_load, 16 * 7)
                v.tensor_scalar(XC0[:, :], XA0[:, :], G1A[:, 0:1], G1A[:, 1:2], ALU.mult, ALU.add).then_inc(sem("p_aff"), 1)
                v.tensor_scalar(XC1[:, :], XA1[:, :], G1B[:, 0:1], G1B[:, 1:2], ALU.mult, ALU.add).then_inc(sem("p_aff"), 1)
                dve.wait_ge(sem("tok1"), 1)
                v.tensor_scalar(TK[0:D, :], PS[0:D, 2, :], VE[0:D, V_B1:V_B1 + 1], None, ALU.add).then_inc(sem("tok1_b"), 1)
                short_ln_dve(dve, "t2", 2, TS // 2, [lambda c: TN[:, c * TS // 2:(c + 1) * TS // 2]])
                dve.wait_ge(sem("t2_done"), 2)
                v.tensor_scalar(TN[:, :], TN[:, :], VE[0:D, V_G2:V_G2 + 1], VE[0:D, V_B2:V_B2 + 1], ALU.mult, ALU.add
                                ).then_inc(sem("t2_aff"), 1)
                dve.wait_ge(sem("tok2"), 1)
                v.tensor_scalar(TK[0:D, :], PS[0:D, 3, :], VE[0:D, V_BP1:V_BP1 + 1], None, ALU.add).then_inc(sem("tok2_b"), 1)
                short_ln_dve(dve, "tp", 2, TS // 2, [lambda c: TN[:, c * TS // 2:(c + 1) * TS // 2]])
                dve.wait_ge(sem("tp_done"), 2)
                v.tensor_scalar(XA1[:, :], TN[:, :], VE[0:D, V_GP:V_GP + 1], VE[0:D, V_BP:V_BP + 1], ALU.mult, ALU.add
                                ).then_inc(sem("tp_aff"), 1)
                dve.wait_ge(sem("tok3"), 1)
                dve.wait_ge(sem("zeroed"), FILL_HU)
                v.tensor_scalar(HU[0:D, :, 0:NI], PS[0:D, 4, :].rearrange("p (b n) -> p b n", b=B),
                                VE[0:D, V_BP2:V_BP2 + 1], None, ALU.add).then_inc(sem("stream"), 1)
                flat = lambda t, c: t[:, 2 * c:2 * c + 2, :].rearrange("p b n -> p (b n)")
                short_ln_dve(dve, "a", 4, 2 * U, [lambda c: flat(XL, c), lambda c: flat(HX, c)])
                dve.wait_ge(sem("a_done"), 8)
                v.tensor_scalar(XAP[0:D, :, 0:U - 1], HX[:, :, 0:U - 1], VE[0:D, V_GA:V_GA + 1], VE[0:D, V_BA:V_BA + 1],
                                ALU.mult, ALU.add).then_inc(sem("a_in"), 1)
                dve.wait_ge(sem("a_in"), 1)
                dve.wait_ge(sem("zeroed"), FILL_XC)
                v.tensor_copy(XC[0:D, :, HALO:HALO + COPIES * NI].rearrange("p b (r n) -> p b r n", r=COPIES),
                              XAP[0:D, :, 0:NI].unsqueeze(2).broadcast_to([D, B, COPIES, NI])).then_inc(sem("seq_built"), 1)
                v.tensor_copy(XC[0:D, :, HALO + COPIES * NI:HALO + N], XAP[0:D, :, NI:NI + NX]).then_inc(sem("seq_built"), 1)
                dve.wait_ge(sem("seq_built"), 2)
                first = GRP - PAD % GRP
                v.tensor_reduce(XAP[0:D, :, U + 1:U + 2], XC[0:D, :, HALO:HALO + first], AX.X, ALU.add
                                ).then_inc(sem("pool_raw"), 1)
                v.tensor_reduce(XAP[0:D, :, U + 2:U + NL],
                                XC[0:D, :, HALO + first:HALO + N].rearrange("p b (j t) -> p b j t", t=GRP),
                                AX.X, ALU.add).then_inc(sem("pool_raw"), 1)
                v.scalar_tensor_tensor(out=HX[:, :, :], in0=HU[0:D, :, :], scalar=VE[0:D, V_BO:V_BO + 1], in1=XL[:, :, :],
                                       op0=ALU.add, op1=ALU.add).then_inc(sem("resid"), 1)
                dve.wait_ge(sem("fb1_mm"), 1)
                dve.wait_ge(sem("wides"), 16)
                v.tensor_scalar(NG[:, :], WI[:, X_GAM:X_GAM + H + 2], -1.0, None, ALU.mult)
                v.tensor_tensor(FB1[:, :], PS[:, 3, 0:2 * E0], WI[:, X_B1:X_B1 + 2 * E0], ALU.add).then_inc(sem("fb1"), 1)
        phase_over()
        S.close()


        S = ExitStack()
        XS = ts("XS_", [KP, UL])
        XW = ts("XW", [128, CW])
        QM = ts("QM", [128, 2, UL])
        KM = ts("KM", [128, 2, 4, UL])
        VU = ts("VU", [KP, 2, H * DH])
        AS = ts("AS", [KP, 2, H, SW])
        M3 = ts("M3", [NL, H])
        E3 = ts("E3", [KP, H, U])
        Z3 = ts("Z3", [NL, 4, H])
        P3 = ts("P3", [KP, H, 2, KP])
        M1 = ts("M1", [UT, 4, 4])
        E1_ = ts("E1_", [UT, H, 2, NL])
        P1 = ts("P1", [KP, 2 * H, NL])
        Z1 = ts("Z1", [UT, 3, 2 * H])
        PT = ts("PT", [KP, 2, H, U])
        ST = ts("ST", [KP, H, SW])
        TA = ts("TA", [KP, H, SW])
        TX = ts("TX", [KP, H, SW])
        TD = ts("TD", [NL, H, SW])
        UU = ts("UU", [KP, H, DH])
        OO = ts("OO", [128, 2, U])
        pads = [AS[D:KP, :, :, :]] + [x[D:KP, :, :] for x in (E3, P1, ST, TA, TX, UU)] + [
            P3[D:KP, :, :, :], VU[D:KP, :, :], PT[D:KP, :, :, :], KM[:, :, :, :]]

        short = ExitStack()

        def ss(name, shape):
            return short.enter_context(nc.sbuf_tensor(name, shape, F32))

        QL = ss("QL", [128, 4, KP])
        DD = ss("DD", [NL, H, NL])
        EE = ss("EE", [NL, H, NL])
        MX = ss("MX", [NL, H])
        MX2 = ss("MX2", [NL, 2, H])
        ZZ = ss("ZZ", [NL, 4, H])
        with nc.Block() as block:
            @block.sync
            def _(sp):
                started(sp, LOOP1)
                sp.sem_inc(sem("n_cm"), 1)
                sp.sem_inc(sem("n_started"), 1)

            @block.gpsimd
            def _(pool):
                for k, pad in enumerate(pads):
                    nc.gpsimd.memset(pad, 0.0).then_inc(sem("n_pad"), 1)
                    pool.wait_ge(sem("n_pad"), k + 1)

            @block.tensor
            def _(pe):
                def proj(i, o):
                    need(pe, ("n_qk", nxt(i, o, 1, 0)))
                    for j in range(4):
                        last = nc.tensor.matmul(PS[:, 0, j * KP:(j + 1) * KP],
                                                MA[0:KP, W_QKV + j * 128:W_QKV + (j + 1) * 128],
                                                XAP[:, bass.ds(i + o, 1), U:UL].rearrange("p a n -> p (a n)"),
                                                start=True, stop=True)
                    last.then_inc(sem("n_proj"), 1)

                def scores(i):
                    need(pe, ("n_qk", at(i, 1, 1)), ("n_sub", at(i, 1, 0)))
                    for h in range(H):
                        r, hh = h % 4, h // 4
                        last = nc.tensor.matmul(PS[0:KP, 1 + r, hh * KP:(hh + 1) * KP],
                                                QL[32 * r:32 * r + 32, hh, :], QL[32 * r:32 * r + 32, 2 + hh, :],
                                                start=True, stop=True)
                    last.then_inc(sem("n_score"), 1)

                pe.wait_ge(sem("n_started"), 1)
                proj(0, 0)
                with pe.Fori(0, B - 1) as i:
                    scores(i)
                    proj(i, 1)
                scores(B - 1)
                pe.wait_ge(sem("n_sub"), B + 1)
                with pe.Fori(0, B // 2) as i:
                    for o in range(2):
                        need(pe, ("n_a", i * 2 + (o + 2)), ("n_cm", at(i, 2, o)))
                        for q in range(2):
                            last = nc.tensor.matmul(PS[0:NL, 4 + 2 * o + q, 0:4 * NL], CO[0:KP, C_D:C_D + NL],
                                                    AA[:, bass.ds(i * 2 + o, 1), 4 * q:4 * q + 4, :].rearrange("p a h n -> p (a h n)"),
                                                    start=True, stop=True)
                        last.then_inc(sem("n_cs"), 1)

            @block.scalar
            def _(act):
                warm(ACT.Exp)
                def copied(i, o):
                    need(act, ("n_proj", nxt(i, o, 1, 1)))
                    nc.scalar.copy(QL[:, :, :], PS[:, 0, 0:4 * KP].rearrange("p (j n) -> p j n", j=4)
                                   ).then_inc(sem("n_qk"), 1)

                def exps(i):
                    need(act, ("n_sub", at(i, 1, 1)), ("n_a", at(i, 1, 0)))
                    nc.scalar.activation(EE[:, :, :], DD[:, :, :], ACT.Exp, scale=SC).then_inc(sem("n_exp"), 1)

                act.wait_ge(sem("n_started"), 1)
                copied(0, 0)
                with act.Fori(0, B - 1) as i:
                    copied(i, 1)
                    exps(i)
                exps(B - 1)

            @block.vector
            def _(dve):
                v = nc.vector
                score = PS[0:NL, 1:5, 0:2 * KP].rearrange("p r (k n) -> p r k n", k=2)[:, :, :, 0:NL]
                with dve.Fori(0, B) as i:
                    need(dve, ("n_score", at(i, 1, 1)))
                    v.tensor_reduce(MX[:, :].rearrange("p (k r) -> p r k", k=2), score, AX.X, ALU.max
                                    ).then_inc(sem("n_max"), 1)
                    need(dve, ("n_max", at(i, 1, 1)), ("n_exp", at(i, 1, 0)))
                    v.tensor_tensor(DD[:, :, :].rearrange("p (k r) n -> p r k n", k=2), score,
                                    MX[:, :].rearrange("p (k r) -> p r k", k=2).unsqueeze(3).broadcast_to([NL, 4, 2, NL]),
                                    ALU.subtract).then_inc(sem("n_sub"), 1)
                    need(dve, ("n_exp", at(i, 1, 1)))
                    v.tensor_reduce(ZZ[:, 0, :], EE[:, :, :], AX.X, ALU.add).then_inc(sem("n_z"), 1)
                    need(dve, ("n_z", at(i, 4, 1)))
                    v.scalar_tensor_tensor(out=ZZ[:, 1, :], in0=EE[:, :, 0], scalar=float(ZL - 1), in1=ZZ[:, 0, :],
                                           op0=ALU.mult, op1=ALU.add).then_inc(sem("n_z"), 1)
                    need(dve, ("n_z", at(i, 4, 2)))
                    v.reciprocal(ZZ[:, 2, :], ZZ[:, 1, :]).then_inc(sem("n_z"), 1)
                    v.tensor_scalar(EE[:, :, 0], EE[:, :, 0], ROOT, None, ALU.mult).then_inc(sem("n_e0"), 1)
                    need(dve, ("n_z", at(i, 4, 3)))
                    v.tensor_scalar(ZZ[:, 3, :], ZZ[:, 2, :], CO[0:NL, C_DV:C_DV + 1], None, ALU.mult
                                    ).then_inc(sem("n_z"), 1)
                    need(dve, ("n_z", at(i, 4, 4)), ("n_e0", at(i, 1, 1)))
                    v.tensor_tensor(AA[0:NL, i, :, :], EE[:, :, :], ZZ[:, 3, :].unsqueeze(2).broadcast_to([NL, H, NL]),
                                    ALU.mult).then_inc(sem("n_a"), 1)
                with dve.Fori(0, B // 2) as i:
                    for o in range(2):
                        need(dve, ("n_cs", at(i, 2, o + 1)))
                        sums = PS[0:NL, 4 + 2 * o:6 + 2 * o, 0:4 * NL].rearrange("p q (k n) -> p q k n", k=4)
                        top = MX2[:, o, :].rearrange("p (q k) -> p q k", k=4)
                        v.tensor_reduce(top, sums[:, :, :, 1:NL], AX.X, ALU.max).then_inc(sem("n_c1"), 1)
                        need(dve, ("n_c1", at(i, 2, o + 1)))
                        v.scalar_tensor_tensor(out=CM[:, bass.ds(i * 2 + o, 1), :].rearrange("p a (q k) -> p q (a k)", k=4),
                                               in0=sums[:, :, :, 0], scalar=1.0 / ROOT, in1=top,
                                               op0=ALU.mult, op1=ALU.max).then_inc(sem("n_cm"), 1)
                dve.wait_ge(sem("n_cm"), B + 2)
                v.tensor_reduce(MX2[:, 0, 0:1], CM[:, :, :], AX.XY, ALU.max).then_inc(sem("n_top"), 1)
                dve.wait_ge(sem("n_top"), 1)
                v.reciprocal(RC[:, :], MX2[:, 0, 0:1]).then_inc(sem("n_rc"), 1)
                dve.wait_ge(sem("n_rc"), 1)
                v.tensor_scalar(RCK[:, :], RC[:, :], (13.0 / 4.0) ** ITERS, None, ALU.mult)
        phase_over()
        short.close()

        HALVES = 2 * ITERS
        TAPS_AT = (0, 3, 2, 2, 1, 1, 1, 1, 0, 4, 0, 2)
        assert sum(TAPS_AT) == HALO + 1
        heads4 = lambda x: x.rearrange("p (g n) -> p g n", g=4)
        SMALL = slice(NL, SW)
        with nc.Block() as block:
            @block.sync
            def _(sp):
                started(sp, LOOP2)
                sp.sem_inc(sem("f_started"), 1)

            @block.tensor
            def _(pe):
                def front(i, o, k):
                    a = o % 2
                    if k == 0:
                        need(pe, ("f_x", atb("f_x", i, o, 1, 1)), ("f_pt", atb("f_pt", i, o, 3, 0)))
                        for j in range(4):
                            last = nc.tensor.matmul(PS[:, j // 2, (j % 2) * UL:(j % 2 + 1) * UL],
                                                    MA[0:KP, W_QKV + j * 128:W_QKV + (j + 1) * 128],
                                                    XS[:, :], start=True, stop=True)
                            if j % 2:
                                last.then_inc(sem("f_pk" if j == 3 else "f_pq"), 1)
                    elif k == 1:
                        need(pe, ("f_x", atb("f_x", i, o, 1, 1)))
                        for t in range(2):
                            last = nc.tensor.matmul(PS[0:UT, 2, t * 256:(t + 1) * 256], XS[:, t * UT:(t + 1) * UT],
                                                    MA[0:KP, W_QKV + 512:W_QKV + 768], start=True, stop=True)
                        last.then_inc(sem("f_v"), 1)
                    elif k in (2, 3):
                        for u in (2 * k - 4, 2 * k - 3):
                            if u == 0:
                                need(pe, ("f_q", atb("f_q", i, o, 1, 1)), ("f_ka", atb("f_ka", i, o, 1, 1)),
                                     ("f_kd", atb("f_kd", i, o, 1, 1)))
                            elif u == 2:
                                need(pe, ("f_vu", atb("f_vu", i, o, 1, 1)))
                            elif u == 3:
                                need(pe, ("f_e3", atb("f_e3", i, o, 4, 1)))
                            nc.tensor.matmul(PS[0:KP, u % 3, 0:2 * U].rearrange("p (g n) -> p g n", g=2),
                                             QM[:, u // 2, U:UL], KM[:, u // 2, u % 2 * 2:u % 2 * 2 + 2, 0:U],
                                             start=True, stop=True).then_inc(sem("f_s3"), 1)
                    elif k in (4, 5):
                        for u in (2 * k - 8, 2 * k - 7):
                            if u < 3:
                                need(pe, ("f_e3", atb("f_e3", i, o, 4, u + 2)))
                            else:
                                need(pe, ("f_sub1", atb("f_sub1", i, o, 4, 1)))
                            nc.tensor.matmul(PS[0:UT, (u + 1) % 3, 0:4 * KP].rearrange("p (g n) -> p g n", g=4),
                                             QM[:, u // 2, u % 2 * UT:(u % 2 + 1) * UT], KM[:, u // 2, :, U:UL],
                                             start=True, stop=True).then_inc(sem("f_s1"), 1)
                    elif k in (6, 7):
                        for u in (2 * k - 12, 2 * k - 11):
                            if u < 3:
                                need(pe, ("f_sub1", atb("f_sub1", i, o, 4, u + 2)))
                            else:
                                need(pe, ("f_p3", atb("f_p3", i, o, 4, 1)))
                            for g in range(2):
                                for t in range(2):
                                    c = (2 * g + t) * KP
                                    last = nc.tensor.transpose(PS[0:UT, (u + 2) % 3, c:c + KP],
                                                               E3[:, 2 * u + g, t * UT:(t + 1) * UT], ident[0:KP, 0:KP])
                            last.then_inc(sem("f_t3"), 1)
                    elif k == 8:
                        need(pe, ("f_p3", atb("f_p3", i, o, 4, 4)))
                        for h in range(H):
                            for t in range(2):
                                last = nc.tensor.matmul(PS[0:NL, 0, h * DH:(h + 1) * DH], P3[:, h, t, 0:NL],
                                                        VU[:, t, h * DH:(h + 1) * DH], start=t == 0, stop=t == 1)
                        last.then_inc(sem("f_w"), 1)
                    elif k in (10, 11):
                        for u in ((0, 1) if k == 10 else (2,)):
                            if u == 0:
                                need(pe, ("f_p1", atb("f_p1", i, o, 1, 1)))
                            elif u == 2:
                                need(pe, ("f_w0", atb("f_w0", i, o, 1, 1)))
                            for h in range(3 * u, min(3 * u + 3, H)):
                                for t in range(2):
                                    c = h % 3 * U + t * UT
                                    last = nc.tensor.transpose(PS[0:NL, (u + 1) % 3, c:c + KP], P1[:, 2 * h + t, :],
                                                               ident[0:KP, 0:KP])
                            last.then_inc(sem("f_t1"), 1)

                def taps(j0, j1):
                    for j in range(j0, j1):
                        c = j % 2 * D
                        nc.tensor.matmul(PS[c:c + D, 3, 0:NP], TAP[:, j, :], XW[:, 2 * j:2 * j + NP],
                                         start=j < 2, stop=j == HALO - 1, skip_group_check=True)

                def start(i, o):
                    a = o % 2
                    need(pe, ("f_as", atb("f_as", i, o, 1, 1)), ("f_w0", atb("f_w0", i, o, 1, 1)))
                    for q in range(2):
                        for h in range(4 * q, 4 * q + 4):
                            last = nc.tensor.matmul(PS[0:NL, 4 + q, (h % 4) * SW:(h % 4 + 1) * SW],
                                                    AS[:, a, h, 0:NL], AS[:, a, h, :], start=True, stop=True)
                        last.then_inc(sem("f_m0"), 1)

                def body(i, o, ahead):
                    j = 0
                    for it in range(ITERS):
                        for n in range(2):
                            for q in range(2):
                                c0 = NL if n and it == ITERS - 1 else 0
                                if n:
                                    need(pe, ("f_ta", atb("f_ta", i, o, HALVES, 2 * it + q + 1)),
                                         ("f_tx", atb("f_tx", i, o, HALVES, 2 * it + q + 1)))
                                elif it:
                                    need(pe, ("f_st", atb("f_st", i, o, HALVES, 2 * it - 1 + q)))
                                else:
                                    need(pe, ("f_y0", atb("f_y0", i, o, 2, q + 1)))
                                x, y = (TA, TX) if n else (ST, ST)
                                for h in range(4 * q, 4 * q + 4):
                                    last = nc.tensor.matmul(PS[0:NL, 4 + 2 * n + q, (h % 4) * SW + c0:(h % 4 + 1) * SW],
                                                            x[:, h, 0:NL], y[:, h, c0:SW], start=True, stop=True)
                                last.then_inc(sem("f_m2" if n else "f_m1"), 1)
                            k = 2 * it + n
                            if ahead:
                                front(i, o + 1, k)
                            if TAPS_AT[k]:
                                if j == 0:
                                    need(pe, ("f_xw", atb("f_xw", i, o, 1, 1)), ("f_res", atb("f_res", i, o, 1, 0)))
                                taps(j, j + TAPS_AT[k])
                                j += TAPS_AT[k]
                    if ahead:
                        start(i, o + 1)
                    need(pe, ("f_u", atb("f_u", i, o, 1, 1)), ("f_pt", atb("f_pt", i, o, 3, 3)))
                    for h in range(H):
                        r, hh = h % 4, h // 4
                        last = nc.tensor.matmul(PS[32 * r:32 * r + 32, 6, hh * U:(hh + 1) * U], UU[:, h, :], PT[:, o, h, :],
                                                start=True, stop=True)
                    last.then_inc(sem("f_o"), 1)
                    need(pe, ("f_oo", atb("f_oo", i, o, 1, 1)))
                    for t in range(2):
                        wo = WI[:, X_WO + t * D:X_WO + (t + 1) * D]
                        nc.tensor.matmul(PS[0:D, 3, 0:COPIES * NI], wo,
                                         OO[:, t, 0:NI].unsqueeze(1).broadcast_to([128, COPIES, NI]),
                                         start=False, stop=False, skip_group_check=True)
                        last = nc.tensor.matmul(PS[0:D, 3, COPIES * NI:N], wo, OO[:, t, NI:NI + NX],
                                                start=False, stop=t == 1, skip_group_check=True)
                    last.then_inc(sem("f_out"), 1)

                pe.wait_ge(sem("f_started"), 1)
                for k in range(HALVES):
                    front(0, 0, k)
                start(0, 0)
                batches(pe, body)

            @block.scalar
            def _(act):
                def front(i, o, k):
                    a = o % 2
                    if k == 0:
                        need(act, ("f_pq", atb("f_pq", i, o, 1, 1)))
                        nc.scalar.copy(QM[:, :, :], PS[:, 0, 0:2 * UL].rearrange("p (j n) -> p j n", j=2)
                                       ).then_inc(sem("f_q"), 1)
                        need(act, ("f_pk", atb("f_pk", i, o, 1, 1)))
                        for r in (2, 3):
                            rows = slice(32 * r, 32 * r + 32)
                            last = nc.scalar.copy(KM[rows, :, r, :], PS[rows, 1, 0:2 * UL].rearrange("p (j n) -> p j n", j=2))
                        last.then_inc(sem("f_ka"), 1)
                    elif k in (2, 3):
                        for u in (2 * k - 4, 2 * k - 3):
                            need(act, ("f_nm3", atb("f_nm3", i, o, 4, u + 1)))
                            for g in range(2):
                                h = 2 * u + g
                                last = nc.scalar.activation(E3[0:NL, h, :], PS[0:NL, u % 3, g * U:(g + 1) * U], ACT.Exp,
                                                            scale=SC, bias=M3[:, h:h + 1], accum_out=Z3[:, 1, h:h + 1])
                            last.then_inc(sem("f_e3"), 1)
                    elif k in (6, 7):
                        if k == 6:
                            need(act, ("f_sub1", atb("f_sub1", i, o, 4, 4)))
                            nc.scalar.activation(E1_[:, :, :, :], E1_[:, :, :, :], ACT.Exp, scale=SC).then_inc(sem("f_e1"), 1)
                        for u in (2 * k - 12, 2 * k - 11):
                            need(act, ("f_t3", atb("f_t3", i, o, 4, u + 1)))
                            nc.scalar.copy(P3[0:UT, 2 * u:2 * u + 2, :, :].rearrange("p g t n -> p (g t n)"),
                                           PS[0:UT, (u + 2) % 3, 0:4 * KP]).then_inc(sem("f_p3"), 1)
                    elif k in (10, 11):
                        for u in ((0, 1) if k == 10 else (2,)):
                            need(act, ("f_t1", atb("f_t1", i, o, 3, u + 1)))
                            n = min(3, H - 3 * u)
                            nc.scalar.copy(PT[0:NL, a, 3 * u:3 * u + n, :].rearrange("p g n -> p (g n)"),
                                           PS[0:NL, (u + 1) % 3, 0:n * U]).then_inc(sem("f_pt"), 1)

                def body(i, o, ahead):
                    for q in range(2):
                        need(act, ("f_m0", atb("f_m0", i, o, 2, q + 1)))
                        both = heads4(PS[0:NL, 4 + q, 0:4 * SW])
                        nc.scalar.mul(ST[0:NL, 4 * q:4 * q + 4, 0:NL], both[:, :, 0:NL], RC[:, 0:1])
                        nc.scalar.copy(ST[0:NL, 4 * q:4 * q + 4, SMALL], both[:, :, SMALL]).then_inc(sem("f_y0"), 1)
                    kappa = 1.0
                    for it in range(ITERS):
                        for q in range(2):
                            need(act, ("f_m1", atb("f_m1", i, o, HALVES, 2 * it + q + 1)))
                            nc.scalar.mul(TA[0:NL, 4 * q:4 * q + 4, :], heads4(PS[0:NL, 4 + q, 0:4 * SW]),
                                          15.0 / 13.0 * kappa).then_inc(sem("f_ta"), 1)
                        if ahead:
                            front(i, o + 1, 2 * it)
                            front(i, o + 1, 2 * it + 1)
                        kappa *= 13.0 / 4.0
                    need(act, ("f_st", atb("f_st", i, o, HALVES, HALVES)))
                    nc.scalar.mul(UU[0:NL, :, :], ST[0:NL, :, SMALL], RCK[:, 0:1]).then_inc(sem("f_u"), 1)
                    need(act, ("f_o", atb("f_o", i, o, 1, 1)))
                    nc.scalar.copy(OO[:, :, :], PS[:, 6, 0:2 * U].rearrange("p (t n) -> p t n", t=2)).then_inc(sem("f_oo"), 1)

                act.wait_ge(sem("f_started"), 1)
                for k in range(HALVES):
                    front(0, 0, k)
                batches(act, body)

            @block.gpsimd
            def _(pool):
                def front(i, o, k):
                    f = bass.ds(i * 2 + o, 1)
                    if k == 0:
                        need(pool, ("f_v", atb("f_v", i, o, 1, 0)))
                        nc.gpsimd.tensor_copy(XS[:, :], XAP[:, f, :].rearrange("p a n -> p (a n)")).then_inc(sem("f_x"), 1)
                    elif k == 4:
                        nc.gpsimd.tensor_copy(AS[:, o % 2, :, 0:NL], AA[:, f, :, :].rearrange("p a h n -> p (a h) n")
                                              ).then_inc(sem("f_as"), 1)
                    elif k == 8:
                        need(pool, ("f_z1", atb("f_z1", i, o, 3, 3)), ("f_e10", atb("f_e10", i, o, 1, 1)))
                        nc.gpsimd.tensor_tensor(P1[0:UT, :, :], E1_[:, :, :, :].rearrange("p h t n -> p (h t) n"),
                                                Z1[:, 2, :].unsqueeze(2).broadcast_to([UT, 2 * H, NL]),
                                                ALU.mult).then_inc(sem("f_p1"), 1)

                def body(i, o, ahead):
                    if ahead:
                        front(i, o + 1, 0)
                    need(pool, ("f_out", atb("f_out", i, o, 1, 0)))
                    nc.gpsimd.tensor_copy(XW[:, :], XC[:, bass.ds(i * 2 + o, 1), :].rearrange("p a n -> p (a n)")
                                          ).then_inc(sem("f_xw"), 1)
                    for it in range(ITERS):
                        c0 = NL if it == ITERS - 1 else 0
                        for q in range(2):
                            need(pool, ("f_ta", atb("f_ta", i, o, HALVES, 2 * it + q + 1)))
                            nc.gpsimd.tensor_tensor(TD[:, 4 * q:4 * q + 4, c0:SW], ST[0:NL, 4 * q:4 * q + 4, c0:SW],
                                                    TA[0:NL, 4 * q:4 * q + 4, c0:SW], ALU.subtract).then_inc(sem("f_td"), 1)
                        if ahead and it:
                            front(i, o + 1, 2 * it)

                pool.wait_ge(sem("f_started"), 1)
                for k in (0, 4, 8):
                    front(0, 0, k)
                batches(pool, body)

            @block.vector
            def _(dve):
                v = nc.vector

                def front(i, o, k):
                    a = o % 2
                    if k == 0:
                        need(dve, ("f_pk", atb("f_pk", i, o, 1, 1)))
                        for r in (0, 1):
                            rows = slice(32 * r, 32 * r + 32)
                            last = v.tensor_copy(KM[rows, :, r, :], PS[rows, 1, 0:2 * UL].rearrange("p (j n) -> p j n", j=2))
                        last.then_inc(sem("f_kd"), 1)
                    elif k == 1:
                        need(dve, ("f_v", atb("f_v", i, o, 1, 1)))
                        v.tensor_tensor(VU[0:UT, :, :], PS[0:UT, 2, :].rearrange("p (t n) -> p t n", t=2),
                                        CO[0:UT, C_KW:C_KW + 2].unsqueeze(2).broadcast_to([UT, 2, H * DH]),
                                        ALU.mult).then_inc(sem("f_vu"), 1)
                    elif k in (2, 3):
                        for u in (2 * k - 4, 2 * k - 3):
                            s3 = PS[0:NL, u % 3, 0:2 * U].rearrange("p (g n) -> p g n", g=2)
                            top = M3[:, 2 * u:2 * u + 2]
                            need(dve, ("f_s3", atb("f_s3", i, o, 4, u + 1)))
                            v.tensor_reduce(top, s3, AX.X, ALU.max).then_inc(sem("f_m3"), 1)
                            need(dve, ("f_m3", atb("f_m3", i, o, 4, u + 1)))
                            v.tensor_scalar(top, top, -SC, None, ALU.mult).then_inc(sem("f_nm3"), 1)
                    elif k in (4, 5):
                        for u in (2 * k - 8, 2 * k - 7):
                            s1 = PS[0:UT, (u + 1) % 3, 0:4 * KP].rearrange("p (g n) -> p g n", g=4)[:, :, 0:NL]
                            need(dve, ("f_s1", atb("f_s1", i, o, 4, u + 1)))
                            v.tensor_reduce(M1[:, u, :], s1, AX.X, ALU.max).then_inc(sem("f_mm1"), 1)
                            need(dve, ("f_mm1", atb("f_mm1", i, o, 4, u + 1)))
                            v.tensor_tensor(E1_[:, u // 2 * 4:u // 2 * 4 + 4, u % 2, :], s1,
                                            M1[:, u, :].unsqueeze(2).broadcast_to([UT, 4, NL]),
                                            ALU.subtract).then_inc(sem("f_sub1"), 1)
                    elif k == 6:
                        e1 = E1_[:, :, :, :].rearrange("p h t n -> p (h t) n")
                        need(dve, ("f_e1", atb("f_e1", i, o, 1, 1)))
                        v.tensor_reduce(Z1[:, 0, :], e1, AX.X, ALU.add).then_inc(sem("f_z1"), 1)
                        need(dve, ("f_z1", atb("f_z1", i, o, 3, 1)))
                        v.scalar_tensor_tensor(out=Z1[:, 1, :], in0=e1[:, :, 0], scalar=float(ZL - 1), in1=Z1[:, 0, :],
                                               op0=ALU.mult, op1=ALU.add).then_inc(sem("f_z1"), 1)
                    elif k == 7:
                        e1 = E1_[:, :, :, :].rearrange("p h t n -> p (h t) n")
                        need(dve, ("f_z1", atb("f_z1", i, o, 3, 2)))
                        v.reciprocal(Z1[:, 2, :], Z1[:, 1, :]).then_inc(sem("f_z1"), 1)
                        v.tensor_scalar(e1[:, :, 0], e1[:, :, 0], ROOT, None, ALU.mult).then_inc(sem("f_e10"), 1)
                        need(dve, ("f_e3", atb("f_e3", i, o, 4, 4)))
                        v.tensor_reduce(Z3[:, 0, :], E3[0:NL, :, 0:NI], AX.X, ALU.add).then_inc(sem("f_z3"), 1)
                    elif k == 8:
                        need(dve, ("f_z3", atb("f_z3", i, o, 4, 1)))
                        v.scalar_tensor_tensor(out=Z3[:, 2, :], in0=Z3[:, 0, :], scalar=float(COPIES - 1), in1=Z3[:, 1, :],
                                               op0=ALU.mult, op1=ALU.add).then_inc(sem("f_z3"), 1)
                        need(dve, ("f_z3", atb("f_z3", i, o, 4, 2)))
                        v.scalar_tensor_tensor(out=Z3[:, 3, :], in0=E3[0:NL, :, U - 1], scalar=float(PAD - 1), in1=Z3[:, 2, :],
                                               op0=ALU.mult, op1=ALU.add).then_inc(sem("f_z3"), 1)
                    elif k == 9:
                        need(dve, ("f_z3", atb("f_z3", i, o, 4, 3)))
                        v.reciprocal(Z3[:, 0, :], Z3[:, 3, :]).then_inc(sem("f_z3"), 1)
                        need(dve, ("f_z3", atb("f_z3", i, o, 4, 4)))
                        v.tensor_scalar(Z3[:, 2, :], Z3[:, 0, :], CO[0:NL, C_DV:C_DV + 1], None, ALU.mult
                                        ).then_inc(sem("f_r3"), 1)
                        need(dve, ("f_w", atb("f_w", i, o, 1, 1)), ("f_r3", atb("f_r3", i, o, 1, 1)))
                        v.tensor_tensor(AS[0:NL, a, :, SMALL], PS[0:NL, 0, 0:H * DH].rearrange("p (g n) -> p g n", g=H),
                                        Z3[:, 2, :].unsqueeze(2).broadcast_to([NL, H, DH]), ALU.mult).then_inc(sem("f_w0"), 1)

                def body(i, o, ahead):
                    kappa = 1.0
                    for it in range(ITERS):
                        c0 = NL if it == ITERS - 1 else 0
                        for q in range(2):
                            need(dve, ("f_ta", atb("f_ta", i, o, HALVES, 2 * it + q + 1)))
                            v.scalar_tensor_tensor(out=TX[0:NL, 4 * q:4 * q + 4, c0:SW], in0=ST[0:NL, 4 * q:4 * q + 4, c0:SW],
                                                   scalar=7.0 * 15.0 / 13.0, in1=TA[0:NL, 4 * q:4 * q + 4, c0:SW],
                                                   op0=ALU.mult, op1=ALU.subtract).then_inc(sem("f_tx"), 1)
                        if ahead:
                            front(i, o + 1, 2 * it)
                        for q in range(2):
                            need(dve, ("f_m2", atb("f_m2", i, o, HALVES, 2 * it + q + 1)),
                                 ("f_td", atb("f_td", i, o, HALVES, 2 * it + q + 1)))
                            v.scalar_tensor_tensor(
                                out=ST[0:NL, 4 * q:4 * q + 4, c0:SW],
                                in0=heads4(PS[0:NL, 6 + q, 0:4 * SW])[:, :, c0:SW],
                                scalar=kappa * 13.0 / 225.0, in1=TD[:, 4 * q:4 * q + 4, c0:SW],
                                op0=ALU.mult, op1=ALU.add).then_inc(sem("f_st"), 1)
                        if ahead:
                            front(i, o + 1, 2 * it + 1)
                        kappa *= 13.0 / 4.0
                    b = bass.ds(i * 2 + o, 1)
                    flat = lambda x: x.rearrange("p a n -> p (a n)")
                    need(dve, ("f_out", atb("f_out", i, o, 1, 1)))
                    v.tensor_tensor(flat(HT[0:D, b, 0:COPIES * NI]).rearrange("p (r n) -> p r n", r=COPIES),
                                    PS[0:D, 3, 0:COPIES * NI].rearrange("p (r n) -> p r n", r=COPIES),
                                    flat(HX[:, b, 0:NI]).unsqueeze(1).broadcast_to([D, COPIES, NI]), ALU.add
                                    ).then_inc(sem("f_hx"), 1)
                    v.tensor_tensor(flat(HT[0:D, b, COPIES * NI:N]), PS[0:D, 3, COPIES * NI:N], flat(HX[:, b, NI:NI + NX]),
                                    ALU.add).then_inc(sem("f_hx"), 1)
                    need(dve, ("f_hx", atb("f_hx", i, o, 2, 2)))
                    v.tensor_tensor(flat(HT[0:D, b, 0:N]), PS[D:128, 3, 0:N], flat(HT[0:D, b, 0:N]), ALU.add
                                    ).then_inc(sem("f_res"), 1)

                dve.wait_ge(sem("f_started"), 1)
                for k in range(HALVES):
                    front(0, 0, k)
                batches(dve, body)
        phase_over()
        S.close()

        first.close()
        XM = sb("XM", [128, B + 1, NP], F32R)
        XR = sb("XR", [D, B, NP])
        XN = sb("XN", [D, B, NP])
        WR = sb("WR", [TT, B * NT, E0])
        WT = sb("WT", [128, B, NP], F32R)

        def chunk(t, c, p=D):
            return t[0:p, :, :].rearrange("p b n -> p (b n)")[:, CH * c:CH * (c + 1)]

        def router_pe(pe, tag, weights, n, ready):
            per = CH // TT
            assert CH % TT == 0
            for k in range(B * NT):
                if k % per == 0:
                    pe.wait_ge(ready, k // per + 1)
                last = nc.tensor.matmul(PS[0:TT, 7, k * n:(k + 1) * n], XR[:, k // NT, k % NT * TT:(k % NT + 1) * TT],
                                        weights, start=True, stop=True)
            last.then_inc(sem(tag + "_logit"), 1)

        def router_turn(pe, tag, n):
            pe.wait_ge(sem(tag + "_w"), 1)
            for k in range(B * NT):
                last = nc.tensor.transpose(PS[0:n, 1 + k // 5, k % 5 * TT:(k % 5 + 1) * TT], WR[:, k, 0:n],
                                           ident[0:TT, 0:TT])
            last.then_inc(sem(tag + "_turned"), 1)

        def router_act(act, tag, n, gates):
            act.wait_ge(sem(tag + "_sub"), 1)
            nc.scalar.activation(RE[:, :, 0:n], RD[:, :, 0:n], ACT.Exp).then_inc(sem(tag + "_exp"), 1)
            if gates:
                act.wait_ge(sem(tag + "_gsub"), 1)
                nc.scalar.activation(RE[:, :, 0:n], RD[:, :, 0:n], ACT.Exp).then_inc(sem(tag + "_gexp"), 1)
            act.wait_ge(sem(tag + "_turned"), 1)
            for q in range(5):
                w = min(5, B * NT - 5 * q) * TT
                nc.scalar.copy(WT[0:n, :, :].rearrange("p b n -> p (b n)")[:, 5 * TT * q:5 * TT * q + w],
                               PS[0:n, 1 + q, 0:w]).then_inc(sem(tag + "_wt"), 1)

        def router_dve(dve, tag, bias, n, gates):
            v = nc.vector
            K = B * NT
            steps = [0]

            def step(ins):
                ins.then_inc(sem(tag + "_step"), 1)
                steps[0] += 1
                dve.wait_ge(sem(tag + "_step"), steps[0])

            wide = lambda x: x.unsqueeze(2).broadcast_to([TT, K, n])
            iota = CO[0:TT, C_IOTA:C_IOTA + n].unsqueeze(1).broadcast_to([TT, K, n])
            L, D_, T, O1, O2 = (x[:, :, 0:n] for x in (RL, RD, RT, R1, R2))
            dve.wait_ge(sem(tag + "_logit"), 1)
            step(v.tensor_tensor(L, PS[0:TT, 7, 0:K * n].rearrange("p (k n) -> p k n", n=n),
                                 bias.unsqueeze(1).broadcast_to([TT, K, n]), ALU.add))
            step(v.tensor_reduce(RM[:, 0, :], L, AX.X, ALU.max))
            v.tensor_tensor(D_, L, wide(RM[:, 0, :]), ALU.subtract).then_inc(sem(tag + "_sub"), 1)
            top = RM[:, 0, :]
            for k, hot in enumerate((O1, O2)):
                step(v.tensor_tensor(T, L, wide(top), ALU.is_lt))
                step(v.scalar_tensor_tensor(out=T, in0=T, scalar=100.0, in1=iota, op0=ALU.mult, op1=ALU.add))
                step(v.tensor_reduce(RM[:, 1, :], T, AX.X, ALU.min))
                step(v.tensor_tensor(hot, iota, wide(RM[:, 1, :]), ALU.is_equal))
                if k == 0:
                    step(v.scalar_tensor_tensor(out=L, in0=hot, scalar=-1e30, in1=L, op0=ALU.mult, op1=ALU.add))
                    step(v.tensor_reduce(RM[:, 2, :], L, AX.X, ALU.max))
                    top = RM[:, 2, :]
            step(v.tensor_tensor(O1, O1, O2, ALU.add))
            dve.wait_ge(sem(tag + "_exp"), 1)
            if gates:
                step(v.tensor_reduce(RM[:, 1, :], RE[:, :, 0:n], AX.X, ALU.add))
                step(v.reciprocal(RM[:, 2, :], RM[:, 1, :]))
                step(v.tensor_tensor(T, RE[:, :, 0:n], wide(RM[:, 2, :]), ALU.mult))
                v.tensor_tensor(D_, T, wide(RM[:, 2, :]), ALU.subtract).then_inc(sem(tag + "_gsub"), 1)
                dve.wait_ge(sem(tag + "_gexp"), 1)
            step(v.tensor_tensor(T, RE[:, :, 0:n], O1, ALU.mult))
            step(v.tensor_reduce(RM[:, 1, :], T, AX.X, ALU.add))
            step(v.reciprocal(RM[:, 2, :], RM[:, 1, :]))
            v.tensor_tensor(WR[:, :, 0:n], T, wide(RM[:, 2, :]), ALU.mult).then_inc(sem(tag + "_w"), 1)
            for q in range(5):
                dve.wait_ge(sem(tag + "_wt"), q + 1)
                w = min(5, K - 5 * q) * TT
                part = WT[:, :, :].rearrange("p b n -> p (b n)")[:, 5 * TT * q:5 * TT * q + w]
                v.tensor_tensor(part[32:32 + n, :], PS[0:n, 1 + q, 0:w], part[0:n, :], ALU.subtract)

        def split_pool(pool, tag, src, done):
            for c in range(NCH):
                pool.wait_ge(sem(tag + "_done"), done(c))
                nc.gpsimd.tensor_copy(chunk(XM, c), chunk(src, c)).then_inc(sem(tag + "_high"), 1)
                pool.wait_ge(sem(tag + "_high"), c + 1)
                nc.gpsimd.tensor_tensor(XM[D:128, :, :].rearrange("p b n -> p (b n)")[:, CH * c:CH * (c + 1)],
                                        chunk(src, c), chunk(XM, c), ALU.subtract).then_inc(sem(tag + "_low"), 1)
                pool.wait_ge(sem(tag + "_low"), c + 1)

        RL, RD, RT, R1, R2, RE = (sb(n, [TT, B * NT, E0]) for n in ("RL", "RD", "RT", "R1", "R2", "RE"))
        RM = sb("RM", [TT, 3, B * NT])
        CH = 360
        NCH = B * NP // CH
        LSQ = sb("LSQb", [128, NCH // 2, CH])
        LST = sb("LSTb", [128, 2, 18])
        LSW = sb("LSWb", [128, 2, 18, D])
        LCE = sb("LCEb", [128, NCH // 2, CH])

        with nc.Block() as block:
            @block.tensor
            def _(pe):
                ln_pe(pe, "b", lambda c: chunk(HT, c, KP), (s_load, 16), NCH, CH, norms=2)
                router_pe(pe, "r", MA[0:D, W_R:W_R + E0], E0, sem("b_done"))
                router_turn(pe, "r", E0)

            @block.gpsimd
            def _(pool):
                nc.gpsimd.memset(WT[:, :, :].bitcast(F32), 0.0).then_inc(sem("clear"), 1)
                pool.wait_ge(sem("clear"), 1)
                nc.gpsimd.memset(XM[:, B, :].bitcast(F32), 0.0).then_inc(sem("clear"), 1)
                pool.wait_ge(sem("clear"), 2)
                split_pool(pool, "b", XN, lambda c: NCH + c + 1)

            @block.scalar
            def _(act):
                ln_act(act, "b", NCH, CH, [False, True])
                act.wait_ge(sem("clear"), 1)
                router_act(act, "r", E0, False)

            @block.vector
            def _(dve):
                ln_dve(dve, "b", NCH, CH, [lambda c: chunk(XR, c), lambda c: chunk(XN, c)])
                router_dve(dve, "r", WI[0:TT, X_BR:X_BR + E0], E0, False)
        phase_over()

        kept = ExitStack()
        YA = kept.enter_context(nc.sbuf_tensor("YA", [128, B, NP], F32))
        S = ExitStack()
        GE = ts("GE", [128, 2 * E0, NP])
        YW = ts("YW", [128, 4, NP])
        WB = ts("WB", [128, 2, NP])
        YS = ts("YS", [128, 2, NP])
        PAIRS = E0 // 2
        AHEAD = 4
        with nc.Block() as block:
            @block.sync
            def _(sp):
                started(sp, LOOP3)
                sp.sem_inc(sem("m_y"), PAIRS)
                sp.sem_inc(sem("m_started"), 1)

            def y_at(i, k):
                return at(i, PAIRS, k) + PAIRS

            @block.tensor
            def _(pe):
                def hidden(x, j):
                    nc.tensor.matmul(PS[:, j % AHEAD, 0:NP], WH[:, Y_F1 + j * 128:Y_F1 + (j + 1) * 128], x,
                                     start=True, stop=False)
                    nc.tensor.matmul(PS[:, j % AHEAD, 0:NP], WL[:, Y_F1 + j * 128:Y_F1 + (j + 1) * 128], x,
                                     start=False, stop=True).then_inc(sem("m_h"), 1)

                pe.wait_ge(sem("m_started"), 1)
                for j in range(AHEAD):
                    hidden(XM[:, 0, :], j)
                with pe.Fori(0, B) as i:
                    for q in range(PAIRS):
                        for k in range(4):
                            need(pe, ("m_g", at(i, 2 * E0, 4 * q + k + 1)))
                            j = 4 * q + k + AHEAD
                            hidden(XM[:, i, :] if j < 2 * E0 else XM[:, bass.ds(i + 1, 1), :].rearrange("p a n -> p (a n)"),
                                   j % (2 * E0))
                            if k == 2:
                                need(pe, ("m_yw", at(i, PAIRS, max(q - 1, 0))))
                                nc.tensor.matmul(PS[:, 6 + q % 2, 0:NP], SEL[:, q * 128:(q + 1) * 128], WT[:, i, :],
                                                 start=True, stop=True).then_inc(sem("m_w"), 1)
                            if k >= 2:
                                for o in range(2):
                                    g = 4 * q + 2 * o + k - 2
                                    last = nc.tensor.matmul(PS[o * D:(o + 1) * D, 4 + q % 2, 0:NP],
                                                            WI[:, X_F2 + g * D:X_F2 + (g + 1) * D], GE[:, g, :],
                                                            start=k == 2, stop=k == 3)
                        last.then_inc(sem("m_y"), 1)

            @block.scalar
            def _(act):
                warm(ACT.Gelu)
                with act.Fori(0, B) as i:
                    for j in range(2 * E0):
                        need(act, ("m_h", at(i, 2 * E0, j + 1)), ("m_y", y_at(i, j // 4 + 1 - PAIRS)))
                        nc.scalar.activation(GE[:, j, :], PS[:, j % AHEAD, 0:NP], ACT.Gelu, bias=FB1[:, j:j + 1]
                                             ).then_inc(sem("m_g"), 1)

            @block.vector
            def _(dve):
                v = nc.vector
                with dve.Fori(0, B) as i:
                    for q in range(PAIRS):
                        need(dve, ("m_w", at(i, PAIRS, q + 1)))
                        v.tensor_copy(WB[:, q % 2, :], PS[:, 6 + q % 2, 0:NP]).then_inc(sem("m_wb"), 1)
                        need(dve, ("m_wb", at(i, PAIRS, q + 1)), ("m_y", y_at(i, q + 1)), ("m_s", at(i, 3, 0 if q < 2 else 1)))
                        v.scalar_tensor_tensor(out=YW[:, q, :], in0=PS[:, 4 + q % 2, 0:NP],
                                               scalar=WI[:, X_B2 + q:X_B2 + q + 1], in1=WB[:, q % 2, :],
                                               op0=ALU.add, op1=ALU.mult).then_inc(sem("m_yw"), 1)

            @block.gpsimd
            def _(pool):
                with pool.Fori(0, B) as i:
                    for o in range(2):
                        need(pool, ("m_yw", at(i, PAIRS, 2 * o + 2)), ("m_s", at(i, 3, 0)))
                        nc.gpsimd.tensor_tensor(YS[:, o, :], YW[:, 2 * o, :], YW[:, 2 * o + 1, :], ALU.add
                                                ).then_inc(sem("m_s"), 1)
                    need(pool, ("m_s", at(i, 3, 2)))
                    nc.gpsimd.tensor_tensor(YA[:, i, :], YS[:, 0, :], YS[:, 1, :], ALU.add).then_inc(sem("m_s"), 1)
        phase_over()
        S.close()

        S = ExitStack()
        NK = 288
        XK = ts("XK", [128, NK], F32R)
        QR = ts("QR", [128, 2, H, NP])
        KA = ts("KA", [128, 2, H, NK])
        SQ = ts("SQ", [128, 4, NK])
        K2 = ts("K2", [128, 2, 2 * H + 2])
        VM = ts("VM", [128, 2, 2, H * D])
        VR = ts("VR", [128, 2, 2, D])
        CL = ts("CL", [128, 3, 2, NP])
        EX = ts("EX", [128, 3, 2, NP])
        with nc.Block() as block:
            @block.tensor
            def _(pe):
                for c in range(NCH):
                    if c >= 2:
                        pe.wait_ge(sem("halves_in"), c - 1)
                    nc.tensor.matmul(PS[0:D, 6 + c % 2, 0:CH], CO[:, C_II:C_II + D], chunk(YA, c, 128),
                                     start=True, stop=True).then_inc(sem("halves"), 1)
                ln_pe(pe, "c", lambda c: chunk(HT, c, KP), (sem("halves_in"), NCH), NCH, CH)

            @block.gpsimd
            def _(pool):
                for k, (rows, value) in enumerate(((XK[:, :].bitcast(F32), 0.0), (KA[D:128, :, :, :], 0.25))):
                    nc.gpsimd.memset(rows, value).then_inc(sem("c_fill"), 1)
                    pool.wait_ge(sem("c_fill"), k + 1)

            @block.scalar
            def _(act):
                ln_act(act, "c", NCH, CH, [True])
                for c in range(NCH):
                    act.wait_ge(sem("c_done"), c + 1)
                    nc.scalar.copy(chunk(XM, c), chunk(XN, c)).then_inc(sem("c_high"), 1)

            @block.vector
            def _(dve):
                for c in range(NCH):
                    dve.wait_ge(sem("halves"), c + 1)
                    nc.vector.tensor_tensor(chunk(HT, c), PS[0:D, 6 + c % 2, 0:CH], chunk(HT, c), ALU.add
                                            ).then_inc(sem("halves_in"), 1)
                ln_dve(dve, "c", NCH, CH, [lambda c: chunk(XN, c)])
                for c in range(NCH):
                    dve.wait_ge(sem("c_high"), c + 1)
                    nc.vector.tensor_tensor(XM[D:128, :, :].rearrange("p b n -> p (b n)")[:, CH * c:CH * (c + 1)],
                                            chunk(XN, c), chunk(XM, c), ALU.subtract)
        phase_over()

        UN = H + 1
        PAIRS = H // 2
        VT0, VT1, VLAST = PAIRS, PAIRS + 1, PAIRS + 2
        with nc.Block() as block:
            @block.sync
            def _(sp):
                started(sp, LOOP4)
                for name, count in FREE.items():
                    sp.sem_inc(sem(name), count)
                sp.sem_inc(sem("d_started"), 1)

            @block.gpsimd
            def _(pool):
                pool.wait_ge(sem("d_started"), 1)

                def batch(i, o):
                    a = o % 2
                    need(pool, ("d_v", atb("d_v", i, o, 3, 0)), ("d_q2", atb("d_q2", i, o, PAIRS, 0)))
                    nc.gpsimd.tensor_copy(XK[:, 0:N], XM[:, bass.ds(i * 2 + o, 1), 0:N].rearrange("p a n -> p (a n)")
                                          ).then_inc(sem("d_x"), 1)
                    for p in range(PAIRS):
                        need(pool, ("d_qa", atb("d_qa", i, o, PAIRS, p + 1)), ("d_x", atb("d_x", i, o, 1, 1)))
                        q = QR[0:D, a, 2 * p:2 * p + 2, :]
                        nc.gpsimd.tensor_tensor(QR[D:128, a, 2 * p:2 * p + 2, :], q, q, ALU.mult).then_inc(sem("d_q2"), 1)

                with pool.Fori(0, B // 2) as i:
                    batch(i, 0)
                    batch(i, 1)

            @block.tensor
            def _(pe):
                def split_product(out_, y, m, x, swap=False):
                    for k, w in enumerate((WH, WL)):
                        last = nc.tensor.matmul(out_, x if swap else w[:, y:y + m], w[:, y:y + m] if swap else x,
                                                start=k == 0, stop=k == 1)
                    return last

                def norms(i, o, p):
                    bank = 7 * (o % 2)
                    if p == 0:
                        need(pe, ("d_res", atb("d_res", i, o, 1, -1)))
                    for t in range(2):
                        c = NP + t * H + 2 * p
                        nc.tensor.matmul(PS[:, bank, c:c + 2], SQ[:, p, t * 128:(t + 1) * 128], CO[:, C_NS:C_NS + 2],
                                         start=True, stop=True)
                    for h in (2 * p, 2 * p + 1):
                        r, c = h % 4, NP + 2 * H + h // 4
                        last = nc.tensor.matmul(PS[32 * r:32 * r + 32, bank, c:c + 1],
                                                SQ[:, p, 256:288], CO[:, C_NS + h % 2:C_NS + h % 2 + 1],
                                                start=True, stop=True)
                    last.then_inc(sem("d_norm"), 1)

                def front(i, o, s):
                    if s < PAIRS:
                        if s == 0:
                            need(pe, ("d_x", atb("d_x", i, o, 1, 1)), ("d_vm", atb("d_vm", i, o, 4, 0)))
                        else:
                            need(pe, ("d_qa", atb("d_qa", i, o, PAIRS, s)))
                        split_product(PS[:, 5, 0:NP], Y_Q + s * 128, 128, XK[:, 0:NP]).then_inc(sem("d_q"), 1)
                        if s:
                            need(pe, ("d_sq", atb("d_sq", i, o, PAIRS, s)))
                        split_product(PS[:, 6, 0:NK], Y_K + s * 128, 128, XK[:, :]).then_inc(sem("d_k"), 1)
                        if s:
                            norms(i, o, s - 1)
                    elif s == VT0:
                        need(pe, ("d_qa", atb("d_qa", i, o, PAIRS, PAIRS)))
                        split_product(PS[:, 5, :], Y_VO, H * D, XK[:, 0:128], True).then_inc(sem("d_v"), 1)
                    elif s == VT1:
                        need(pe, ("d_sq", atb("d_sq", i, o, PAIRS, PAIRS)))
                        split_product(PS[:, 6, :], Y_VO, H * D, XK[:, 128:256], True).then_inc(sem("d_v"), 1)
                        norms(i, o, PAIRS - 1)
                    elif s == VLAST:
                        need(pe, ("d_vm", atb("d_vm", i, o, 4, 2)))
                        split_product(PS[0:32, 5, :], Y_VO, H * D, XK[:, 256:288], True).then_inc(sem("d_v"), 1)

                def scores(i, o, u):
                    a = o % 2
                    if u == 0:
                        need(pe, ("d_ka", atb("d_ka", i, o, PAIRS, PAIRS)), ("d_q2", atb("d_q2", i, o, PAIRS, PAIRS)))
                    for t in range(2):
                        bank = 1 + (2 * UN * a + 2 * u + t) % 4
                        need(pe, ("d_cl", atb("d_cl", i, o, 2 * UN, 2 * u + t - 3)))
                        if u < H:
                            last = nc.tensor.matmul(PS[:, bank, 0:NP], KA[:, a, u, t * 128:(t + 1) * 128],
                                                    QR[:, a, u, :], start=True, stop=True)
                        else:
                            for r in range(4):
                                last = nc.tensor.matmul(PS[32 * r:32 * r + 32, bank, 0:NP],
                                                        KA[:, a, 4 * t + r, 256:288], QR[:, a, 4 * t + r, :],
                                                        start=True, stop=True)
                        last.then_inc(sem("d_s"), 1)

                def body(i, o, ahead):
                    for u in range(UN):
                        need(pe, ("d_e", atb("d_e", i, o, UN, u + 1)))
                        if u == 0:
                            need(pe, ("d_res", atb("d_res", i, o, 1, -1)), ("d_vm", atb("d_vm", i, o, 4, 4)))
                        for t in range(2):
                            last = nc.tensor.matmul(PS[t * D:(t + 1) * D, 7 * o, 0:NP],
                                                    VM[:, o, t, u * D:(u + 1) * D] if u < H else VR[:, o, t, :],
                                                    EX[:, u % 3, t, :], start=u == 0, stop=u == UN - 1)
                        last.then_inc(sem("d_pv"), 1)
                        if u + 2 < UN:
                            scores(i, o, u + 2)
                        elif ahead:
                            scores(i, o + 1, u + 2 - UN)
                        if ahead:
                            front(i, o + 1, u)

                pe.wait_ge(sem("d_started"), 1)
                for s in range(VLAST + 1):
                    front(0, 0, s)
                for u in range(2):
                    scores(0, 0, u)
                batches(pe, body)

            @block.scalar
            def _(act):
                def front(i, o, s):
                    a = o % 2
                    if 1 <= s <= PAIRS:
                        need(act, ("d_ka", atb("d_ka", i, o, PAIRS, s)))
                        nc.scalar.activation(SQ[:, s - 1, :], PS[:, 6, 0:NK], ACT.Square).then_inc(sem("d_sq"), 1)
                    if s >= PAIRS:
                        return
                    need(act, ("d_q", atb("d_q", i, o, PAIRS, s + 1)))
                    for k in range(2):
                        half = PS[k * D:(k + 1) * D, 5, 0:NP]
                        last = nc.scalar.mul(QR[0:D, a, 2 * s + k, :], half, -2.0)
                    last.then_inc(sem("d_qa"), 1)

                def exps(i, o, u):
                    need(act, ("d_cl", atb("d_cl", i, o, 2 * UN, 2 * u + 2)), ("d_pv", atb("d_pv", i, o, UN, u - 2)))
                    if u < H:
                        nc.scalar.activation(EX[:, u % 3, :, :], CL[:, u % 3, :, :], ACT.Exp,
                                             scale=NG[:, u:u + 1]).then_inc(sem("d_e"), 1)
                    else:
                        nc.scalar.activation(EX[:, u % 3, 0, :], CL[:, u % 3, 0, :], ACT.Exp, scale=NG[:, H:H + 1])
                        nc.scalar.activation(EX[:, u % 3, 1, :], CL[:, u % 3, 1, :], ACT.Exp,
                                             scale=NG[:, H + 1:H + 2]).then_inc(sem("d_e"), 1)

                def body(i, o, ahead):
                    for u in range(UN):
                        if u + 1 < UN:
                            exps(i, o, u + 1)
                        elif ahead:
                            exps(i, o + 1, 0)
                        if ahead:
                            front(i, o + 1, u)

                act.wait_ge(sem("d_started"), 1)
                for s in range(PAIRS + 1):
                    front(0, 0, s)
                exps(0, 0, 0)
                batches(act, body)

            @block.vector
            def _(dve):
                v = nc.vector

                def front(i, o, s):
                    a = o % 2
                    if s < PAIRS:
                        need(dve, ("d_k", atb("d_k", i, o, PAIRS, s + 1)))
                        for k in range(2):
                            last = v.tensor_copy(KA[0:D, a, 2 * s + k, :], PS[k * D:(k + 1) * D, 6, 0:NK])
                        last.then_inc(sem("d_ka"), 1)
                    elif s in (VT0, VT1):
                        need(dve, ("d_v", atb("d_v", i, o, 3, s - VT0 + 1)))
                        v.tensor_copy(VM[:, a, s - VT0, :], PS[:, 5 + s - VT0, :]).then_inc(sem("d_vm"), 1)
                    elif s == VLAST:
                        need(dve, ("d_v", atb("d_v", i, o, 3, 3)))
                        need(dve, ("d_norm", atb("d_norm", i, o, PAIRS, PAIRS)))
                        v.tensor_copy(K2[:, a, :], PS[:, 7 * a, NP:NP + 2 * H + 2]).then_inc(sem("d_vm"), 1)
                        for r in range(4):
                            last = v.tensor_copy(VR[32 * r:32 * r + 32, a, :, :],
                                                 PS[0:32, 5, :].rearrange("p (t r d) -> p t r d", t=2, r=4)[:, :, r, :])
                        last.then_inc(sem("d_vm"), 1)

                def clamp(i, o, u):
                    a = o % 2
                    if u == 0:
                        need(dve, ("d_vm", atb("d_vm", i, o, 4, 3)))
                    for t in range(2):
                        bank = 1 + (2 * UN * a + 2 * u + t) % 4
                        c = t * H + u if u < H else 2 * H + t
                        need(dve, ("d_s", atb("d_s", i, o, 2 * UN, 2 * u + t + 1)),
                             ("d_e", atb("d_e", i, o, UN, u - 2)))
                        v.tensor_scalar(CL[:, u % 3, t, :], PS[:, bank, 0:NP], K2[:, a, c:c + 1], 0.0, ALU.add, ALU.max
                                        ).then_inc(sem("d_cl"), 1)

                def body(i, o, ahead):
                    for u in range(UN):
                        if u + 2 < UN:
                            clamp(i, o, u + 2)
                        elif ahead:
                            clamp(i, o + 1, u + 2 - UN)
                        if ahead:
                            front(i, o + 1, u)
                    need(dve, ("d_pv", atb("d_pv", i, o, UN, UN)))
                    mine = HT[0:D, bass.ds(i * 2 + o, 1), 0:N].rearrange("p a n -> p (a n)")
                    v.tensor_tensor(mine, PS[0:D, 7 * o, 0:N], mine, ALU.add).then_inc(sem("d_half"), 1)
                    need(dve, ("d_half", atb("d_half", i, o, 1, 1)))
                    v.tensor_tensor(mine, PS[D:128, 7 * o, 0:N], mine, ALU.add).then_inc(sem("d_res"), 1)

                dve.wait_ge(sem("d_started"), 1)
                for s in range(VLAST + 1):
                    front(0, 0, s)
                for u in range(2):
                    clamp(0, 0, u)
                batches(dve, body)
        phase_over()
        S.close()
        kept.close()

        with nc.Block() as block:
            @block.tensor
            def _(pe):
                ln_pe(pe, "d", lambda c: chunk(HT, c, KP), (s_load, 16), NCH, CH)
                router_pe(pe, "g", MA[0:D, W_G:W_G + E1], E1, sem("d_done"))
                router_turn(pe, "g", E1)

            @block.gpsimd
            def _(pool):
                split_pool(pool, "d", XR, lambda c: c + 1)

            @block.scalar
            def _(act):
                ln_act(act, "d", NCH, CH, [False])
                router_act(act, "g", E1, True)

            @block.vector
            def _(dve):
                ln_dve(dve, "d", NCH, CH, [lambda c: chunk(XR, c)])
                router_dve(dve, "g", WI[0:TT, X_GB:X_GB + E1], E1, True)
        phase_over()

        S = ExitStack()
        H1 = ts("H1", [128, E1, NP])
        S1 = ts("S1", [KP, NP])
        H2 = ts("H2", [128, 2, NP])
        S2 = ts("S2", [128, NP])
        GB = ts("GB", [128, 2, NP])
        YG = ts("YG", [128, 2, NP])
        GA = ts("GA", [128, NP])
        HF = ts("HF", [KP, NP])
        OS = ts("OS", [TT, NT, D])

        with nc.Block() as block:
            @block.sync
            def _(sp):
                started(sp, LOOP5)
                sp.sem_inc(sem("g_started"), 1)
                with sp.Fori(0, B) as i:
                    need(sp, ("g_os", at(i, 1, 1)))
                    sp.dma_start(out[bass.ds(i, 1), 0:2 * TT, :].rearrange("b (t p) d -> p (b t) d", p=TT),
                                 OS[:, 0:2, :]).then_inc(sem("g_put"), 16)
                    sp.dma_start(out[bass.ds(i, 1), 2 * TT:N, :].rearrange("b p d -> p (b d)"), OS[0:N - 2 * TT, 2, :]
                                 ).then_inc(sem("g_put"), 16)
                sp.wait_ge(sem("g_put"), 32 * B + 1)

            @block.gpsimd
            def _(pool):
                for k, pad in enumerate((S1[D:KP, :], HF[D:KP, :])):
                    nc.gpsimd.memset(pad, 0.0).then_inc(sem("g_pad"), 1)
                    pool.wait_ge(sem("g_pad"), k + 1)
                with pool.Fori(0, B) as i:
                    need(pool, ("g_fin", at(i, 1, 0)))
                    nc.gpsimd.tensor_tensor(HF[0:D, :], HT[0:D, i, :], WI[0:D, X_SB3:X_SB3 + 1].broadcast_to([D, NP]),
                                            ALU.add).then_inc(sem("g_hf"), 1)
                    need(pool, ("g_yg", at(i, 2, 2)))
                    nc.gpsimd.tensor_tensor(GA[:, :], YG[:, 0, :], YG[:, 1, :], ALU.add).then_inc(sem("g_ga"), 1)

            @block.tensor
            def _(pe):
                def first_layer(i, o):
                    x = XM[:, bass.ds(i + o, 1), :].rearrange("p a n -> p (a n)")
                    need(pe, ("g_h1", nxt(i, o, 4, 0)))
                    for bank, y, m in ((0, Y_E1, 128), (1, Y_E1 + 128, 128), (2, Y_E1 + 256, 128),
                                       (3, Y_E1 + 384, 128), (4, Y_S1, D)):
                        if bank == 3:
                            need(pe, ("g_s2", nxt(i, o, 1, 0)), ("g_os", at(i, 1, 0)))
                        for k, w in enumerate((WH, WL)):
                            last = nc.tensor.matmul(PS[0:m, bank, 0:NP], w[:, y:y + m], x, start=k == 0, stop=k == 1)
                        last.then_inc(sem("g_l1"), 1)

                def second_layer(i, o):
                    need(pe, ("g_s1", nxt(i, o, 1, 1)))
                    nc.tensor.matmul(PS[:, 4, 0:NP], MA[0:KP, W_S2:W_S2 + 128], S1[:, :], start=True, stop=True
                                     ).then_inc(sem("g_l2"), 1)
                    need(pe, ("g_h1", nxt(i, o, 4, 4)), ("g_yg", nxt(i, o, 2, 0)))
                    for e in range(E1):
                        last = nc.tensor.matmul(PS[e % 2 * D:(e % 2 + 1) * D, 5 + e // 2, 0:NP],
                                                WI[:, X_E2 + e * D:X_E2 + (e + 1) * D], H1[:, e, :],
                                                start=True, stop=True)
                        if e % 2:
                            last.then_inc(sem("g_l2"), 1)

                def third_layer(i):
                    for q in range(2):
                        need(pe, ("g_gb", at(i, 2, q)))
                        nc.tensor.matmul(PS[:, 7, 0:NP], SEL[:, q * 128:(q + 1) * 128],
                                         WT[:, bass.ds(i + 0, 1), :].rearrange("p a n -> p (a n)"),
                                         start=True, stop=True).then_inc(sem("g_gate"), 1)
                        if q == 0:
                            need(pe, ("g_h2", at(i, 2, 2)))
                        nc.tensor.matmul(PS[:, 5 + q, 0:NP], WI[:, X_E3 + q * 128:X_E3 + (q + 1) * 128],
                                         H2[:, q, :], start=True, stop=True).then_inc(sem("g_l3"), 1)

                def output(i, ahead):
                    need(pe, ("g_ga", at(i, 1, 1)), ("g_hf", at(i, 1, 1)), ("g_s2", at(i, 1, 1)))
                    if ahead:
                        need(pe, ("g_h1", nxt(i, 1, 4, 4)))
                    for t in range(NT):
                        tok = slice(t * TT, (t + 1) * TT)
                        fin = PS[0:TT, 3, t * D:(t + 1) * D]
                        nc.tensor.matmul(fin, GA[:, tok], CO[:, C_II:C_II + D], start=True, stop=False)
                        nc.tensor.matmul(fin, S2[:, tok], WI[:, X_S3:X_S3 + D], start=False, stop=False)
                        last = nc.tensor.matmul(fin, HF[:, tok], ident[0:KP, 0:D], start=False, stop=True)
                    last.then_inc(sem("g_fin"), 1)

                pe.wait_ge(sem("g_started"), 1)
                pe.wait_ge(sem("g_pad"), 2)
                first_layer(0, 0)
                second_layer(0, 0)
                with pe.Fori(0, B - 1) as i:
                    first_layer(i, 1)
                    third_layer(i)
                    second_layer(i, 1)
                    output(i, True)
                third_layer(B - 1)
                output(B - 1, False)

            @block.scalar
            def _(act):
                def layers(i, o):
                    need(act, ("g_l1", nxt(i, o, 5, 1)), ("g_l2", nxt(i, o, 3, 0)))
                    nc.scalar.activation(H1[:, 0, :], PS[:, 0, 0:NP], ACT.Relu, bias=WI[:, X_EB1:X_EB1 + 1]
                                         ).then_inc(sem("g_h1"), 1)
                    need(act, ("g_l1", nxt(i, o, 5, 3)))
                    nc.scalar.activation(H1[:, 2, :], PS[:, 2, 0:NP], ACT.Relu, bias=WI[:, X_EB1 + 2:X_EB1 + 3]
                                         ).then_inc(sem("g_h1"), 1)
                    need(act, ("g_l1", nxt(i, o, 5, 5)))
                    nc.scalar.activation(S1[0:D, :], PS[0:D, 4, 0:NP], ACT.Relu, bias=VE[0:D, V_SB1:V_SB1 + 1]
                                         ).then_inc(sem("g_s1"), 1)

                def layers2(i, o):
                    need(act, ("g_l2", nxt(i, o, 3, 2)), ("g_l3", nxt(i, o, 2, 0)))
                    nc.scalar.activation(H2[:, 0, :], PS[:, 5, 0:NP], ACT.Relu, bias=WI[:, X_EB2:X_EB2 + 1]
                                         ).then_inc(sem("g_h2"), 1)
                    need(act, ("g_l2", nxt(i, o, 3, 1)), ("g_fin", nxt(i, o, 1, 0)))
                    nc.scalar.activation(S2[:, :], PS[:, 4, 0:NP], ACT.Relu, bias=WI[:, X_SB2:X_SB2 + 1]
                                         ).then_inc(sem("g_s2"), 1)

                def gates(i):
                    for q in range(2):
                        need(act, ("g_gate", at(i, 2, q + 1)), ("g_yg", at(i, 2, 0)))
                        nc.scalar.copy(GB[:, q, :], PS[:, 7, 0:NP]).then_inc(sem("g_gb"), 1)

                layers(0, 0)
                layers2(0, 0)
                with act.Fori(0, B - 1) as i:
                    layers(i, 1)
                    gates(i)
                    layers2(i, 1)
                gates(B - 1)

            @block.vector
            def _(dve):
                v = nc.vector

                def layers(i, o):
                    for e in (1, 3):
                        need(dve, ("g_l1", nxt(i, o, 5, e + 1)), ("g_l2", nxt(i, o, 3, 0)))
                        v.tensor_scalar(H1[:, e, :], PS[:, e, 0:NP], WI[:, X_EB1 + e:X_EB1 + e + 1], 0.0, ALU.add, ALU.max
                                        ).then_inc(sem("g_h1"), 1)

                def layers2(i, o):
                    need(dve, ("g_l2", nxt(i, o, 3, 3)), ("g_l3", nxt(i, o, 2, 0)))
                    v.tensor_scalar(H2[:, 1, :], PS[:, 6, 0:NP], WI[:, X_EB2 + 1:X_EB2 + 2], 0.0, ALU.add, ALU.max
                                    ).then_inc(sem("g_h2"), 1)

                def gated(i):
                    for q in range(2):
                        need(dve, ("g_l3", at(i, 2, q + 1)), ("g_gb", at(i, 2, q + 1)), ("g_ga", at(i, 1, 0)))
                        v.scalar_tensor_tensor(out=YG[:, q, :], in0=PS[:, 5 + q, 0:NP],
                                               scalar=WI[:, X_EB3 + q:X_EB3 + q + 1], in1=GB[:, q, :],
                                               op0=ALU.add, op1=ALU.mult).then_inc(sem("g_yg"), 1)

                def output(i):
                    need(dve, ("g_fin", at(i, 1, 1)), ("g_put", at(i, 32, 0)))
                    v.tensor_copy(OS[:, :, :], PS[0:TT, 3, 0:NT * D].rearrange("p (t d) -> p t d", t=NT)
                                  ).then_inc(sem("g_os"), 1)

                layers(0, 0)
                layers2(0, 0)
                with dve.Fori(0, B - 1) as i:
                    layers(i, 1)
                    gated(i)
                    layers2(i, 1)
                    output(i)
                gated(B - 1)
                output(B - 1)
        phase_over()
        S.close()


_OUT = (B, N, D)


def kernel(**inputs):
    import concourse.bacc as bacc
    from concourse.bass_utils import run_bass_kernel_spmd as run

    a = {k: np.asarray(v) for k, v in inputs.items()}
    t = lambda m: np.ascontiguousarray(m)
    x = a["x"].reshape(B, 3, 8, 8, 8, 8).transpose(3, 5, 1, 0, 2, 4).reshape(PF, B * NI)
    txt = a["txt"].transpose(2, 0, 1).reshape(D, B * NX)
    ln1 = np.stack([a["L0_tok_ln1_g"], a["L0_tok_ln1_b"]], 1)
    names = ["L0_tok_b1", "L0_tok_ln2_g", "L0_tok_ln2_b", "L0_tok_bp1", "L0_tok_lnp_g", "L0_tok_lnp_b", "L0_tok_bp2",
             "L0_attn_ln_g", "L0_attn_ln_b", "L0_attn_b_out", "L1_attn_ln_scale", "L1_ffn_sb1"]
    vec = np.concatenate([np.stack([a[n] for n in names], 1), a["L0_ffn_ln_g"].T, a["L0_ffn_ln_b"].T], 1)
    side = lambda w: w.transpose(1, 0, 2).reshape(w.shape[1], -1)
    w_qkv = a["L0_attn_w_qkv"]
    mat = np.concatenate([
        a["L0_tok_Wp1"], a["L0_tok_Wp2"], w_qkv, a["L0_ffn_Wr"], a["L1_ffn_gW"], a["L1_ffn_sW1"], a["L1_ffn_sW2"],
        side(a["L1_ffn_eW1"]), side(a["L1_attn_W_q"]), side(a["L1_attn_W_k"]),
        side(a["L1_attn_W_v"].transpose(0, 2, 1)),
        a["L1_attn_W_o"].reshape(D, H, D).transpose(2, 1, 0).reshape(D, H * D),
        side(a["L0_ffn_W1"])], 1)
    rows = lambda r: np.broadcast_to(r[None, :], (128, r.shape[0]))
    halves = lambda w: w.reshape(2, 128, -1).transpose(1, 0, 2)
    kd = halves(np.repeat(a["L0_attn_res_kernel"].reshape(H, TAPS), DH, 0)).reshape(128, -1)
    wvt = halves(w_qkv[:, 512:768].T)
    e3 = np.zeros((2, D, 2, 2, D), np.float32)
    for o in range(2):
        e3[o, :, :, o, :] = a["L1_ffn_eW3"][o::2].transpose(1, 0, 2)
    e3 = e3.reshape(128, 2 * 128)
    wide = np.concatenate([
        a["L0_ffn_b1"].reshape(E0 * 2, 128).T, a["L1_ffn_sb2"][:, None], a["L1_ffn_eb1"].T,
        a["L1_ffn_eb2"].reshape(2, 128).T, rows(a["L1_attn_gamma"].reshape(H)),
        np.repeat(a["L1_attn_gamma"].reshape(2, 4), 32, 1).T, rows(a["L0_ffn_br"]),
        rows(a["L1_ffn_gb"]), kd, a["L1_ffn_sW3"], side(a["L1_ffn_eW2"]), e3,
        np.concatenate([wvt, wvt], 2).reshape(128, -1), halves(a["L0_attn_w_out"]).reshape(128, -1),
        a["L0_ffn_W2"].reshape(E0 * 2, 128, D).transpose(1, 0, 2).reshape(128, -1),
        a["L0_ffn_b2"].reshape(4, 128).T, np.concatenate([a["L1_ffn_sb3"]] * 2)[:, None],
        a["L1_ffn_eb3"].reshape(2, 128).T], 1)
    arrays = {"xpatch": x, "txt": txt, "w1": a["L0_tok_W1"], "ln1": ln1, "vec": np.concatenate([vec, vec], 0), "mat": np.concatenate([mat, mat], 0), "wide": wide,
              "const": shape_constants()}
    arrays = {k: t(v) for k, v in arrays.items()}
    nc = bacc.Bacc("TRN2", target_bir_lowering=False, num_devices=1)
    args = [nc.dram_tensor(k, v.shape, F32, kind="ExternalInput").ap() for k, v in arrays.items()]
    args.append(nc.dram_tensor("out_0", _OUT, F32, kind="ExternalOutput").ap())
    program(nc, *args)
    return run(nc, [arrays], core_ids=[0]).results[0]["out_0"]
```
